# Optimizing a Trainium2 kernel written in Bass

```python
import numpy as np
import jax
import jax.numpy as jnp

def _softmax(x, axis=-1):
    return jax.nn.softmax(x, axis=axis)

def _gelu(x):
    return jax.nn.gelu(x, approximate=True)

def _silu(x):
    return jax.nn.silu(x)

def _sigmoid(x):
    return jax.nn.sigmoid(x)

def _layernorm(x, axis=-1, eps=1e-05):
    m = jnp.mean(x, axis=axis, keepdims=True)
    v = jnp.var(x, axis=axis, keepdims=True)
    return (x - m) / jnp.sqrt(v + eps)

def _scatter_add(tgt, idx, src, axis=0):
    return tgt.at[idx].add(src)

def _segment_sum(src, seg, n):
    return jax.ops.segment_sum(src, seg, n)
kernel_name = 'mk_seq_postln_d2_jaxref_r8_3ec474'

def setup_inputs(seed: int=0):
    np.random.seed(seed)
    _w = jnp.asarray

    def _L0_attn_setup():
        import jax, jax.numpy as jnp
        import numpy as np
        B, S, D, H = (2, 256, 128, 16)
        HD = D // H
        key = jax.random.key(seed)
        ks = jax.random.split(key, 6)
        s = 1.0 / np.sqrt(D)
        return {'x': jax.random.normal(ks[0], (B, S, D), dtype=jnp.float32), 'Wq': jax.random.normal(ks[1], (D, D), dtype=jnp.float32) * s, 'Wk': jax.random.normal(ks[2], (D, D), dtype=jnp.float32) * s, 'Wv': jax.random.normal(ks[3], (D, D), dtype=jnp.float32) * s, 'Wo': jax.random.normal(ks[4], (D, D), dtype=jnp.float32) * s, 'bo': jnp.zeros((D,), dtype=jnp.float32)}
    _L0_attn_in = _L0_attn_setup()

    def _L0_ffn_setup():
        import jax, jax.numpy as jnp
        import numpy as np
        import math
        D = 128
        H = 16
        E = 8
        TOPK = 2
        LAT = D // 2
        KPH = LAT // H
        HD = D // H

        def _forward(hs, q_w, q_b, k_w, k_b, v_w, v_b, o_w, o_b, router_w, router_b, w1, b1, w2, b2):
            B, S, _ = hs.shape
            Q = (hs @ q_w + q_b).reshape(B, S, H, HD).transpose(0, 2, 1, 3)
            K = (hs @ k_w + k_b).reshape(B, S, H, KPH).transpose(0, 2, 1, 3)
            V = (hs @ v_w + v_b).reshape(B, S, H, KPH).transpose(0, 2, 1, 3)
            scores = jnp.einsum('bhsk,bhtk->bhst', Q[..., :KPH], K) / math.sqrt(KPH)
            attn = jax.nn.softmax(scores, axis=-1)
            ao = jnp.einsum('bhst,bhtv->bhsv', attn, V)
            ao = ao.transpose(0, 2, 1, 3).reshape(B, S, H * KPH)
            ao = jnp.concatenate([ao, jnp.zeros((B, S, D - LAT), ao.dtype)], axis=-1)
            mla_out = ao @ o_w + o_b
            probs = jax.nn.softmax(mla_out @ router_w + router_b, axis=-1)
            topw, topi = jax.lax.top_k(probs, TOPK)
            topw = topw / (topw.sum(-1, keepdims=True) + 1e-08)
            combine = jnp.sum(jax.nn.one_hot(topi, E, dtype=probs.dtype) * topw[..., None], axis=-2)
            h1 = jnp.einsum('bsd,edf->ebsf', mla_out, w1) + b1[:, None, None, :]
            h1 = jax.nn.gelu(h1, approximate=False)
            h2 = jnp.einsum('ebsf,efd->ebsd', h1, w2) + b2[:, None, None, :]
            moe_out = jnp.einsum('bse,ebsd->bsd', combine, h2)
            return hs + 0.3 * moe_out
        key = jax.random.key(seed)
        ks = jax.random.split(key, 16)
        s = 0.02
        inp = {'hidden_states': jax.random.normal(ks[0], (2, 256, D), jnp.float32), 'q_w': jax.random.normal(ks[1], (D, D), jnp.float32) * s, 'q_b': jnp.zeros((D,), jnp.float32), 'k_w': jax.random.normal(ks[2], (D, LAT), jnp.float32) * s, 'k_b': jnp.zeros((LAT,), jnp.float32), 'v_w': jax.random.normal(ks[3], (D, LAT), jnp.float32) * s, 'v_b': jnp.zeros((LAT,), jnp.float32), 'o_w': jax.random.normal(ks[4], (D, D), jnp.float32) * s, 'o_b': jnp.zeros((D,), jnp.float32), 'router_w': jax.random.normal(ks[5], (D, E), jnp.float32) * s, 'router_b': jnp.zeros((E,), jnp.float32), 'w1': jax.random.normal(ks[6], (E, D, 2 * D), jnp.float32) * s, 'b1': jnp.zeros((E, 2 * D), jnp.float32), 'w2': jax.random.normal(ks[7], (E, 2 * D, D), jnp.float32) * s, 'b2': jnp.zeros((E, D), jnp.float32)}
        return inp
    _L0_ffn_in = _L0_ffn_setup()

    def _L1_attn_setup():
        import jax, jax.numpy as jnp
        import numpy as np
        B, T, E = (4, 256, 128)
        H, HS = (16, 64)
        key = jax.random.key(seed)
        ks = jax.random.split(key, 6)
        return {'x': jax.random.normal(ks[0], (B, T, E), dtype=jnp.float32), 'Wq': jax.random.normal(ks[1], (H, E, HS), dtype=jnp.float32) * 0.02, 'Wk': jax.random.normal(ks[2], (H, E, HS), dtype=jnp.float32) * 0.02, 'Wv': jax.random.normal(ks[3], (H, E, HS), dtype=jnp.float32) * 0.02, 'proj_w': jax.random.normal(ks[4], (E, H * HS), dtype=jnp.float32) * 0.02, 'proj_b': jax.random.normal(ks[5], (E,), dtype=jnp.float32) * 0.02}
    _L1_attn_in = _L1_attn_setup()

    def _L1_ffn_setup():
        import jax, jax.numpy as jnp
        import numpy as np
        B, S, D, E, F = (2, 128, 128, 14, 256)
        key = jax.random.key(seed)
        k0, k1, k2, k3 = jax.random.split(key, 4)
        h = jax.random.normal(k0, (B, S, D), jnp.float32)
        gate_w = jax.random.normal(k1, (E, D), jnp.float32) * 0.02
        w1 = jax.random.normal(k2, (E, D, F), jnp.float32) * (1.0 / np.sqrt(D).astype(np.float32))
        b1 = jnp.zeros((E, F), jnp.float32)
        w2 = jax.random.normal(k3, (E, F, D), jnp.float32) * (1.0 / np.sqrt(F).astype(np.float32))
        b2 = jnp.zeros((E, D), jnp.float32)
        return {'h': h, 'gate_w': gate_w, 'w1': w1, 'b1': b1, 'w2': w2, 'b2': b2}
    _L1_ffn_in = _L1_ffn_setup()
    _d = {'L0_attn_x': _L0_attn_in['x'], 'L0_attn_Wq': _L0_attn_in['Wq'], 'L0_attn_Wk': _L0_attn_in['Wk'], 'L0_attn_Wv': _L0_attn_in['Wv'], 'L0_attn_Wo': _L0_attn_in['Wo'], 'L0_attn_bo': _L0_attn_in['bo'], 'L0_ffn_q_w': _L0_ffn_in['q_w'], 'L0_ffn_q_b': _L0_ffn_in['q_b'], 'L0_ffn_k_w': _L0_ffn_in['k_w'], 'L0_ffn_k_b': _L0_ffn_in['k_b'], 'L0_ffn_v_w': _L0_ffn_in['v_w'], 'L0_ffn_v_b': _L0_ffn_in['v_b'], 'L0_ffn_o_w': _L0_ffn_in['o_w'], 'L0_ffn_o_b': _L0_ffn_in['o_b'], 'L0_ffn_router_w': _L0_ffn_in['router_w'], 'L0_ffn_router_b': _L0_ffn_in['router_b'], 'L0_ffn_w1': _L0_ffn_in['w1'], 'L0_ffn_b1': _L0_ffn_in['b1'], 'L0_ffn_w2': _L0_ffn_in['w2'], 'L0_ffn_b2': _L0_ffn_in['b2'], 'L1_attn_Wq': _L1_attn_in['Wq'], 'L1_attn_Wk': _L1_attn_in['Wk'], 'L1_attn_Wv': _L1_attn_in['Wv'], 'L1_attn_proj_w': _L1_attn_in['proj_w'], 'L1_attn_proj_b': _L1_attn_in['proj_b'], 'L1_ffn_gate_w': _L1_ffn_in['gate_w'], 'L1_ffn_w1': _L1_ffn_in['w1'], 'L1_ffn_b1': _L1_ffn_in['b1'], 'L1_ffn_w2': _L1_ffn_in['w2'], 'L1_ffn_b2': _L1_ffn_in['b2']}
    _x0 = _d['L0_attn_x']
    _d['L0_attn_x'] = jax.random.normal(jax.random.fold_in(jax.random.key(seed), 1), (2, 1024, 128), dtype=_x0.dtype)
    del _x0
    return _d

def reference(L0_attn_x, L0_attn_Wq, L0_attn_Wk, L0_attn_Wv, L0_attn_Wo, L0_attn_bo, L0_ffn_q_w, L0_ffn_q_b, L0_ffn_k_w, L0_ffn_k_b, L0_ffn_v_w, L0_ffn_v_b, L0_ffn_o_w, L0_ffn_o_b, L0_ffn_router_w, L0_ffn_router_b, L0_ffn_w1, L0_ffn_b1, L0_ffn_w2, L0_ffn_b2, L1_attn_Wq, L1_attn_Wk, L1_attn_Wv, L1_attn_proj_w, L1_attn_proj_b, L1_ffn_gate_w, L1_ffn_w1, L1_ffn_b1, L1_ffn_w2, L1_ffn_b2):

    def _L0_attn_ref(x, Wq, Wk, Wv, Wo, bo):
        import jax, jax.numpy as jnp
        import numpy as np
        B, S, D, H = (2, 256, 128, 16)
        HD = D // H
        b, n, _ = x.shape

        def split_heads(t):
            return t.reshape(b, n, H, HD).transpose(0, 2, 1, 3)
        q = split_heads(x @ Wq)
        k = split_heads(x @ Wk)
        v = split_heads(x @ Wv)
        scores = jnp.einsum('bhqd,bhkd->bhqk', q, k)
        causal = jnp.tril(jnp.ones((n, n), dtype=bool))
        scores = jnp.where(causal, scores, -jnp.inf)
        attn = jax.nn.softmax(scores / np.sqrt(HD).astype(np.float32), axis=-1)
        ctx = jnp.einsum('bhqk,bhkd->bhqd', attn, v)
        ctx = ctx.transpose(0, 2, 1, 3).reshape(b, n, D)
        return ctx @ Wo + bo

    def _L0_ffn_ref(hidden_states, q_w, q_b, k_w, k_b, v_w, v_b, o_w, o_b, router_w, router_b, w1, b1, w2, b2):
        import jax, jax.numpy as jnp
        import numpy as np
        import math
        D = 128
        H = 16
        E = 8
        TOPK = 2
        LAT = D // 2
        KPH = LAT // H
        HD = D // H

        def _forward(hs, q_w, q_b, k_w, k_b, v_w, v_b, o_w, o_b, router_w, router_b, w1, b1, w2, b2):
            B, S, _ = hs.shape
            Q = (hs @ q_w + q_b).reshape(B, S, H, HD).transpose(0, 2, 1, 3)
            K = (hs @ k_w + k_b).reshape(B, S, H, KPH).transpose(0, 2, 1, 3)
            V = (hs @ v_w + v_b).reshape(B, S, H, KPH).transpose(0, 2, 1, 3)
            scores = jnp.einsum('bhsk,bhtk->bhst', Q[..., :KPH], K) / math.sqrt(KPH)
            attn = jax.nn.softmax(scores, axis=-1)
            ao = jnp.einsum('bhst,bhtv->bhsv', attn, V)
            ao = ao.transpose(0, 2, 1, 3).reshape(B, S, H * KPH)
            ao = jnp.concatenate([ao, jnp.zeros((B, S, D - LAT), ao.dtype)], axis=-1)
            mla_out = ao @ o_w + o_b
            probs = jax.nn.softmax(mla_out @ router_w + router_b, axis=-1)
            topw, topi = jax.lax.top_k(probs, TOPK)
            topw = topw / (topw.sum(-1, keepdims=True) + 1e-08)
            combine = jnp.sum(jax.nn.one_hot(topi, E, dtype=probs.dtype) * topw[..., None], axis=-2)
            h1 = jnp.einsum('bsd,edf->ebsf', mla_out, w1) + b1[:, None, None, :]
            h1 = jax.nn.gelu(h1, approximate=False)
            h2 = jnp.einsum('ebsf,efd->ebsd', h1, w2) + b2[:, None, None, :]
            moe_out = jnp.einsum('bse,ebsd->bsd', combine, h2)
            return hs + 0.3 * moe_out
        return _forward(hidden_states, q_w, q_b, k_w, k_b, v_w, v_b, o_w, o_b, router_w, router_b, w1, b1, w2, b2)

    def _L1_attn_ref(x, Wq, Wk, Wv, proj_w, proj_b):
        import jax, jax.numpy as jnp
        import numpy as np
        B, T, E = (4, 256, 128)
        H, HS = (16, 64)
        b, t, e = x.shape
        h, _, hs = Wq.shape
        q = jnp.einsum('bxy,iyk->bxik', x, Wq).reshape(h, b, t, hs)
        k = jnp.einsum('bxy,iyk->bxik', x, Wk).reshape(h, b, t, hs)
        v = jnp.einsum('bxy,iyk->bxik', x, Wv).reshape(h, b, t, hs)
        wei = jnp.einsum('hbqd,hbkd->hbqk', q, k) * hs ** (-0.5)
        causal = jnp.tril(jnp.ones((t, t), dtype=bool))
        wei = jnp.where(causal, wei, -jnp.inf)
        wei = jax.nn.softmax(wei, axis=-1)
        out = jnp.einsum('hbqk,hbkd->hbqd', wei, v)
        out = out.reshape(b, t, h * hs)
        out = out @ proj_w.T + proj_b
        return out

    def _L1_ffn_ref(h, gate_w, w1, b1, w2, b2):
        import jax, jax.numpy as jnp
        import numpy as np
        B, S, D, E, F = (2, 128, 128, 14, 256)
        Bb, Ss, Dd = h.shape
        x = h.reshape(Bb * Ss, Dd)
        logits = x @ gate_w.T
        probs = jax.nn.softmax(logits, axis=-1)
        top2_p, top2_i = jax.lax.top_k(probs, 2)
        w = top2_p / jnp.maximum(top2_p.sum(-1, keepdims=True), 1e-10)
        hh = jnp.einsum('nd,edf->nef', x, w1) + b1
        hh = jax.nn.gelu(hh, approximate=False)
        all_out = jnp.einsum('nef,efd->ned', hh, w2) + b2
        n = jnp.arange(x.shape[0])
        out0 = all_out[n, top2_i[:, 0]]
        out1 = all_out[n, top2_i[:, 1]]
        moe_out = w[:, 0:1] * out0 + w[:, 1:2] * out1
        result = jnp.clip(x + moe_out, -100.0, 100.0).reshape(Bb, Ss, Dd)
        return result
    x = L0_attn_x
    x = _layernorm(x + _L0_attn_ref(x, L0_attn_Wq, L0_attn_Wk, L0_attn_Wv, L0_attn_Wo, L0_attn_bo), axis=-1)
    x = _layernorm(x + _L0_ffn_ref(x, L0_ffn_q_w, L0_ffn_q_b, L0_ffn_k_w, L0_ffn_k_b, L0_ffn_v_w, L0_ffn_v_b, L0_ffn_o_w, L0_ffn_o_b, L0_ffn_router_w, L0_ffn_router_b, L0_ffn_w1, L0_ffn_b1, L0_ffn_w2, L0_ffn_b2), axis=-1)
    x = _layernorm(x + _L1_attn_ref(x, L1_attn_Wq, L1_attn_Wk, L1_attn_Wv, L1_attn_proj_w, L1_attn_proj_b), axis=-1)
    x = _layernorm(x + _L1_ffn_ref(x, L1_ffn_gate_w, L1_ffn_w1, L1_ffn_b1, L1_ffn_w2, L1_ffn_b2), axis=-1)
    return x

_drawn_inputs = setup_inputs


def setup_inputs(seed=0):
    import zlib

    import numpy as np

    out = dict(_drawn_inputs(seed))
    spreads = {'L0_attn_bo': (0.0, 0.1),
     'L0_ffn_q_b': (0.0, 0.8),
     'L0_ffn_k_b': (0.0, 0.8),
     'L0_ffn_v_b': (0.0, 0.8),
     'L0_ffn_o_b': (0.0, 0.318),
     'L0_ffn_router_b': (0.0, 0.348),
     'L0_ffn_b1': (0.0, 0.8),
     'L0_ffn_b2': (0.0, 0.326),
     'L1_ffn_b1': (0.0, 0.333),
     'L1_ffn_b2': (0.0, 0.1)}
    factors = {'L0_ffn_q_w': 8.0,
     'L0_ffn_k_w': 8.0,
     'L0_ffn_v_w': 8.0,
     'L0_ffn_o_w': 8.0,
     'L0_ffn_router_w': 3.27,
     'L0_ffn_w1': 8.0,
     'L0_ffn_w2': 6.548,
     'L1_attn_Wq': 8.0,
     'L1_attn_Wk': 8.0}
    for name, (base, spread) in spreads.items():
        noise = np.random.default_rng([zlib.crc32(name.encode()), seed]).standard_normal(out[name].shape)
        drawn = base * np.exp(spread * noise) if base else spread * noise
        out[name] = jnp.asarray(drawn.astype(out[name].dtype))
    for name, factor in factors.items():
        out[name] = (out[name] * factor).astype(out[name].dtype)
    return out
```

```python
from contextlib import ExitStack, contextmanager

import concourse.bass as bass
from concourse import mybir

F32 = mybir.dt.float32
F32R = mybir.dt.float32r
BF16 = mybir.dt.bfloat16
ALU = mybir.AluOpType
ACT = mybir.ActivationFunctionType
AX = mybir.AxisListType

P = 128
D = 128
B, S = 2, 1024
NT = B * S
NC = NT // P
H = 16
BANK = 512
NB = NT // BANK
CB = BANK // P
CH = S // P
G = 4
HG = H // G
ONE = 8
MROW = 24
GW = 4 * P + 2
E0, E1 = 8, 14
F = 256
FC = F // P
HS = 64
XP = S // H
NP = NT // XP
EPS = 1e-5


class Phase:

    def __init__(self, nc, tag):
        self.nc, self.tag, self.buffers, self.semaphores = nc, tag, ExitStack(), []

    def sb(self, name, shape, dt=F32):
        return self.buffers.enter_context(self.nc.sbuf_tensor(f"{self.tag}_{name}", shape, dt))

    def sem(self, name):
        self.semaphores.append(self.nc.alloc_semaphore(name=f"{self.tag}_{name}"))
        return self.semaphores[-1]

    @contextmanager
    def block(self):
        with self.buffers:
            with self.nc.Block() as block:
                yield block
            self.nc.clear_and_free_semaphores(self.semaphores)
            self.nc.all_engine_barrier()


class Banks:

    def __init__(self, ph, tensors):
        self.full = [ph.sem(f"bank{i}_full") for i in range(2)]
        self.free = [ph.sem(f"bank{i}_free") for i in range(2)]
        self.tensors = tensors

    def claim(self, pe, half, k):
        if not (isinstance(half, int) and half + k // 2 == 0):
            pe.wait_ge(self.free[k % 2], half + k // 2)
        return self.tensors[k % 2]

    def filled(self, eng, half, k):
        eng.wait_ge(self.full[k % 2], half + k // 2 + 1)
        return self.tensors[k % 2]

    def read(self, eng, half, k):
        eng.wait_ge(self.free[k % 2], half + k // 2 + 1)

    def all_read(self, eng, half, k=0):
        if not (isinstance(half, int) and half + k == 0):
            eng.wait_ge(self.free[0], half + (k + 1) // 2)
            eng.wait_ge(self.free[1], half + k // 2)


def group_units(causal, proj, smax, den):
    u = []
    if den:
        u += [("den", 0), ("den", 1)]
    for k in range(1, CH + 1):
        if smax:
            for j in range(HG):
                u += [("max", k - 1, j, h) for h in range(key_tiles(causal, k - 1))]
        if k == 1 and smax:
            u += [("v", 0), ("v", 1)]
        if k == 2 and proj:
            u += [("k", 0), ("k", 1)]
        if k == 3 and proj:
            u += [("q", 0), ("q", 1)]
        if k in (5, 8) and smax:
            u += [("t", 0 if k == 5 else 1)]
    return {x: n for n, x in enumerate(u)}


def key_tiles(causal, c):
    return 1 if causal and c < CB else 2


def pieces(q0):
    return [(max(q0, a), a + BANK) for a in range(0, S, BANK) if q0 < a + BANK]


def load_phase(nc, K, src):
    ph = Phase(nc, "load")
    mf = [ph.sb(f"maskf{i}", [P, P]) for i in range(2)]
    s_in, s_x, s_b = ph.sem("in"), ph.sem("x"), ph.sem("cast")
    banks = Banks(ph, K.work)
    X, XT = K.X, K.XT
    xv = src["x"].rearrange("b (c p) d -> p (b c) d", p=P)
    with ph.block() as block:

        @block.sync
        def _(sp):
            sp.dma_start(K.ident[:], src["ident"]).then_inc(s_in, 16)
            for n in range(NB):
                sp.dma_start(X[:, CB * n:CB * n + CB, :], xv[:, CB * n:CB * n + CB, :]).then_inc(s_x, 16)

        @block.scalar
        def _(act):
            act.dma_start(mf[0][:], src["maskq"]).then_inc(s_b, 16)
            act.dma_start(mf[1][:], src["maskk"]).then_inc(s_b, 16)
            for n in range(NB):
                t = banks.filled(act, 0, n)
                act.activation(XT[:, BANK * n:BANK * n + BANK], t[:], ACT.Copy).then_inc(banks.free[n % 2], 1)

        @block.vector
        def _(dve):
            dve.wait_ge(s_b, 32)
            dve.tensor_copy(K.maskq[:], mf[0][:])
            dve.tensor_copy(K.maskk[:], mf[1][:])
            dve.wait_ge(s_in, 16)
            dve.tensor_copy(K.identb[:], K.ident[:])

        @block.tensor
        def _(pe):
            pe.wait_ge(s_in, 16)
            for n in range(NB):
                pe.wait_ge(s_x, 16 * NB)
                t = banks.claim(pe, 0, n)
                for c in range(CB):
                    last = pe.transpose(t[:, P * c:P * c + P], X[:, CB * n + c, :], K.ident[:])
                last.then_inc(banks.full[n % 2], 1)


def groups_phase(nc, K, src, tag, causal, scale):
    ph = Phase(nc, tag)
    ident, XT, CT = K.ident, K.XT, K.CT
    gw = ph.sb("gw", [P, G, GW])
    wkq = ph.sb("wkq", [P, 2 * P + 2])
    wv = ph.sb("wv", [P, 2 * P])
    negc = ph.sb("negc", [P, 2])
    sel = ph.sb("sel", [P, P])
    raw = ph.sb("raw", [P, 2, BANK])
    hi = ph.sb("hi", [P, 2, BANK], F32R)
    kc = ph.sb("kc", [P, S], F32R)
    kpad = [ph.sb(f"kpad{i}", [P, HG, S], F32R) for i in range(2)]
    qp = [ph.sb(f"qp{i}", [P, S], F32R) for i in range(2)]
    qa = [ph.sb(f"qa{i}", [P, S], F32R) for i in range(2)]
    v = [ph.sb(f"v{i}", [P, CH, P]) for i in range(2)]
    pr = [[ph.sb(f"p{i}{j}", [P, S]) for j in range(HG)] for i in range(2)]
    mx = ph.sb("mx", [P, 2, HG, 2])
    mz = ph.sb("mz", [P, CH, P])
    oe = ph.sb("oe", [P, S])
    rd = ph.sb("rd", [P, 2, BANK])
    credit = ph.sb("credit", [P, 4])

    banks = Banks(ph, K.work)
    s_alone = ph.sem("alone")
    s_load = ph.sem("loaded")
    s_zero = ph.sem("zeroed")
    s_wkq = ph.sem("wkq_staged")
    s_wv = ph.sem("wv_staged")
    s_hi = ph.sem("hi_made")
    s_kc = ph.sem("kc_made")
    s_qp = ph.sem("qp_made")
    s_kpad = ph.sem("kpad_staged")
    s_mz = ph.sem("maxima")
    s_st = ph.sem("scores_t")
    s_p = ph.sem("exp_done")
    s_pv = ph.sem("pv_done")
    s_oe = ph.sem("outputs_evacuated")
    s_ct = ph.sem("context_made")

    first = group_units(causal, True, False, False)
    second = group_units(causal, True, True, False)
    full = group_units(causal, True, True, True)
    tail = group_units(causal, False, True, True)
    ends = group_units(causal, False, False, True)
    U, half0 = len(full) // 2, (len(first) + len(second)) // 2
    NQ = sum(key_tiles(causal, c) == 2 for c in range(CH))

    def q0_of(c):
        return P * c if causal else 0

    def turns(eng, body):
        body(-2, -1, 0, first, 0, False, False, True)
        body(-1, -1, 1, second, len(first) // 2, False, True, True)
        with eng.Fori(0, G - 1) as g:
            for p in range(B):
                body(2 * g + p, g, p, full, (2 * g + p) * U + half0, True, True, True)
        t, before = B * (G - 1), B * (G - 1) * U + half0
        body(t, G - 1, 0, tail, before, True, True, False)
        body(t + 1, G - 1, 1, ends, before + len(tail) // 2, True, False, False)
        body(t + 2, G, 0, ends, before + len(tail) // 2 + 1, False, False, False)

    def is_den(units):
        return ("den", 0) in units

    with ph.block() as block:

        @block.sync
        def _(sp):
            sp.dma_start(gw[:], src["gw"]).then_inc(s_load, 16)
            sp.dma_start(negc[:], src["negc"]).then_inc(s_load, 16)
            sp.dma_start(sel[:], src["sel"]).then_inc(s_load, 16)
            sp.wait_ge(s_zero, 4)

            def body(t, g, p, units, half, st, smax, proj):
                if smax:
                    sp.wait_ge(s_kc, 2 * (t + 2))
                    sp.sem_inc(s_alone, 1)
                    if st:
                        sp.wait_ge(s_p, HG * CH * t + 2)
                        sp.sem_inc(s_alone, 1)
                    for j in range(HG):
                        r = slice(32 * j, 32 * j + 32)
                        sp.dma_start(kpad[1 - p][r, j, :].bitcast(F32), kc[r, :].bitcast(F32)).then_inc(s_kpad, 16)

            turns(sp, body)

        @block.gpsimd
        def _(pool):
            pool.memset(kpad[0][:].bitcast(F32), 0.0).then_inc(s_zero, 1)
            pool.memset(kpad[1][:].bitcast(F32), 0.0).then_inc(s_zero, 1)
            pool.memset(mz[:], 0.0).then_inc(s_zero, 1)
            pool.memset(oe[:], 1.0).then_inc(s_zero, 1)
            pool.memset(credit[:, 0:1], 0.0).then_inc(s_p, 2)
            pool.memset(credit[:, 2:3], 0.0).then_inc(s_oe, 1)
            pool.memset(credit[:, 1:2], 0.0).then_inc(s_pv, 2)
            pool.wait_ge(s_load, 48)

            def body(t, g, p, units, half, st, smax, proj):
                if st and (proj or smax):
                    banks.all_read(pool, half)
                pool.sem_inc(s_alone, 1)
                if proj and p == 0:
                    pool.tensor_copy(wkq[:, 0:2 * P], gw[:, g + 1, 0:2 * P])
                    pool.tensor_copy(wkq[:, 2 * P:], gw[:, g + 1, 4 * P:]).then_inc(s_wkq, 1)
                if smax and p == 1:
                    pool.tensor_copy(wv[:], gw[:, g + 1, 2 * P:4 * P]).then_inc(s_wv, 1)
                if proj:
                    for w, (dst, s_dst, what) in enumerate(((kc, s_kc, 0), (kc, s_kc, 0),
                                                            (qp[p], s_qp, 1), (qp[p], s_qp, 1))):
                        n = w % 2
                        banks.read(pool, half, units["kq"[what], n])
                        if w >= 2:
                            pool.wait_ge(s_kc, 2 * (t + 2) + n + 1)
                        elif isinstance(t, int) and t == -2:
                            pass
                        else:
                            pool.wait_ge(s_qp, 2 * (t + 2) + n - 1)
                        pool.sem_inc(s_alone, 1)
                        pool.tensor_scalar(hi[:, n, :], raw[:, n, :], negc[:, what:what + 1], None,
                                           ALU.mult).then_inc(s_hi, 1)
                        if w == 0 and smax:
                            pool.wait_ge(s_kpad, 16 * HG * (t + 2))
                        pool.wait_ge(s_hi, 4 * (t + 2) + w + 1)
                        pool.tensor_tensor(dst[:, BANK * n:BANK * n + BANK], raw[:, n, :],
                                           hi[:, n, :].bitcast(F32), ALU.add).then_inc(s_dst, 1)

            turns(pool, body)

        @block.scalar
        def _(act):
            def body(t, g, p, units, half, st, smax, proj):
                if not st:
                    return
                for k in range(CH):
                    q0 = q0_of(k)
                    act.wait_ge(s_pv, CH * t + k + 1)
                    for j in range(HG):
                        act.wait_ge(s_st, HG * (CH * t + k) + j + 1)
                        act.activation(pr[k % 2][j][:, q0:], K.st[j % 2][:, q0:], ACT.Exp,
                                       scale=scale).then_inc(s_p, 1)
                act.wait_ge(s_pv, CH * t + CH + 2)
                act.wait_ge(s_ct, 2 * (t + 1))
                act.activation(oe[:], K.o_ps[:], ACT.Copy).then_inc(s_oe, 1)

            turns(act, body)

        @block.vector
        def _(dve):
            dve.wait_ge(s_zero, 4)
            dve.wait_ge(s_load, 48)

            def body(t, g, p, units, half, st, smax, proj):
                if is_den(units):
                    for h in range(2):
                        n = units["den", h]
                        w = banks.filled(dve, half, n)
                        dve.reciprocal(rd[:, h, :], w[:]).then_inc(banks.free[n % 2], 1)
                        banks.read(dve, half, n)
                        dve.tensor_tensor(CT[:, t, BANK * h:BANK * h + BANK],
                                          oe[:, BANK * h:BANK * h + BANK], rd[:, h, :],
                                          ALU.mult).then_inc(s_ct, 1)
                for k in range(1, CH + 1):
                    c = k - 1
                    if smax:
                        tiles = key_tiles(causal, c)
                        for j in range(HG):
                            for h in range(tiles):
                                n = units["max", c, j, h]
                                w = banks.filled(dve, half, n)
                                cols = min(BANK, P * (c + 1) - BANK * h) if causal else BANK
                                dst = mx[:, c % 2, j, h:h + 1] if tiles == 2 else \
                                    mz[:, c, 32 * j + MROW:32 * j + MROW + 1]
                                dve.reduce_max(dst, w[:, 0:cols], AX.X, negate=True)\
                                   .then_inc(banks.free[n % 2], 1)
                        if tiles == 2:
                            banks.read(dve, half, n - 1)
                            banks.read(dve, half, n)
                            dve.tensor_tensor(mz[:, c, MROW::32], mx[:, c % 2, :, 0], mx[:, c % 2, :, 1],
                                              ALU.min).then_inc(s_mz, 1)
                    if k == 1 and smax:
                        for h in range(2):
                            n = units["v", h]
                            w = banks.filled(dve, half, n)
                            dve.tensor_tensor(v[1 - p][:, CB * h:CB * h + CB, :],
                                              w[:].rearrange("p (c d) -> p c d", d=P),
                                              wv[:, P:].unsqueeze(1).broadcast_to([P, CB, P]),
                                              ALU.add).then_inc(banks.free[n % 2], 1)
                    if k in (2, 3) and proj:
                        for h in range(2):
                            n = units["kq"[k - 2], h]
                            w = banks.filled(dve, half, n)
                            if k == 2 and smax:
                                dve.wait_ge(s_qp, 2 * (t + 1) + h + 1)
                            if k == 3:
                                dve.wait_ge(s_kc, 2 * (t + 2) + h + 1)
                            dve.tensor_scalar(raw[:, h, :], w[:], wkq[:, 2 * P + k - 2:2 * P + k - 1], None,
                                              ALU.add).then_inc(banks.free[n % 2], 1)
                    if k in (5, 8) and smax:
                        n = units["t", k // 8]
                        w = banks.filled(dve, half, n)
                        a = slice(BANK * (k // 8), BANK * (k // 8) + BANK)
                        dve.tensor_tensor(qa[1 - p][:, a], qp[1 - p][:, a].bitcast(F32), w[:],
                                          ALU.add).then_inc(banks.free[n % 2], 1)

            turns(dve, body)

        @block.tensor
        def _(pe):
            pe.wait_ge(s_load, 48)
            pe.wait_ge(s_zero, 4)

            def weigh(k, h, t, p):
                a, b = max(q0_of(k), BANK * h), BANK * h + BANK
                if a >= b:
                    return None
                last_k = CB * h + CB - 1 if causal else CH - 1
                for j in range(HG):
                    r = slice(32 * j, 32 * j + 32)
                    last = pe.matmul(K.o_ps[r, a:b], v[p][:, k, r], pr[k % 2][j][:, a:b],
                                     start=(k == 0), stop=(k == last_k))
                return last

            def body(t, g, p, units, half, st, smax, proj):
                banks.all_read(pe, half)
                if st:
                    pe.wait_ge(s_kpad, 16 * HG * (t + 1))
                for k in range(CH + 1):
                    if k == 1 and smax:
                        pe.wait_ge(s_kpad, 16 * HG * (t + 2))
                        pe.wait_ge(s_qp, 2 * (t + 2))
                    for j in range(HG):
                        if smax and k >= 1:
                            c = k - 1
                            for h in range(key_tiles(causal, c)):
                                n = units["max", c, j, h]
                                w = banks.claim(pe, half, n)
                                cols = min(BANK, P * (c + 1) - BANK * h) if causal else BANK
                                diag = causal and BANK * h + cols == P * (c + 1)
                                last = pe.matmul(w[:, 0:cols], qp[1 - p][:, P * c:P * c + P],
                                                 kpad[1 - p][:, j, BANK * h:BANK * h + cols],
                                                 start=True, stop=not diag)
                                if diag:
                                    last = pe.matmul(w[:, cols - P:cols], K.identb[:], K.maskq[:],
                                                     start=False, stop=True)
                                last.then_inc(banks.full[n % 2], 1)
                        if st and k < CH:
                            m = HG * (CH * t + k) + j
                            pe.wait_ge(s_p, m + 1)
                            for a, b in pieces(q0_of(k)):
                                diag = causal and a == q0_of(k)
                                last = pe.matmul(K.st[j % 2][:, a:b], kpad[p][:, j, P * k:P * k + P],
                                                 qa[p][:, a:b], start=True, stop=not diag)
                                if diag:
                                    last = pe.matmul(K.st[j % 2][:, a:a + P], K.identb[:], K.maskk[:],
                                                     start=False, stop=True)
                            last.then_inc(s_st, 1)
                        if st and k >= 1 and j % 2 == 1:
                            if j == 1:
                                pe.wait_ge(s_p, HG * (CH * t + k) + 2)
                                if k == 1:
                                    pe.wait_ge(s_oe, t + 1)
                            last = weigh(k - 1, j // 2, t, p)
                            if j == 3:
                                last.then_inc(s_pv, 1)
                    if k == 0 and is_den(units):
                        pe.wait_ge(s_oe, t + 1)
                        for h in range(2):
                            n = units["den", h]
                            w = banks.claim(pe, half, n)
                            pe.matmul(w[:], sel[:], oe[:, BANK * h:BANK * h + BANK],
                                      start=True, stop=True).then_inc(banks.full[n % 2], 1)
                    if k == 1 and smax:
                        pe.wait_ge(s_wv, g + 1 + p)
                        for h in range(2):
                            n = units["v", h]
                            w = banks.claim(pe, half, n)
                            for c in range(CB):
                                a = (1 - p) * S + P * (CB * h + c)
                                last = pe.matmul(w[:, P * c:P * c + P], XT[:, a:a + P], wv[:, 0:P],
                                                 start=True, stop=True)
                            last.then_inc(banks.full[n % 2], 1)
                    if k in (2, 3) and proj:
                        pe.wait_ge(s_wkq, g + 2)
                        for h in range(2):
                            n = units["kq"[k - 2], h]
                            w = banks.claim(pe, half, n)
                            pe.matmul(w[:], wkq[:, P * (k - 2):P * (k - 1)],
                                      XT[:, p * S + BANK * h:p * S + BANK * h + BANK],
                                      start=True, stop=True).then_inc(banks.full[n % 2], 1)
                    if k in (5, 8) and smax:
                        i = k // 8
                        n = units["t", i]
                        w = banks.claim(pe, half, n)
                        ready = sum(key_tiles(causal, c) == 2 for c in range(CB * i + CB))
                        if ready:
                            pe.wait_ge(s_mz, NQ * (t + 1) + ready)
                        for c in range(CB):
                            last = pe.transpose(w[:, P * c:P * c + P], mz[:, CB * i + c, :], ident[:])
                        last.then_inc(banks.full[n % 2], 1)

            turns(pe, body)


class Kept:

    def __init__(self, nc, stack):
        def sb(name, shape, dt=F32):
            return stack.enter_context(nc.sbuf_tensor(name, shape, dt))

        self.X = sb("X", [P, NC, D])
        self.XT = sb("XT", [D, NT])
        self.CT = None
        self.xh = sb("xh", [D, NT], F32R)
        self.xl = sb("xl", [D, NT], F32R)
        self.comb = sb("comb", [P, E1, NC])
        self.acc_slots = sb("acc", [P, NC + 1, D])
        self.acc = self.acc_slots[:, 1:, :]
        self.ident = sb("ident_sb", [P, P])
        self.identb = sb("identb", [P, P], BF16)
        self.maskq = sb("maskq_sb", [P, P], BF16)
        self.maskk = sb("maskk_sb", [P, P], BF16)
        self.st = [stack.enter_context(nc.psum_tensor(f"st{i}", [P, S], F32)) for i in range(2)]
        self.work = [stack.enter_context(nc.psum_tensor(f"work{i}", [P, BANK], F32)) for i in range(2)]
        self.o_ps = stack.enter_context(nc.psum_tensor("o_ps", [P, S], F32))


def norm_phase(nc, K, src, tag, add, out=None):
    ph = Phase(nc, tag)
    X, XT, CT = K.X, K.XT, K.CT
    bias = ph.sb("bias", [P, D])
    wo = ph.sb("wo", [P, G, D])
    z = ph.sb("z", [P, 2, CB, D])
    stats = ph.sb("stats", [P, 2, CB, 6])
    mv = ph.sb("mv", [P, 2, CB, 2])
    var = ph.sb("var", [P, 2, CB])
    std = ph.sb("std", [P, 2, CB])
    rs = ph.sb("rs", [P, 2, CB])
    banks = Banks(ph, K.work)
    s_load, s_v, s_var, s_std, s_x, s_out = (ph.sem(x) for x in ("loaded", "step", "variance", "std", "x", "out"))
    s_y = ph.sem("projected")
    s_yr = ph.sem("projection_read")
    needs = {"context": 32, "rows": 16}.get(add, 0)

    with ph.block() as block:

        @block.sync
        def _(sp):
            if add == "context":
                sp.dma_start(wo[:], src["wo"]).then_inc(s_load, 16)
            if needs:
                sp.dma_start(bias[:], src["bias"].partition_broadcast(P)).then_inc(s_load, 16)
            if out is not None:
                ov = out.rearrange("b (c p) d -> p (b c) d", p=P)
                for n in range(NB):
                    sp.wait_ge(s_x, n + 1)
                    sp.dma_start(ov[:, CB * n:CB * n + CB, :], X[:, CB * n:CB * n + CB, :]).then_inc(s_out, 16)
                sp.wait_ge(s_out, 16 * NB)

        @block.scalar
        def _(act):
            for n in range(NB):
                act.wait_ge(s_var, n + 1)
                act.activation(std[:, n % 2, :], var[:, n % 2, :], ACT.Sqrt).then_inc(s_std, 1)
                if out is None and n:
                    w = banks.filled(act, 0, n - 1)
                    act.activation(XT[:, BANK * (n - 1):BANK * n], w[:], ACT.Copy)\
                       .then_inc(banks.free[(n - 1) % 2], 1)
            if out is None:
                w = banks.filled(act, 0, NB - 1)
                act.activation(XT[:, BANK * (NB - 1):], w[:], ACT.Copy).then_inc(banks.free[(NB - 1) % 2], 1)

        @block.vector
        def _(dve):
            steps = [0]

            def then(ins):
                steps[0] += 1
                ins.then_inc(s_v, 1)
                dve.wait_ge(s_v, steps[0])

            if needs:
                dve.wait_ge(s_load, needs)
            for n in range(NB):
                xs, zs = X[:, CB * n:CB * n + CB, :], z[:, n % 2]
                bc = bias[:].unsqueeze(1).broadcast_to([P, CB, D])
                if add == "context":
                    dve.wait_ge(s_y, n + 1)
                    w = K.st[n % 2][:, 0:BANK].rearrange("p (c d) -> p c d", d=D)
                    ins = dve.tensor_tensor(zs, w, xs, ALU.add)
                    ins.then_inc(s_yr, 1)
                    dve.wait_ge(s_yr, n + 1)
                    then(dve.tensor_tensor(zs, zs, bc, ALU.add))
                elif add == "moe":
                    then(dve.scalar_tensor_tensor(zs, K.acc[:, CB * n:CB * n + CB, :], 0.3, xs, ALU.mult, ALU.add))
                    then(dve.tensor_tensor(zs, zs, xs, ALU.add))
                elif add == "rows":
                    then(dve.tensor_tensor(zs, K.acc[:, CB * n:CB * n + CB, :], xs, ALU.add))
                    then(dve.tensor_tensor(zs, zs, bc, ALU.add))
                else:
                    then(dve.tensor_tensor(zs, K.acc[:, CB * n:CB * n + CB, :], xs, ALU.add))
                    then(dve.tensor_scalar(zs, zs, -100.0, 100.0, ALU.max, ALU.min))
                    then(dve.tensor_tensor(zs, zs, xs, ALU.add))
                for c in range(CB):
                    last = dve.bn_stats(stats[:, n % 2, c, :], z[:, n % 2, c, :])
                then(last)
                for c in range(CB):
                    last = dve.bn_aggr(mv[:, n % 2, c, :], stats[:, n % 2, c, :])
                then(last)
                dve.tensor_scalar(var[:, n % 2, :], mv[:, n % 2, :, 1], EPS, None, ALU.add).then_inc(s_var, 1)
                dve.wait_ge(s_std, n + 1)
                then(dve.reciprocal(rs[:, n % 2, :], std[:, n % 2, :]))
                for c in range(CB):
                    last = dve.tensor_scalar(X[:, CB * n + c, :], z[:, n % 2, c, :], mv[:, n % 2, c, 0:1],
                                             rs[:, n % 2, c:c + 1], ALU.subtract, ALU.mult)
                last.then_inc(s_x, 1)

        @block.tensor
        def _(pe):
            if add == "context":
                pe.wait_ge(s_load, 32)

            def project(n):
                if n >= 2:
                    pe.wait_ge(s_yr, n - 1)
                for c in range(CB):
                    b, a = divmod(P * (CB * n + c), S)
                    for g in range(G):
                        last = pe.matmul(K.st[n % 2][:, P * c:P * c + P], CT[:, B * g + b + 1, a:a + P],
                                         wo[:, g, :], start=(g == 0), stop=(g == G - 1))
                last.then_inc(s_y, 1)

            if add == "context":
                project(0)
            for n in range(NB):
                if add == "context" and n + 1 < NB:
                    project(n + 1)
                if out is None:
                    pe.wait_ge(s_x, n + 1)
                    w = banks.claim(pe, 0, n)
                    for c in range(CB):
                        last = pe.transpose(w[:, P * c:P * c + P], X[:, CB * n + c, :], K.ident[:])
                    last.then_inc(banks.full[n % 2], 1)


def route_phase(nc, K, src, tag, experts, latent, floor, plus):
    ph = Phase(nc, tag)
    E = experts
    CT = K.CT
    wo = ph.sb("wo", [P, G, D])
    ob = ph.sb("ob", [P, 1])
    rw = ph.sb("rw", [D, E])
    rb = ph.sb("rb", [P, E])
    rank = ph.sb("rank", [P, E])
    lg = ph.sb("lg", [P, NC, E])
    pb = ph.sb("probs", [P, NC, E])
    eq = ph.sb("eq", [P, NC, E])
    one = ph.sb("one", [P, 2, NC, E])
    m = ph.sb("m", [P, 8, NC])
    MT = ph.sb("MT", [D, NT]) if latent else K.XT
    s_load, s_lg, s_v, s_e, s_s = (ph.sem(x) for x in ("loaded", "logits", "step", "shifted", "exp"))
    s_hi, s_lo = ph.sem("hi"), ph.sem("lo")
    s_mt = ph.sem("mt")
    banks = Banks(ph, K.work)

    def over(x):
        return x.unsqueeze(2).broadcast_to([P, NC, E])

    with ph.block() as block:

        @block.sync
        def _(sp):
            sp.dma_start(rw[:], src["rw"]).then_inc(s_load, 16)
            sp.dma_start(rank[:], src["rank"]).then_inc(s_load, 16)
            sp.dma_start(rb[:], src["rb"].partition_broadcast(P)).then_inc(s_load, 16)
            if latent:
                sp.dma_start(wo[:], src["wo"]).then_inc(s_load, 16)
                sp.dma_start(ob[:], src["ob"]).then_inc(s_load, 16)

        @block.scalar
        def _(act):
            if latent:
                act.wait_ge(s_load, 80)
                for n in range(NB):
                    w = banks.filled(act, 0, n)
                    act.activation(MT[:, BANK * n:BANK * n + BANK], w[:], ACT.Identity,
                                   bias=ob[:]).then_inc(banks.free[n % 2], 1)
            act.wait_ge(s_e, 1)
            act.activation(pb[:], lg[:], ACT.Exp).then_inc(s_s, 1)

        @block.gpsimd
        def _(pool):
            for n in range(NB):
                a = slice(BANK * n, BANK * n + BANK)
                if latent:
                    banks.read(pool, 0, n)
                pool.tensor_copy(K.xh[:, a], MT[:, a]).then_inc(s_hi, 1)
                pool.wait_ge(s_hi, n + 1)
                pool.tensor_tensor(K.xl[:, a], MT[:, a], K.xh[:, a].bitcast(F32), ALU.subtract).then_inc(s_lo, 1)

        @block.vector
        def _(dve):
            steps = [0]

            def then(ins):
                steps[0] += 1
                ins.then_inc(s_v, 1)
                dve.wait_ge(s_v, steps[0])

            dve.wait_ge(s_load, 80 if latent else 48)
            dve.wait_ge(s_lg, 1)
            w = K.o_ps[:, 0:NC * E].rearrange("p (c e) -> p c e", e=E)
            then(dve.tensor_tensor(lg[:], w, rb[:].unsqueeze(1).broadcast_to([P, NC, E]), ALU.add))
            then(dve.reduce_max(m[:, 0, :], lg[:], AX.X))
            dve.tensor_tensor(lg[:], lg[:], over(m[:, 0, :]), ALU.subtract).then_inc(s_e, 1)
            dve.wait_ge(s_s, 1)
            then(dve.reduce_sum(m[:, 1, :], pb[:], AX.X))
            then(dve.reciprocal(m[:, 2, :], m[:, 1, :]))
            then(dve.tensor_tensor(pb[:], pb[:], over(m[:, 2, :]), ALU.mult))
            for i in range(2):
                then(dve.reduce_max(m[:, 3 + i, :], pb[:], AX.X))
                then(dve.tensor_tensor(eq[:], pb[:], over(m[:, 3 + i, :]), ALU.is_equal))
                then(dve.tensor_tensor(eq[:], eq[:], rank[:].unsqueeze(1).broadcast_to([P, NC, E]), ALU.mult))
                then(dve.reduce_max(m[:, 5, :], eq[:], AX.X))
                then(dve.tensor_tensor(one[:, i], eq[:], over(m[:, 5, :]), ALU.is_equal))
                if i == 0:
                    then(dve.scalar_tensor_tensor(pb[:], one[:, 0], -4.0, pb[:], ALU.mult, ALU.add))
            then(dve.tensor_tensor(m[:, 6, :], m[:, 3, :], m[:, 4, :], ALU.add))
            then(dve.tensor_scalar(m[:, 6, :], m[:, 6, :], plus, floor, ALU.add, ALU.max))
            then(dve.reciprocal(m[:, 7, :], m[:, 6, :]))
            for i in range(2):
                then(dve.tensor_tensor(m[:, 3 + i, :], m[:, 3 + i, :], m[:, 7, :], ALU.mult))
                then(dve.tensor_tensor(one[:, i], one[:, i], over(m[:, 3 + i, :]), ALU.mult))
            then(dve.tensor_tensor(K.comb[:, 0:E, :].rearrange("p e c -> p c e"), one[:, 0], one[:, 1], ALU.add))

        @block.tensor
        def _(pe):
            pe.wait_ge(s_load, 80 if latent else 48)
            if latent:
                for n in range(NB):
                    w = banks.claim(pe, 0, n)
                    b, a = divmod(BANK * n, S)
                    for g in range(G):
                        last = pe.matmul(w[:], wo[:, g, :], CT[:, B * g + b + 1, a:a + BANK],
                                         start=(g == 0), stop=(g == G - 1))
                    last.then_inc(banks.full[n % 2], 1)
                banks.read(pe, 0, NB - 2)
                banks.read(pe, 0, NB - 1)
            for c in range(NC):
                last = pe.matmul(K.o_ps[:, E * c:E * c + E], MT[:, P * c:P * c + P], rw[:], start=True, stop=True)
            last.then_inc(s_lg, 1)


def experts_phase(nc, K, src, tag, experts):
    ph = Phase(nc, tag)
    E = experts
    w1 = [ph.sb(f"w1{i}", [D, F]) for i in range(2)]
    w2 = [ph.sb(f"w2{i}", [P, FC, D]) for i in range(2)]
    b1 = [ph.sb(f"b1{i}", [P, FC]) for i in range(2)]
    b2 = [ph.sb(f"b2{i}", [P, D]) for i in range(2)]
    w1h = [ph.sb(f"w1h{i}", [D, F], F32R) for i in range(2)]
    w1l = [ph.sb(f"w1l{i}", [D, F], F32R) for i in range(2)]
    hid = [ph.sb(f"hid{i}", [P, FC, BANK]) for i in range(2)]
    y = [ph.sb(f"y{i}", [P, CB, D]) for i in range(2)]
    credit = ph.sb("credit", [P, 4])
    s_w = [ph.sem(f"weights{i}") for i in range(2)]
    s_alone = ph.sem("alone")
    s_wh, s_ws = ph.sem("w1_hi"), ph.sem("w1_split")
    s_up, s_g, s_dn, s_y, s_yc, s_a = (ph.sem(x) for x in ("up", "gelu", "down", "biased", "weighted", "added"))

    with ph.block() as block:

        def pairs(eng, body):
            with eng.Fori(0, E // 2) as q:
                for p in range(2):
                    body(2 * q + p, q, p)

        @block.sync
        def _(sp):
            def body(e, q, p):
                sp.wait_ge(s_yc, NB * e + 1)
                sp.sem_inc(s_alone, 1)
                sp.dma_start(w1[p][:], src["w1"][e]).then_inc(s_w[p], 16)
                sp.dma_start(w2[p][:], src["w2"][e].rearrange("(c p) d -> p c d", p=P))\
                  .then_inc(s_w[p], 16)
                sp.dma_start(b1[p][:], src["b1"][e]).then_inc(s_w[p], 16)
                sp.dma_start(b2[p][:], src["b2"][e].partition_broadcast(P))\
                  .then_inc(s_w[p], 16)

            pairs(sp, body)

        @block.gpsimd
        def _(pool):
            pool.memset(K.acc, 0.0).then_inc(s_a, 2)
            pool.memset(credit[:, 0:1], 0.0).then_inc(s_g, 4)
            pool.memset(credit[:, 1:2], 0.0).then_inc(s_dn, 2)
            pool.memset(credit[:, 2:3], 0.0).then_inc(s_yc, NB + 1)

            def body(e, q, p):
                pool.wait_ge(s_w[p], 64 * (q + 1))
                pool.sem_inc(s_alone, 1)
                pool.tensor_copy(w1h[p][:], w1[p][:]).then_inc(s_wh, 1)
                pool.wait_ge(s_wh, e + 1)
                pool.tensor_tensor(w1l[p][:], w1[p][:], w1h[p][:].bitcast(F32), ALU.subtract).then_inc(s_ws, 1)

            def add(e, n):
                m = NB * e + n
                a = slice(CB * n, CB * n + CB)
                pool.wait_ge(s_yc, m + 2 + NB)
                pool.wait_ge(s_a, 2 + m)
                pool.tensor_tensor(K.acc[:, a, :], K.acc[:, a, :], y[n % 2][:], ALU.add).then_inc(s_a, 1)

            def both(e, q, p):
                body(e, q, p)
                for n in range(NB):
                    add(e, n)

            pairs(pool, both)

        @block.scalar
        def _(act):
            def body(e, q, p):
                act.wait_ge(s_w[p], 64 * (q + 1))
                for n in range(NB):
                    m = NB * e + n
                    act.wait_ge(s_dn, m + 1)
                    for f in range(FC):
                        act.wait_ge(s_up, FC * m + f + 1)
                        act.activation(hid[n % 2][:, f, :], K.st[f][:, BANK * (n % 2):BANK * (n % 2) + BANK],
                                       ACT.Gelu, bias=b1[p][:, f:f + 1]).then_inc(s_g, 1)

            pairs(act, body)

        @block.vector
        def _(dve):
            def body(e, q, p):
                dve.wait_ge(s_w[p], 64 * (q + 1))
                for n in range(NB):
                    m = NB * e + n
                    dve.wait_ge(s_dn, m + 3)
                    dve.wait_ge(s_a, m + 1)
                    dve.tensor_tensor(y[n % 2][:], K.work[n % 2][:].rearrange("p (c d) -> p c d", d=D),
                                      b2[p][:].unsqueeze(1).broadcast_to([P, CB, D]), ALU.add).then_inc(s_y, 1)
                    dve.wait_ge(s_y, m + 1)
                    dve.tensor_tensor(y[n % 2][:], y[n % 2][:],
                                      K.comb[:, e, CB * n:CB * n + CB].unsqueeze(2).broadcast_to([P, CB, D]), ALU.mult).then_inc(s_yc, 1)

            pairs(dve, body)

        @block.tensor
        def _(pe):
            def up(e, p, n):
                m = NB * e + n
                for f in range(FC):
                    pe.wait_ge(s_g, FC * m + f + 1)
                    t = K.st[f][:, BANK * (n % 2):BANK * (n % 2) + BANK]
                    a, r = slice(P * f, P * f + P), slice(BANK * n, BANK * n + BANK)
                    pe.matmul(t, w1h[p][:, a], K.xh[:, r], start=True, stop=False)
                    pe.matmul(t, w1h[p][:, a], K.xl[:, r], start=False, stop=False)
                    pe.matmul(t, w1l[p][:, a], K.xh[:, r], start=False, stop=True).then_inc(s_up, 1)

            def down(e, p, n, m):
                pe.wait_ge(s_g, FC * m + FC + 4)
                for c in range(CB):
                    for f in range(FC):
                        last = pe.matmul(K.work[n % 2][:, P * c:P * c + P], hid[n % 2][:, f, P * c:P * c + P],
                                         w2[p][:, f, :], start=(f == 0), stop=(f == FC - 1))
                last.then_inc(s_dn, 1)

            def body(e, q, p):
                pe.wait_ge(s_ws, e + 1)
                for n in range(NB):
                    up(e, p, n)
                    if n:
                        pe.wait_ge(s_yc, NB * e + n - 1 + NB)
                        down(e, p, n - 1, NB * e + n - 1)
                pe.wait_ge(s_yc, NB * e + NB - 1 + NB)
                down(e, p, NB - 1, NB * e + NB - 1)

            pairs(pe, body)


def row_units(proj, smax, st, den, out):
    u = []
    for k in range(1, CH + 1):
        if smax:
            u += [("max", k - 1, h) for h in range(key_tiles(True, k - 1))]
        if proj:
            u += [("k", k // 2)] if k < CH and k % 2 == 0 else [("q", k // 2)] if k < CH else \
                 [("v", 0), ("v", 1)]
            if k == 7:
                u += [("k", 0)]
        if k == 1 and den:
            u += [("den", 0)]
        if k == 3 and out:
            u += [("out", 0)]
        if k in (5, 8) and smax:
            u += [("t", k // 8)]
    return u


def rows_phase(nc, K, src, tag, scale):
    ph = Phase(nc, tag)
    XT, acc = K.XT, K.acc_slots
    wq = ph.sb("wq", [D, H, P])
    wk = ph.sb("wk", [D, H, P])
    wv = ph.sb("wv", [D, H * HS])
    pw = ph.sb("pw", [P, H // 2, D])
    xt = ph.sb("xt", [D, P])
    qa = [ph.sb(f"qa{i}", [P, 2 * S], F32R) for i in range(2)]
    qb = [ph.sb(f"qb{i}", [P, 2 * S], F32R) for i in range(2)]
    ka = [ph.sb(f"ka{i}", [P, 2 * S], F32R) for i in range(2)]
    kb = [ph.sb(f"kb{i}", [P, 2 * S], F32R) for i in range(2)]
    vs = ph.sb("vs", [P, H * HS])
    v = [ph.sb(f"v{i}", [P, 2 * CH, HS]) for i in range(2)]
    ps = [ph.sb(f"ps{i}", [P, S]) for i in range(2)]
    pr = [None] + [ph.sb(f"p{c}", [P, S - P * c]) for c in range(1, CH)]
    ones = ph.sb("ones", [P, HS])
    mx = ph.sb("mx", [P, 2, 2])
    mz = ph.sb("mz", [P, CH, P])
    rd = ph.sb("rd", [P, BANK])
    on = [ph.sb(f"on{i}", [P, BANK]) for i in range(2)]
    credit = ph.sb("credit", [P, 4])
    vd = [nc.dram_tensor(f"{tag}_values{i}", [P * H, HS], F32).ap() for i in range(2)]

    banks = Banks(ph, K.work)
    s_alone = ph.sem("alone")
    s_set = ph.sem("rows_set")
    s_load, s_zero, s_xt, s_rnd, s_kb, s_vs, s_vd, s_v = (ph.sem(x) for x in (
        "loaded", "zeroed", "tokens_staged", "rounded", "kb_made", "values", "values_in_dram", "values_in_rows"))
    s_mz, s_st, s_p, s_pv, s_add, s_on = (ph.sem(x) for x in (
        "maxima", "scores_t", "exp_done", "pv_done", "added", "normalized"))

    head = [row_units(True, False, False, False, False), row_units(False, True, False, False, False)]
    quad = [row_units(r % 2 == 0, True, True, True, r % 2 == 0) for r in range(4)]
    last = [row_units(True, True, True, True, True), quad[1], row_units(False, True, True, True, True),
            row_units(False, False, True, True, False), row_units(False, False, False, True, True)]

    def places(lists):
        found, at = [], 0
        for u in lists:
            found.append(({x: at + n for n, x in enumerate(u)}, at))
            at += len(u)
        return found, at

    (head_at, n_head), (quad_at, n_quad), (last_at, _) = places(head), places(quad), places(last)
    NQUAD = NP // 4

    def turns(eng, body):
        body(-2, 2, -1, *head_at[0], 0, True, False, False)
        body(-1, 3, -1, *head_at[1], 0, False, True, False)
        with eng.Fori(0, NQUAD - 1) as q:
            for r in range(4):
                body(4 * q + r, r, 2 * q + r // 2, *quad_at[r], q * (n_quad // 2) + n_head // 2,
                     r % 2 == 0, True, True)
        n, half = NP - 4, (NQUAD - 1) * (n_quad // 2) + n_head // 2
        for r in range(5):
            body(n + r, r % 4, (n + r) // 2, *last_at[r], half, r == 0, r < 3, r < 4)

    with ph.block() as block:

        @block.sync
        def _(sp):
            for dst, name in ((wk, "wk"), (wq, "wq"), (wv, "wv"), (pw, "pw")):
                sp.dma_start(dst[:], src[name]).then_inc(s_load, 16)

            def body(n, r, pair, at, first, half, proj, smax, st):
                if proj:
                    i = 1 - r // 2
                    sp.wait_ge(s_vs, 2 * (pair + 2))
                    sp.dma_start(vd[i].rearrange("(x i) k -> x (i k)", i=H), vs[:]).then_inc(s_vd, 16)
                    sp.wait_ge(s_vd, 16 * (pair + 2))
                    sp.dma_start(v[i][:], vd[i].rearrange("(c p) k -> p c k", p=P)).then_inc(s_v, 16)

            turns(sp, body)

        @block.gpsimd
        def _(pool):
            pool.memset(mz[:], 0.0).then_inc(s_zero, 1)
            pool.memset(ones[:], 1.0).then_inc(s_zero, 1)
            pool.memset(ps[1][:], 1.0).then_inc(s_zero, 1)
            pool.memset(on[0][:], 0.0).then_inc(s_zero, 1)
            pool.memset(credit[:, 0:1], 0.0).then_inc(s_p, 2)
            pool.memset(credit[:, 3:4], 0.0).then_inc(s_on, 1)
            pool.memset(credit[:, 1:2], 0.0).then_inc(s_pv, CH)
            pool.memset(credit[:, 2:3], 0.0).then_inc(s_add, CH - 1)

            def body(n, r, pair, at, first, half, proj, smax, st):
                i = 1 - r // 2
                if proj:
                    banks.all_read(pool, half, first)
                    pool.sem_inc(s_alone, 1)
                    pool.tensor_copy(xt[:], XT[:, bass.ds((pair + 1) * P, P)]).then_inc(s_xt, 1)
                for c in range(1, CH):
                    if st:
                        if c == 1:
                            pool.wait_ge(s_pv, CH * n + 1 + CH)
                        pool.wait_ge(s_p, CH * n + c + 1 + 2)
                        pool.wait_ge(s_add, (CH - 1) * n + c - 1 + CH - 1)
                        pool.tensor_tensor(ps[r % 2][:, P * c:], ps[r % 2][:, P * c:], pr[c][:],
                                           ALU.add).then_inc(s_add, 1)
                if proj:
                    for h in range(4):
                        banks.read(pool, half, at["k", h])
                    pool.sem_inc(s_alone, 1)
                    pool.tensor_copy(kb[i][0:HS, :], ka[i][0:HS, :].bitcast(F32)).then_inc(s_kb, 1)

            turns(pool, body)

        @block.scalar
        def _(act):
            act.wait_ge(s_set, 7)

            def body(n, r, pair, at, first, half, proj, smax, st):
                i = 1 - r // 2
                for k in range(CH + 1):
                    if st and k < CH:
                        if k == 0:
                            act.wait_ge(s_on, n + 1)
                        else:
                            act.wait_ge(s_add, (CH - 1) * n + k)
                            act.wait_ge(s_pv, CH * n + k + 1)
                        act.wait_ge(s_st, CH * n + k + 1)
                        dst = pr[k][:] if k else ps[r % 2][:]
                        act.activation(dst, K.st[k % 2][:, P * k:], ACT.Exp, scale=scale).then_inc(s_p, 1)
                    if proj and k >= 1:
                        for x, u in enumerate(u for u in at if u[0] in "kq" and step_of(u) == k):
                            w = banks.filled(act, half, at[u])
                            dst = (ka if u[0] == "k" else qa)[i][:].rearrange("p (t i) -> p i t", i=H)
                            act.activation(dst[:, 4 * u[1]:4 * u[1] + 4, :],
                                           w[:].rearrange("p (i t) -> p i t", i=4), ACT.Copy).then_inc(s_rnd, 1)
                        if k == CH:
                            if not (isinstance(n, int) and n < 0):
                                act.wait_ge(s_vd, 16 * (pair + 1))
                            for h in range(2):
                                w = banks.filled(act, half, at["v", h])
                                act.activation(vs[:, BANK * h:BANK * h + BANK], w[:], ACT.Copy)\
                                   .then_inc(banks.free[at["v", h] % 2], 1)
                                banks.read(act, half, at["v", h])
                                act.nop().then_inc(s_vs, 1)
                    if k in (5, 8) and smax:
                        u = at["t", k // 8]
                        w = banks.filled(act, half, u)
                        m, j = (r + 1) % 4 // 2, (r + 1) % 2
                        a = S * j + BANK * (k // 8)
                        act.activation(qb[m][HS:HS + 1, a:a + BANK], w[HS:HS + 1, :], ACT.Copy)\
                           .then_inc(banks.free[u % 2], 1)

            turns(act, body)

        @block.vector
        def _(dve):

            def body(n, r, pair, at, first, half, proj, smax, st):
                i = 1 - r // 2
                for k in range(1, CH + 1):
                    c = k - 1
                    if smax:
                        tiles = key_tiles(True, c)
                        for h in range(tiles):
                            u = at["max", c, h]
                            w = banks.filled(dve, half, u)
                            cols = min(BANK, P * (c + 1) - BANK * h)
                            dst = mx[:, c % 2, h:h + 1] if tiles == 2 else mz[:, c, HS:HS + 1]
                            dve.reduce_max(dst, w[:, 0:cols], AX.X, negate=True).then_inc(banks.free[u % 2], 1)
                        if tiles == 2:
                            banks.read(dve, half, u - 1)
                            banks.read(dve, half, u)
                            dve.tensor_tensor(mz[:, c, HS:HS + 1], mx[:, c % 2, 0:1], mx[:, c % 2, 1:2],
                                              ALU.min).then_inc(s_mz, 1)
                    if proj:
                        for x in (x for x in at if x[0] in "kq" and step_of(x) == k):
                            w = banks.filled(dve, half, at[x])
                            done = [y for y in at if y[0] in "kq"].index(x)
                            dve.wait_ge(s_rnd, 8 * (pair + 1) + done + 1)
                            hi, lo, rows = (ka, ka, slice(HS, P)) if x[0] == "k" else (qa, qb, slice(0, HS))
                            hi, lo = (b[i][rows, :].rearrange("p (t i) -> p i t", i=H)[:, 4 * x[1]:4 * x[1] + 4, :]
                                      for b in (hi, lo))
                            dve.tensor_tensor(lo, w[rows, :].rearrange("p (i t) -> p i t", i=4),
                                              hi.bitcast(F32), ALU.subtract).then_inc(banks.free[at[x] % 2], 1)
                    if k == 1 and ("den", 0) in at:
                        u = at["den", 0]
                        w = banks.filled(dve, half, u)
                        dve.wait_ge(s_on, n + 1)
                        dve.reciprocal(rd[:], w[:]).then_inc(banks.free[u % 2], 1)
                        banks.read(dve, half, u)
                        o = (r + 1) % 2
                        dve.tensor_tensor(on[o][:], K.o_ps[:, BANK * o:BANK * o + BANK], rd[:],
                                          ALU.mult).then_inc(s_on, 1)
                    if k == 3 and ("out", 0) in at:
                        u = at["out", 0]
                        w = banks.filled(dve, half, u)
                        dve.tensor_copy(acc[:, pair, :], w[:, 0:D]).then_inc(banks.free[u % 2], 1)

            for i in range(2):
                dve.memset(kb[i][HS:P, :].bitcast(F32), 0.0).then_inc(s_set, 1)
                dve.memset(qb[i][HS:P, :].bitcast(F32), 0.0).then_inc(s_set, 1)
            dve.memset(K.o_ps[:, BANK:], 0.0).then_inc(s_set, 1)
            dve.wait_ge(s_set, 5)
            dve.memset(kb[0][HS:HS + 1, :].bitcast(F32), 1.0).then_inc(s_set, 1)
            dve.memset(kb[1][HS:HS + 1, :].bitcast(F32), 1.0).then_inc(s_set, 1)
            dve.wait_ge(s_zero, 4)
            turns(dve, body)

        @block.tensor
        def _(pe):
            pe.wait_ge(s_load, 64)
            pe.wait_ge(s_set, 7)
            pe.wait_ge(s_zero, 4)

            def body(n, r, pair, at, first, half, proj, smax, st):
                cur, j = r // 2, r % 2
                nxt, nj = (r + 1) % 4 // 2, (r + 1) % 2
                banks.all_read(pe, half, first)
                if st:
                    pe.wait_ge(s_kb, pair + 1)
                    if j == 0:
                        pe.wait_ge(s_v, 16 * (pair + 1))
                for k in range(CH + 1):
                    if smax and k >= 1:
                        c = k - 1
                        for h in range(key_tiles(True, c)):
                            u = at["max", c, h]
                            w = banks.claim(pe, half, u)
                            cols = min(BANK, P * (c + 1) - BANK * h)
                            diag = BANK * h + cols == P * (c + 1)
                            a = S * nj
                            last = pe.matmul(w[:, 0:cols], qa[nxt][:, a + P * c:a + P * c + P],
                                             ka[nxt][:, a + BANK * h:a + BANK * h + cols],
                                             start=True, stop=not diag)
                            if diag:
                                last = pe.matmul(w[:, cols - P:cols], K.identb[:], K.maskq[:],
                                                 start=False, stop=True)
                            last.then_inc(banks.full[u % 2], 1)
                    if st and k < CH:
                        pe.wait_ge(s_p, CH * n + k + 1)
                        s0 = S * j
                        for a, b in pieces(P * k):
                            t = K.st[k % 2][:, a:b]
                            diag = a == P * k
                            pe.matmul(t, ka[cur][:, s0 + P * k:s0 + P * k + P], qa[cur][:, s0 + a:s0 + b],
                                      start=True, stop=False)
                            last = pe.matmul(t, kb[cur][:, s0 + P * k:s0 + P * k + P], qb[cur][:, s0 + a:s0 + b],
                                             start=False, stop=not diag)
                            if diag:
                                last = pe.matmul(K.st[k % 2][:, a:a + P], K.identb[:], K.maskk[:],
                                                 start=False, stop=True)
                        last.then_inc(s_st, 1)
                    if st and k >= 1:
                        c = k - 1
                        pe.wait_ge(s_p, CH * n + c + 1 + 2)
                        if c == 0:
                            pe.wait_ge(s_on, n + 1)
                        p = pr[c] if c else ps[j]
                        for odd in range(2):
                            last = pe.matmul(K.o_ps[HS * odd:HS * odd + HS, BANK * j + P // 2 * c:BANK * (j + 1)],
                                             v[cur][:, CH * j + c, :], p[:, odd::2],
                                             start=(c == 0), stop=(c == CH - 1))
                        last.then_inc(s_pv, 1)
                    if proj and k >= 1:
                        if k == 1:
                            pe.wait_ge(s_xt, pair + 2)
                        for x in (x for x in at if x[0] in "kq" and step_of(x) == k):
                            w = banks.claim(pe, half, at[x])
                            for e in range(4):
                                last = pe.matmul(w[:, P * e:P * e + P], (wk if x[0] == "k" else wq)[:, 4 * x[1] + e, :],
                                                 xt[:], start=True, stop=True)
                            last.then_inc(banks.full[at[x] % 2], 1)
                        if k == CH:
                            for h in range(2):
                                w = banks.claim(pe, half, at["v", h])
                                pe.matmul(w[:], xt[:], wv[:, BANK * h:BANK * h + BANK],
                                          start=True, stop=True).then_inc(banks.full[at["v", h] % 2], 1)
                    if k == 1 and ("den", 0) in at:
                        u = at["den", 0]
                        w = banks.claim(pe, half, u)
                        pe.wait_ge(s_add, (CH - 1) * n + CH - 1)
                        for odd in range(2):
                            last = pe.matmul(w[HS * odd:HS * odd + HS, :], ones[:], ps[1 - j][:, odd::2],
                                             start=True, stop=True)
                        last.then_inc(banks.full[u % 2], 1)
                    if k == 3 and ("out", 0) in at:
                        u = at["out", 0]
                        w = banks.claim(pe, half, u)
                        pe.wait_ge(s_on, n + 2)
                        for e in range(H // 2):
                            for m in range(2):
                                last = pe.matmul(w[HS * m:HS * m + HS, 0:D], on[m][:, e::H // 2], pw[:, e, :],
                                                 start=(e == 0), stop=(e == H // 2 - 1))
                        last.then_inc(banks.full[u % 2], 1)
                    if k in (5, 8) and smax:
                        u = at["t", k // 8]
                        w = banks.claim(pe, half, u)
                        if k == 8:
                            pe.wait_ge(s_mz, CB * (n + 2))
                        for c in range(CB):
                            last = pe.transpose(w[:, P * c:P * c + P], mz[:, CB * (k // 8) + c, :], K.ident[:])
                        last.then_inc(banks.full[u % 2], 1)

            turns(pe, body)


def step_of(unit):
    kind, h = unit
    return {"q": 2 * h + 1, "k": 2 * h if h else 7}[kind]


def build(nc, t):
    with ExitStack() as stack:
        K = Kept(nc, stack)
        load_phase(nc, K, {n: t[n] for n in ("x", "ident", "maskq", "maskk")})
        with ExitStack() as layer0:
            K.CT = layer0.enter_context(nc.sbuf_tensor("CT", [P, G * B + 1, S], F32))
            groups_phase(nc, K, {"gw": t["gw0"], "negc": t["negc"], "sel": t["sel"]}, "attn0", True, 8 ** -0.5)
            norm_phase(nc, K, {"wo": t["wo0"], "bias": t["bo0"]}, "norm0", "context")
            groups_phase(nc, K, {"gw": t["gw1"], "negc": t["negc"], "sel": t["sel"]}, "attn1", False, 0.5)
            route_phase(nc, K, {"wo": t["wo1"], "ob": t["ob1"], "rw": t["rw0"], "rb": t["rb0"],
                                      "rank": t["rank0"]}, "route0", E0, True, 0.0, 1e-8)
        experts_phase(nc, K, {n: t[n + "_0"] for n in ("w1", "b1", "w2", "b2")}, "moe0", E0)
        norm_phase(nc, K, {}, "norm1", "moe")
        rows_phase(nc, K, {"wq": t["wq2"], "wk": t["wk2"], "wv": t["wv2"], "pw": t["pw2"]}, "attn2", HS ** -0.5)
        norm_phase(nc, K, {"bias": t["pb2"]}, "norm2", "rows")
        route_phase(nc, K, {"rw": t["rw1"], "rb": t["rb1"], "rank": t["rank1"]}, "route1", E1, False,
                    1e-10, 0.0)
        experts_phase(nc, K, {n: t[n + "_1"] for n in ("w1", "b1", "w2", "b2")}, "moe1", E1)
        norm_phase(nc, K, {}, "norm3", "clip", out=t["out"])


def kernel(**inputs):
    import numpy as np
    import concourse.bacc as bacc
    from concourse.bass_utils import run_bass_kernel_spmd

    a = {n: np.asarray(v) for n, v in inputs.items()}
    f32 = np.float32

    def packed(wk, bk, wq, bq, wv, bv, hd, stride):
        gw = np.zeros((P, G, GW), f32)
        for h in range(H):
            g, at = divmod(h, HG)
            for part in range(3):
                c = 32 * at + ONE * part
                gw[:, g, c:c + hd] = wk[:, hd * h:hd * h + hd]
                gw[:, g, P + c:P + c + hd] = wq[:, stride * h:stride * h + hd]
                gw[c:c + hd, g, 4 * P] = bk[hd * h:hd * h + hd]
                gw[c:c + hd, g, 4 * P + 1] = bq[stride * h:stride * h + hd]
            c = 32 * at
            gw[:, g, 2 * P + c:2 * P + c + hd] = wv[:, hd * h:hd * h + hd]
            gw[:, g, 3 * P + c:3 * P + c + hd] = bv[hd * h:hd * h + hd]
            gw[:, g, 3 * P + c + ONE] = 1.0
            gw[c + MROW, g, 4 * P] = 1.0
        return gw

    def rows_of(w, hd):
        wo = np.zeros((P, G, D), f32)
        for h in range(H):
            g, at = divmod(h, HG)
            wo[32 * at:32 * at + hd, g] = w[hd * h:hd * h + hd]
        return wo

    zero = np.zeros(D, f32)
    rows = np.arange(P)
    negc = np.zeros((P, 2), f32)
    negc[rows % 32 // ONE == 1, 0] = -1.0
    negc[rows % 32 // ONE == 2, 1] = -1.0
    later = rows[:, None] < rows[None, :]
    wq, wk, wv = (a[f"L1_attn_W{x}"].transpose(1, 0, 2) for x in "qkv")
    arrays = {
        "x": a["L0_attn_x"],
        "ident": np.eye(P, dtype=f32),
        "maskq": np.where(later, f32(-1e30), f32(0.0)),
        "maskk": np.where(later.T, f32(-1e30), f32(0.0)),
        "negc": negc,
        "sel": (rows[:, None] == rows[None, :] // 32 * 32 + ONE).astype(f32),
        "gw0": packed(a["L0_attn_Wk"], zero, a["L0_attn_Wq"], zero, a["L0_attn_Wv"], zero, D // H, D // H),
        "wo0": rows_of(a["L0_attn_Wo"], D // H),
        "bo0": a["L0_attn_bo"],
        "gw1": packed(a["L0_ffn_k_w"], a["L0_ffn_k_b"], a["L0_ffn_q_w"], a["L0_ffn_q_b"], a["L0_ffn_v_w"],
                      a["L0_ffn_v_b"], D // H // 2, D // H),
        "wo1": rows_of(a["L0_ffn_o_w"], D // H // 2),
        "ob1": a["L0_ffn_o_b"].reshape(D, 1),
        "rw0": a["L0_ffn_router_w"],
        "rb0": a["L0_ffn_router_b"],
        "rank0": np.tile(np.arange(E0, 0, -1, dtype=f32), (P, 1)),
        "wq2": np.concatenate([wq, wq], axis=2),
        "wk2": np.concatenate([wk, wk], axis=2),
        "wv2": wv.reshape(D, H * HS),
        "pw2": a["L1_attn_proj_w"].reshape(D, H // 2, 2 * HS).transpose(2, 1, 0),
        "pb2": a["L1_attn_proj_b"],
        "rw1": a["L1_ffn_gate_w"].T,
        "rb1": np.zeros(E1, f32),
        "rank1": np.tile(np.arange(E1, 0, -1, dtype=f32), (P, 1)),
    }
    for n, layer in enumerate(("L0_ffn", "L1_ffn")):
        arrays[f"w1_{n}"] = a[f"{layer}_w1"]
        arrays[f"b1_{n}"] = a[f"{layer}_b1"].reshape(-1, FC, P).transpose(0, 2, 1)
        arrays[f"w2_{n}"] = a[f"{layer}_w2"]
        arrays[f"b2_{n}"] = a[f"{layer}_b2"]

    nc = bacc.Bacc("TRN2", target_bir_lowering=False, num_devices=1)
    feeds, tensors = {}, {}
    for name, array in arrays.items():
        array = np.ascontiguousarray(array)
        feeds[f"in_{name}"] = array
        tensors[name] = nc.dram_tensor(f"in_{name}", array.shape, mybir.dt.from_np(array.dtype),
                                       kind="ExternalInput").ap()
    tensors["out"] = nc.dram_tensor("out", (B, S, D), F32, kind="ExternalOutput").ap()
    build(nc, tensors)
    result = run_bass_kernel_spmd(nc, [feeds], core_ids=[0])
    return result.results[0]["out"]
```

```python
from contextlib import ExitStack, contextmanager

import concourse.bass as bass
from concourse import mybir

F32 = mybir.dt.float32
F32R = mybir.dt.float32r
BF16 = mybir.dt.bfloat16
ALU = mybir.AluOpType
ACT = mybir.ActivationFunctionType
AX = mybir.AxisListType

P = 128
D = 128
B, S = 2, 1024
NT = B * S
NC = NT // P
H = 16
BANK = 512
NB = NT // BANK
CB = BANK // P
CH = S // P
G = 4
HG = H // G
ONE = 8
MROW = 24
GW = 4 * P + 2
E0, E1 = 8, 14
F = 256
FC = F // P
HS = 64
XP = S // H
NP = NT // XP
EPS = 1e-5


class Phase:

    def __init__(self, nc, tag):
        self.nc, self.tag, self.buffers, self.semaphores = nc, tag, ExitStack(), []

    def sb(self, name, shape, dt=F32):
        return self.buffers.enter_context(self.nc.sbuf_tensor(f"{self.tag}_{name}", shape, dt))

    def sem(self, name):
        self.semaphores.append(self.nc.alloc_semaphore(name=f"{self.tag}_{name}"))
        return self.semaphores[-1]

    @contextmanager
    def block(self):
        with self.buffers:
            with self.nc.Block() as block:
                yield block
            self.nc.clear_and_free_semaphores(self.semaphores)
            self.nc.all_engine_barrier()


class Banks:

    def __init__(self, ph, tensors):
        self.full = [ph.sem(f"bank{i}_full") for i in range(len(tensors))]
        self.free = [ph.sem(f"bank{i}_free") for i in range(len(tensors))]
        self.tensors = tensors

    def claim(self, pe, base, place):
        b, i = place
        if not (isinstance(base[b], int) and base[b] + i == 0):
            pe.wait_ge(self.free[b], base[b] + i)
        return self.tensors[b]

    def filled(self, eng, base, place):
        b, i = place
        eng.wait_ge(self.full[b], base[b] + i + 1)
        return self.tensors[b]

    def read(self, eng, base, place):
        b, i = place
        eng.wait_ge(self.free[b], base[b] + i + 1)

    def all_read(self, eng, base, first, but_last=False):
        for b, i in enumerate(first):
            i -= but_last and b == len(first) - 1
            if not (isinstance(base[b], int) and base[b] + i == 0):
                eng.wait_ge(self.free[b], base[b] + i)


class Places:

    def __init__(self, turns):
        self.at, self.first, self.total = [], [], [0] * WB
        for units in turns:
            self.first.append(list(self.total))
            self.at.append({})
            for n, u in enumerate(units):
                b = WB - 1 if u == ("t", 1) else n % WB
                self.at[-1][u] = (b, self.total[b])
                self.total[b] += 1

    def turn(self, r):
        return self.at[r], self.first[r]


class Scores:

    def __init__(self, keys):
        self.at = {key: n for n, key in enumerate(keys)}
        self.n = len(keys)

    def bank(self, key):
        return self.at[key] % SB

    def through(self, t, key):
        return self.n * t + self.at[key] + 1 + SB

    def before(self, t, key):
        n = self.at[key]
        m = n - SB if n >= SB else max(m for m in range(self.n) if m % SB == n % SB) - self.n
        return self.n * t + m + 1 + SB


WB, SB = 3, 3
NONE = (0,) * WB


def alternate(n):
    return n % 2, n // 2


def group_units(causal, proj, smax, den):
    u = []
    for k in range(1, CH + 1):
        if smax:
            for j in range(HG):
                u += [("max", k - 1, j, h) for h in range(key_tiles(causal, k - 1))]
        if k == 2 and proj:
            u += [("k", 0), ("k", 1)]
        if k == 3 and proj:
            u += [("q", 0), ("q", 1)]
        if k == 4 and den:
            u += [("den", 0), ("den", 1)]
        if k == 8 and smax:
            u += [("v", 0), ("v", 1)]
        if k in (5, 8) and smax:
            u += [("t", k // 8)]
    return u


def key_tiles(causal, c):
    return 1 if causal and c < CB else 2


def pieces(q0):
    return [(max(q0, a), a + BANK) for a in range(0, S, BANK) if q0 < a + BANK]


def load_phase(nc, K, gb, src):
    ph = Phase(nc, "load")
    mf = [ph.sb(f"maskf{i}", [P, P]) for i in range(2)]
    s_in, s_x, s_b = ph.sem("in"), ph.sem("x"), ph.sem("cast")
    banks = Banks(ph, K.work[:2])
    X, XT = K.X, K.XT
    xv = src["x"].rearrange("b (c p) d -> p (b c) d", p=P)
    s_w = ph.sem("weights")
    with ph.block() as block:

        @block.gpsimd
        def _(pool):
            pool.memset(gb.kpad[0][:].bitcast(F32), 0.0)

        @block.sync
        def _(sp):
            sp.dma_start(K.ident[:], src["ident"]).then_inc(s_in, 16)
            for n in range(NB):
                sp.dma_start(X[:, CB * n:CB * n + CB, :], xv[:, CB * n:CB * n + CB, :]).then_inc(s_x, 16)
            sp.dma_start(gb.gw[:], src["gw"]).then_inc(s_w, 16)
            sp.dma_start(gb.negc[:], src["negc"]).then_inc(s_w, 16)
            sp.dma_start(gb.sel[:], src["sel"]).then_inc(s_w, 16)
            sp.wait_ge(s_w, 48)

        @block.scalar
        def _(act):
            act.dma_start(mf[0][:], src["maskq"]).then_inc(s_b, 16)
            act.dma_start(mf[1][:], src["maskk"]).then_inc(s_b, 16)
            for n in range(NB):
                t = banks.filled(act, NONE, alternate(n))
                act.activation(XT[:, BANK * n:BANK * n + BANK], t[:], ACT.Copy).then_inc(banks.free[n % 2], 1)

        @block.vector
        def _(dve):
            dve.memset(gb.kpad[1][:].bitcast(F32), 0.0)
            dve.memset(gb.mz[:], 0.0)
            dve.memset(gb.rr[:], 0.0)
            dve.memset(gb.oe[:], 1.0)
            dve.wait_ge(s_b, 32)
            dve.tensor_copy(K.maskq[:], mf[0][:])
            dve.tensor_copy(K.maskk[:], mf[1][:])
            dve.wait_ge(s_in, 16)
            dve.tensor_copy(K.identb[:], K.ident[:])

        @block.tensor
        def _(pe):
            pe.wait_ge(s_in, 16)
            for n in range(NB):
                pe.wait_ge(s_x, 16 * NB)
                t = banks.claim(pe, NONE, alternate(n))
                for c in range(CB):
                    last = pe.transpose(t[:, P * c:P * c + P], X[:, CB * n + c, :], K.ident[:])
                last.then_inc(banks.full[n % 2], 1)


def groups_phase(nc, K, gb, tag, causal, scale):
    ph = Phase(nc, tag)
    ident, XT, CT = K.ident, K.XT, K.CT
    gw, negc, sel, kpad, mz, oe, rr = gb.gw, gb.negc, gb.sel, gb.kpad, gb.mz, gb.oe, gb.rr
    wkq = ph.sb("wkq", [P, 2 * P + 2])
    wv = ph.sb("wv", [P, 2 * P])
    raw = ph.sb("raw", [P, 2, BANK])
    hi = ph.sb("hi", [P, 2, BANK], F32R)
    kc = ph.sb("kc", [P, S], F32R)
    qp = [ph.sb(f"qp{i}", [P, S], F32R) for i in range(2)]
    qa = [ph.sb(f"qa{i}", [P, S], F32R) for i in range(2)]
    v = [ph.sb(f"v{i}", [P, CH, P]) for i in range(2)]
    pr = [[ph.sb(f"p{i}{j}", [P, S]) for j in range(HG)] for i in range(2)]
    mx = ph.sb("mx", [P, 2, HG, 2])
    dn = ph.sb("dn", [P, 32])
    rd = ph.sb("rd", [P, 32])
    credit = ph.sb("credit", [P, 4])

    banks = Banks(ph, K.work)
    s_alone = ph.sem("alone")
    s_wkq = ph.sem("wkq_staged")
    s_wv = ph.sem("wv_staged")
    s_hi = ph.sem("hi_made")
    s_kc = ph.sem("kc_made")
    s_dn = ph.sem("denominators_spread")
    s_rd = ph.sem("reciprocals")
    s_rr = ph.sem("reciprocals_back")
    s_qp = ph.sem("qp_made")
    s_kpad = ph.sem("kpad_staged")
    s_mz = ph.sem("maxima")
    s_st = ph.sem("scores_t")
    s_p = ph.sem("exp_done")
    s_pv = ph.sem("pv_done")
    s_oe = ph.sem("outputs_evacuated")

    head = Places([group_units(causal, True, False, False), group_units(causal, True, True, False)])
    pair = Places([group_units(causal, True, True, True)] * B)
    tail = Places([group_units(causal, False, True, True), group_units(causal, False, False, True),
                   group_units(causal, False, False, True)])
    NQ = sum(key_tiles(causal, c) == 2 for c in range(CH))

    def q0_of(c):
        return P * c if causal else 0

    scores = Scores([(c, j, i) for c in range(CH) for j in range(HG) for i in range(len(pieces(q0_of(c))))])

    def last_of(c):
        return c, HG - 1, len(pieces(q0_of(c))) - 1

    def turns(eng, body):
        body(-2, -1, 0, *head.turn(0), NONE, False, False, True)
        body(-1, -1, 1, *head.turn(1), NONE, False, True, True)
        with eng.Fori(0, G - 1) as g:
            base = [n + m * g for n, m in zip(head.total, pair.total)]
            for p in range(B):
                body(2 * g + p, g, p, *pair.turn(p), base, True, True, True)
        t, base = B * (G - 1), [n + m * (G - 1) for n, m in zip(head.total, pair.total)]
        body(t, G - 1, 0, *tail.turn(0), base, True, True, False)
        body(t + 1, G - 1, 1, *tail.turn(1), base, True, False, False)
        body(t + 2, G, 0, *tail.turn(2), base, False, False, False)

    with ph.block() as block:

        @block.sync
        def _(sp):
            def body(t, g, p, units, first, base, st, smax, proj):
                if smax:
                    sp.wait_ge(s_kc, 2 * (t + 2))
                    sp.sem_inc(s_alone, 1)
                    if st:
                        sp.wait_ge(s_p, scores.n * t + SB)
                        sp.sem_inc(s_alone, 1)
                    for j in range(HG):
                        r = slice(32 * j, 32 * j + 32)
                        sp.dma_start(kpad[1 - p][r, j, :].bitcast(F32), kc[r, :].bitcast(F32))\
                          .then_inc(s_kpad, 16)
                if ("den", 0) in units:
                    sp.wait_ge(s_oe, t + 1)
                    sp.sem_inc(s_alone, 1)
                    sp.dma_start(dn[:], oe[ONE::32, :].rearrange("j (a f) -> j a f", f=32)).then_inc(s_dn, 16)
                    sp.wait_ge(s_rd, t + 1)
                    sp.sem_inc(s_alone, 1)
                    sp.dma_start(rr[ONE::32, :].rearrange("j (a f) -> j a f", f=32), rd[:]).then_inc(s_rr, 16)

            turns(sp, body)

        @block.gpsimd
        def _(pool):
            pool.memset(credit[:, 0:1], 0.0).then_inc(s_p, SB)
            pool.memset(credit[:, 2:3], 0.0).then_inc(s_oe, 1)
            pool.memset(credit[:, 1:2], 0.0).then_inc(s_pv, 2)

            def body(t, g, p, units, first, base, st, smax, proj):
                if st and (proj or smax):
                    banks.all_read(pool, base, first)
                pool.sem_inc(s_alone, 1)
                if proj and p == 0:
                    pool.tensor_copy(wkq[:, 0:2 * P], gw[:, g + 1, 0:2 * P])
                    pool.tensor_copy(wkq[:, 2 * P:], gw[:, g + 1, 4 * P:]).then_inc(s_wkq, 1)
                if smax and p == 1:
                    pool.tensor_copy(wv[:], gw[:, g + 1, 2 * P:4 * P]).then_inc(s_wv, 1)
                if proj:
                    for w, (dst, s_dst, what) in enumerate(((kc, s_kc, 0), (kc, s_kc, 0),
                                                            (qp[p], s_qp, 1), (qp[p], s_qp, 1))):
                        n = w % 2
                        banks.read(pool, base, units["kq"[what], n])
                        if w >= 2:
                            pool.wait_ge(s_kc, 2 * (t + 2) + n + 1)
                        elif isinstance(t, int) and t == -2:
                            pass
                        else:
                            pool.wait_ge(s_qp, 2 * (t + 2) + n - 1)
                        pool.sem_inc(s_alone, 1)
                        pool.tensor_scalar(hi[:, n, :], raw[:, n, :], negc[:, what:what + 1], None,
                                           ALU.mult).then_inc(s_hi, 1)
                        if w == 0 and smax:
                            pool.wait_ge(s_kpad, 16 * HG * (t + 2))
                        pool.wait_ge(s_hi, 4 * (t + 2) + w + 1)
                        pool.tensor_tensor(dst[:, BANK * n:BANK * n + BANK], raw[:, n, :],
                                           hi[:, n, :].bitcast(F32), ALU.add).then_inc(s_dst, 1)

            turns(pool, body)

        @block.scalar
        def _(act):
            def body(t, g, p, units, first, base, st, smax, proj):
                if not st:
                    return
                for k in range(CH):
                    act.wait_ge(s_pv, CH * t + k + 1)
                    for j in range(HG):
                        for i, (a, b) in enumerate(pieces(q0_of(k))):
                            act.wait_ge(s_st, scores.n * t + scores.at[k, j, i] + 1)
                            act.activation(pr[k % 2][j][:, a:b], K.st[scores.bank((k, j, i))][:, 0:b - a], ACT.Exp,
                                           scale=scale).then_inc(s_p, 1)
                act.wait_ge(s_pv, CH * t + CH + 2)
                for h in range(2):
                    banks.read(act, base, units["den", h])
                act.activation(oe[:], K.o_ps[:], ACT.Copy).then_inc(s_oe, 1)

            turns(act, body)

        @block.vector
        def _(dve):
            def body(t, g, p, units, first, base, st, smax, proj):
                for k in range(1, CH + 1):
                    c = k - 1
                    if smax:
                        tiles = key_tiles(causal, c)
                        for j in range(HG):
                            for h in range(tiles):
                                n = units["max", c, j, h]
                                w = banks.filled(dve, base, n)
                                cols = min(BANK, P * (c + 1) - BANK * h) if causal else BANK
                                dst = mx[:, c % 2, j, h:h + 1] if tiles == 2 else \
                                    mz[:, c, 32 * j + MROW:32 * j + MROW + 1]
                                dve.reduce_max(dst, w[:, 0:cols], AX.X, negate=True)\
                                   .then_inc(banks.free[n[0]], 1)
                        if tiles == 2:
                            banks.read(dve, base, units["max", c, HG - 1, 0])
                            banks.read(dve, base, n)
                            dve.tensor_tensor(mz[:, c, MROW::32], mx[:, c % 2, :, 0], mx[:, c % 2, :, 1],
                                              ALU.min).then_inc(s_mz, 1)
                    if k in (2, 3) and proj:
                        for h in range(2):
                            n = units["kq"[k - 2], h]
                            w = banks.filled(dve, base, n)
                            if k == 2 and smax:
                                dve.wait_ge(s_qp, 2 * (t + 1) + h + 1)
                            if k == 3:
                                dve.wait_ge(s_kc, 2 * (t + 2) + h + 1)
                            dve.tensor_scalar(raw[:, h, :], w[:], wkq[:, 2 * P + k - 2:2 * P + k - 1], None,
                                              ALU.add).then_inc(banks.free[n[0]], 1)
                    if k == 1 and ("den", 0) in units:
                        dve.wait_ge(s_dn, 16 * (t + 1))
                        dve.reciprocal(rd[:], dn[:]).then_inc(s_rd, 1)
                    if k == 4 and ("den", 0) in units:
                        for h in range(2):
                            n = units["den", h]
                            w = banks.filled(dve, base, n)
                            dve.tensor_tensor(CT[:, t, BANK * h:BANK * h + BANK], oe[:, BANK * h:BANK * h + BANK],
                                              w[:], ALU.mult).then_inc(banks.free[n[0]], 1)
                    if k == 8 and smax:
                        for h in range(2):
                            n = units["v", h]
                            w = banks.filled(dve, base, n)
                            dve.tensor_tensor(v[1 - p][:, CB * h:CB * h + CB, :],
                                              w[:].rearrange("p (c d) -> p c d", d=P),
                                              wv[:, P:].unsqueeze(1).broadcast_to([P, CB, P]),
                                              ALU.add).then_inc(banks.free[n[0]], 1)
                    if k in (5, 8) and smax:
                        n = units["t", k // 8]
                        w = banks.filled(dve, base, n)
                        a = slice(BANK * (k // 8), BANK * (k // 8) + BANK)
                        dve.tensor_tensor(qa[1 - p][:, a], qp[1 - p][:, a].bitcast(F32), w[:],
                                          ALU.add).then_inc(banks.free[n[0]], 1)

            turns(dve, body)

        @block.tensor
        def _(pe):
            def weigh(k, h, t, p):
                a, b = max(q0_of(k), BANK * h), BANK * h + BANK
                if a >= b:
                    return None
                last_k = CB * h + CB - 1 if causal else CH - 1
                for j in range(HG):
                    r = slice(32 * j, 32 * j + 32)
                    last = pe.matmul(K.o_ps[r, a:b], v[p][:, k, r], pr[k % 2][j][:, a:b],
                                     start=(k == 0), stop=(k == last_k))
                return last

            def body(t, g, p, units, first, base, st, smax, proj):
                banks.all_read(pe, base, first, but_last=st)
                if st:
                    pe.wait_ge(s_kpad, 16 * HG * (t + 1))
                for k in range(CH + 1):
                    if k == 1 and smax:
                        pe.wait_ge(s_kpad, 16 * HG * (t + 2))
                        pe.wait_ge(s_qp, 2 * (t + 2))
                    for j in range(HG):
                        for h in range(2):
                            if smax and k >= 1 and h < key_tiles(causal, k - 1):
                                c = k - 1
                                n = units["max", c, j, h]
                                w = banks.claim(pe, base, n)
                                cols = min(BANK, P * (c + 1) - BANK * h) if causal else BANK
                                diag = causal and BANK * h + cols == P * (c + 1)
                                last = pe.matmul(w[:, 0:cols], qp[1 - p][:, P * c:P * c + P],
                                                 kpad[1 - p][:, j, BANK * h:BANK * h + cols],
                                                 start=True, stop=not diag)
                                if diag:
                                    last = pe.matmul(w[:, cols - P:cols], K.identb[:], K.maskq[:],
                                                     start=False, stop=True)
                                last.then_inc(banks.full[n[0]], 1)
                            if st and k < CH and h < len(pieces(q0_of(k))):
                                a, b = pieces(q0_of(k))[h]
                                if k == 0 and j == 0 and h == 1:
                                    banks.all_read(pe, base, first)
                                pe.wait_ge(s_p, scores.before(t, (k, j, h)))
                                bank = K.st[scores.bank((k, j, h))]
                                diag = causal and a == q0_of(k)
                                last = pe.matmul(bank[:, 0:b - a], kpad[p][:, j, P * k:P * k + P],
                                                 qa[p][:, a:b], start=True, stop=not diag)
                                if diag:
                                    last = pe.matmul(bank[:, 0:P], K.identb[:], K.maskk[:],
                                                     start=False, stop=True)
                                last.then_inc(s_st, 1)
                        if st and k >= 1 and j % 2 == 1:
                            if j == 1:
                                pe.wait_ge(s_p, scores.through(t, last_of(k - 1)))
                                if k == 1:
                                    pe.wait_ge(s_oe, t + 1)
                            last = weigh(k - 1, j // 2, t, p) or last
                            if j == 3:
                                last.then_inc(s_pv, 1)
                    if k == 4 and ("den", 0) in units:
                        pe.wait_ge(s_rr, 16 * (t + 1))
                        for h in range(2):
                            n = units["den", h]
                            w = banks.claim(pe, base, n)
                            pe.matmul(w[:], sel[:], rr[:, BANK * h:BANK * h + BANK],
                                      start=True, stop=True).then_inc(banks.full[n[0]], 1)
                    if k in (2, 3) and proj:
                        pe.wait_ge(s_wkq, g + 2)
                        for h in range(2):
                            n = units["kq"[k - 2], h]
                            w = banks.claim(pe, base, n)
                            pe.matmul(w[:], wkq[:, P * (k - 2):P * (k - 1)],
                                      XT[:, p * S + BANK * h:p * S + BANK * h + BANK],
                                      start=True, stop=True).then_inc(banks.full[n[0]], 1)
                    if k == 8 and smax:
                        pe.wait_ge(s_wv, g + 1 + p)
                        for h in range(2):
                            n = units["v", h]
                            w = banks.claim(pe, base, n)
                            for c in range(CB):
                                a = (1 - p) * S + P * (CB * h + c)
                                last = pe.matmul(w[:, P * c:P * c + P], XT[:, a:a + P], wv[:, 0:P],
                                                 start=True, stop=True)
                            last.then_inc(banks.full[n[0]], 1)
                    if k in (5, 8) and smax:
                        i = k // 8
                        n = units["t", i]
                        w = banks.claim(pe, base, n)
                        ready = sum(key_tiles(causal, c) == 2 for c in range(CB * i + CB))
                        if ready:
                            pe.wait_ge(s_mz, NQ * (t + 1) + ready)
                        for c in range(CB):
                            last = pe.transpose(w[:, P * c:P * c + P], mz[:, CB * i + c, :], ident[:])
                        last.then_inc(banks.full[n[0]], 1)

            turns(pe, body)


class Kept:

    def __init__(self, nc, stack):
        def sb(name, shape, dt=F32):
            return stack.enter_context(nc.sbuf_tensor(name, shape, dt))

        self.X = sb("X", [P, NC, D])
        self.XT = sb("XT", [D, NT])
        self.CT = None
        self.xh = sb("xh", [D, NT], F32R)
        self.xl = sb("xl", [D, NT], F32R)
        self.comb = sb("comb", [P, E1, NC])
        self.acc_slots = sb("acc", [P, NC + 1, D])
        self.acc = self.acc_slots[:, 1:, :]
        self.ident = sb("ident_sb", [P, P])
        self.identb = sb("identb", [P, P], BF16)
        self.maskq = sb("maskq_sb", [P, P], BF16)
        self.maskk = sb("maskk_sb", [P, P], BF16)
        self.st = [stack.enter_context(nc.psum_tensor(f"st{i}", [P, BANK], F32)) for i in range(SB)]
        self.work = [stack.enter_context(nc.psum_tensor(f"work{i}", [P, BANK], F32)) for i in range(WB)]
        self.o_ps = stack.enter_context(nc.psum_tensor("o_ps", [P, S], F32))


class GroupBuffers:

    def __init__(self, nc, stack):
        def sb(name, shape, dt=F32):
            return stack.enter_context(nc.sbuf_tensor(name, shape, dt))

        self.gw = sb("gw", [P, G, GW])
        self.negc = sb("negc_sb", [P, 2])
        self.sel = sb("sel_sb", [P, P])
        self.kpad = [sb(f"kpad{i}", [P, HG, S], F32R) for i in range(2)]
        self.mz = sb("mz", [P, CH, P])
        self.oe = sb("oe", [P, S])
        self.rr = sb("rr", [P, S])


def norm_phase(nc, K, src, tag, add, out=None, ahead=()):
    ph = Phase(nc, tag)
    X, XT, CT = K.X, K.XT, K.CT
    bias = ph.sb("bias", [P, D])
    wo = ph.sb("wo", [P, G, D])
    z = ph.sb("z", [P, 2, CB, D])
    stats = ph.sb("stats", [P, 2, CB, 6])
    mv = ph.sb("mv", [P, 2, CB, 2])
    var = ph.sb("var", [P, 2, CB])
    std = ph.sb("std", [P, 2, CB])
    rs = ph.sb("rs", [P, 2, CB])
    banks = Banks(ph, K.work[:2])
    s_load, s_v, s_var, s_std, s_x, s_out = (ph.sem(x) for x in ("loaded", "step", "variance", "std", "x", "out"))
    s_y = ph.sem("projected")
    s_ahead = ph.sem("ahead")
    s_yr = ph.sem("projection_read")
    needs = {"context": 32, "rows": 16}.get(add, 0)

    with ph.block() as block:

        @block.sync
        def _(sp):
            if add == "context":
                sp.dma_start(wo[:], src["wo"]).then_inc(s_load, 16)
            if needs:
                sp.dma_start(bias[:], src["bias"].partition_broadcast(P)).then_inc(s_load, 16)
            for dst, tensor in ahead:
                sp.dma_start(dst[:], tensor).then_inc(s_ahead, 16)
            if ahead:
                sp.wait_ge(s_ahead, 16 * len(ahead))
            if out is not None:
                ov = out.rearrange("b (c p) d -> p (b c) d", p=P)
                for n in range(NB):
                    sp.wait_ge(s_x, n + 1)
                    sp.dma_start(ov[:, CB * n:CB * n + CB, :], X[:, CB * n:CB * n + CB, :]).then_inc(s_out, 16)
                sp.wait_ge(s_out, 16 * NB)

        @block.scalar
        def _(act):
            for n in range(NB):
                act.wait_ge(s_var, n + 1)
                act.activation(std[:, n % 2, :], var[:, n % 2, :], ACT.Sqrt).then_inc(s_std, 1)
                if out is None and n:
                    w = banks.filled(act, NONE, alternate(n - 1))
                    act.activation(XT[:, BANK * (n - 1):BANK * n], w[:], ACT.Copy)\
                       .then_inc(banks.free[(n - 1) % 2], 1)
            if out is None:
                w = banks.filled(act, NONE, alternate(NB - 1))
                act.activation(XT[:, BANK * (NB - 1):], w[:], ACT.Copy).then_inc(banks.free[(NB - 1) % 2], 1)

        @block.vector
        def _(dve):
            steps = [0]

            def then(ins):
                steps[0] += 1
                ins.then_inc(s_v, 1)
                dve.wait_ge(s_v, steps[0])

            if needs:
                dve.wait_ge(s_load, needs)
            for n in range(NB):
                xs, zs = X[:, CB * n:CB * n + CB, :], z[:, n % 2]
                bc = bias[:].unsqueeze(1).broadcast_to([P, CB, D])
                if add == "context":
                    dve.wait_ge(s_y, n + 1)
                    w = K.st[n % 2][:, 0:BANK].rearrange("p (c d) -> p c d", d=D)
                    ins = dve.tensor_tensor(zs, w, xs, ALU.add)
                    ins.then_inc(s_yr, 1)
                    dve.wait_ge(s_yr, n + 1)
                    then(dve.tensor_tensor(zs, zs, bc, ALU.add))
                elif add == "moe":
                    then(dve.scalar_tensor_tensor(zs, K.acc[:, CB * n:CB * n + CB, :], 0.3, xs, ALU.mult, ALU.add))
                    then(dve.tensor_tensor(zs, zs, xs, ALU.add))
                elif add == "rows":
                    then(dve.tensor_tensor(zs, K.acc[:, CB * n:CB * n + CB, :], xs, ALU.add))
                    then(dve.tensor_tensor(zs, zs, bc, ALU.add))
                else:
                    then(dve.tensor_tensor(zs, K.acc[:, CB * n:CB * n + CB, :], xs, ALU.add))
                    then(dve.tensor_scalar(zs, zs, -100.0, 100.0, ALU.max, ALU.min))
                    then(dve.tensor_tensor(zs, zs, xs, ALU.add))
                for c in range(CB):
                    last = dve.bn_stats(stats[:, n % 2, c, :], z[:, n % 2, c, :])
                then(last)
                for c in range(CB):
                    last = dve.bn_aggr(mv[:, n % 2, c, :], stats[:, n % 2, c, :])
                then(last)
                dve.tensor_scalar(var[:, n % 2, :], mv[:, n % 2, :, 1], EPS, None, ALU.add).then_inc(s_var, 1)
                dve.wait_ge(s_std, n + 1)
                then(dve.reciprocal(rs[:, n % 2, :], std[:, n % 2, :]))
                for c in range(CB):
                    last = dve.tensor_scalar(X[:, CB * n + c, :], z[:, n % 2, c, :], mv[:, n % 2, c, 0:1],
                                             rs[:, n % 2, c:c + 1], ALU.subtract, ALU.mult)
                last.then_inc(s_x, 1)

        @block.tensor
        def _(pe):
            if add == "context":
                pe.wait_ge(s_load, 32)

            def project(n):
                if n >= 2:
                    pe.wait_ge(s_yr, n - 1)
                for c in range(CB):
                    b, a = divmod(P * (CB * n + c), S)
                    for g in range(G):
                        last = pe.matmul(K.st[n % 2][:, P * c:P * c + P], CT[:, B * g + b + 1, a:a + P],
                                         wo[:, g, :], start=(g == 0), stop=(g == G - 1))
                last.then_inc(s_y, 1)

            if add == "context":
                project(0)
            for n in range(NB):
                if add == "context" and n + 1 < NB:
                    project(n + 1)
                if out is None:
                    pe.wait_ge(s_x, n + 1)
                    w = banks.claim(pe, NONE, alternate(n))
                    for c in range(CB):
                        last = pe.transpose(w[:, P * c:P * c + P], X[:, CB * n + c, :], K.ident[:])
                    last.then_inc(banks.full[n % 2], 1)


def route_phase(nc, K, src, tag, experts, latent, floor, plus):
    ph = Phase(nc, tag)
    E = experts
    CT = K.CT
    wo = ph.sb("wo", [P, G, D])
    ob = ph.sb("ob", [P, 1])
    rw = ph.sb("rw", [D, E])
    rb = ph.sb("rb", [P, E])
    rank = ph.sb("rank", [P, E])
    lg = ph.sb("lg", [P, NC, E])
    pb = ph.sb("probs", [P, NC, E])
    eq = ph.sb("eq", [P, NC, E])
    one = ph.sb("one", [P, 2, NC, E])
    m = ph.sb("m", [P, 8, NC])
    MT = ph.sb("MT", [D, NT]) if latent else K.XT
    s_load, s_lg, s_v, s_e, s_s = (ph.sem(x) for x in ("loaded", "logits", "step", "shifted", "exp"))
    s_hi, s_lo = ph.sem("hi"), ph.sem("lo")
    s_mt = ph.sem("mt")
    banks = Banks(ph, K.work[:2])

    def over(x):
        return x.unsqueeze(2).broadcast_to([P, NC, E])

    with ph.block() as block:

        @block.sync
        def _(sp):
            sp.dma_start(rw[:], src["rw"]).then_inc(s_load, 16)
            sp.dma_start(rank[:], src["rank"]).then_inc(s_load, 16)
            sp.dma_start(rb[:], src["rb"].partition_broadcast(P)).then_inc(s_load, 16)
            if latent:
                sp.dma_start(wo[:], src["wo"]).then_inc(s_load, 16)
                sp.dma_start(ob[:], src["ob"]).then_inc(s_load, 16)

        @block.scalar
        def _(act):
            if latent:
                act.wait_ge(s_load, 80)
                for n in range(NB):
                    w = banks.filled(act, NONE, alternate(n))
                    act.activation(MT[:, BANK * n:BANK * n + BANK], w[:], ACT.Identity,
                                   bias=ob[:]).then_inc(banks.free[n % 2], 1)
            act.wait_ge(s_e, 1)
            act.activation(pb[:], lg[:], ACT.Exp).then_inc(s_s, 1)

        @block.gpsimd
        def _(pool):
            for n in range(NB):
                a = slice(BANK * n, BANK * n + BANK)
                if latent:
                    banks.read(pool, NONE, alternate(n))
                pool.tensor_copy(K.xh[:, a], MT[:, a]).then_inc(s_hi, 1)
                pool.wait_ge(s_hi, n + 1)
                pool.tensor_tensor(K.xl[:, a], MT[:, a], K.xh[:, a].bitcast(F32), ALU.subtract).then_inc(s_lo, 1)

        @block.vector
        def _(dve):
            steps = [0]

            def then(ins):
                steps[0] += 1
                ins.then_inc(s_v, 1)
                dve.wait_ge(s_v, steps[0])

            dve.wait_ge(s_load, 80 if latent else 48)
            dve.wait_ge(s_lg, 1)
            w = K.o_ps[:, 0:NC * E].rearrange("p (c e) -> p c e", e=E)
            then(dve.tensor_tensor(lg[:], w, rb[:].unsqueeze(1).broadcast_to([P, NC, E]), ALU.add))
            then(dve.reduce_max(m[:, 0, :], lg[:], AX.X))
            dve.tensor_tensor(lg[:], lg[:], over(m[:, 0, :]), ALU.subtract).then_inc(s_e, 1)
            dve.wait_ge(s_s, 1)
            then(dve.reduce_sum(m[:, 1, :], pb[:], AX.X))
            then(dve.reciprocal(m[:, 2, :], m[:, 1, :]))
            then(dve.tensor_tensor(pb[:], pb[:], over(m[:, 2, :]), ALU.mult))
            for i in range(2):
                then(dve.reduce_max(m[:, 3 + i, :], pb[:], AX.X))
                then(dve.tensor_tensor(eq[:], pb[:], over(m[:, 3 + i, :]), ALU.is_equal))
                then(dve.tensor_tensor(eq[:], eq[:], rank[:].unsqueeze(1).broadcast_to([P, NC, E]), ALU.mult))
                then(dve.reduce_max(m[:, 5, :], eq[:], AX.X))
                then(dve.tensor_tensor(one[:, i], eq[:], over(m[:, 5, :]), ALU.is_equal))
                if i == 0:
                    then(dve.scalar_tensor_tensor(pb[:], one[:, 0], -4.0, pb[:], ALU.mult, ALU.add))
            then(dve.tensor_tensor(m[:, 6, :], m[:, 3, :], m[:, 4, :], ALU.add))
            then(dve.tensor_scalar(m[:, 6, :], m[:, 6, :], plus, floor, ALU.add, ALU.max))
            then(dve.reciprocal(m[:, 7, :], m[:, 6, :]))
            for i in range(2):
                then(dve.tensor_tensor(m[:, 3 + i, :], m[:, 3 + i, :], m[:, 7, :], ALU.mult))
                then(dve.tensor_tensor(one[:, i], one[:, i], over(m[:, 3 + i, :]), ALU.mult))
            then(dve.tensor_tensor(K.comb[:, 0:E, :].rearrange("p e c -> p c e"), one[:, 0], one[:, 1], ALU.add))

        @block.tensor
        def _(pe):
            pe.wait_ge(s_load, 80 if latent else 48)
            if latent:
                for n in range(NB):
                    w = banks.claim(pe, NONE, alternate(n))
                    b, a = divmod(BANK * n, S)
                    for g in range(G):
                        last = pe.matmul(w[:], wo[:, g, :], CT[:, B * g + b + 1, a:a + BANK],
                                         start=(g == 0), stop=(g == G - 1))
                    last.then_inc(banks.full[n % 2], 1)
                banks.read(pe, NONE, alternate(NB - 2))
                banks.read(pe, NONE, alternate(NB - 1))
            for c in range(NC):
                last = pe.matmul(K.o_ps[:, E * c:E * c + E], MT[:, P * c:P * c + P], rw[:], start=True, stop=True)
            last.then_inc(s_lg, 1)


def experts_phase(nc, K, src, tag, experts, ahead=()):
    ph = Phase(nc, tag)
    E = experts
    w1 = [ph.sb(f"w1{i}", [D, F]) for i in range(2)]
    w2 = [ph.sb(f"w2{i}", [P, FC, D]) for i in range(2)]
    b1 = [ph.sb(f"b1{i}", [P, FC]) for i in range(2)]
    b2 = [ph.sb(f"b2{i}", [P, D]) for i in range(2)]
    w1h = [ph.sb(f"w1h{i}", [D, F], F32R) for i in range(2)]
    w1l = [ph.sb(f"w1l{i}", [D, F], F32R) for i in range(2)]
    hid = [ph.sb(f"hid{i}", [P, FC, BANK]) for i in range(2)]
    y = [ph.sb(f"y{i}", [P, CB, D]) for i in range(2)]
    credit = ph.sb("credit", [P, 4])
    s_w = [ph.sem(f"weights{i}") for i in range(2)]
    s_alone = ph.sem("alone")
    s_ahead = ph.sem("ahead")
    s_wh, s_ws = ph.sem("w1_hi"), ph.sem("w1_split")
    s_up, s_g, s_dn, s_y, s_yc, s_a = (ph.sem(x) for x in ("up", "gelu", "down", "biased", "weighted", "added"))

    with ph.block() as block:

        def pairs(eng, body):
            with eng.Fori(0, E // 2 - 1) as q:
                for p in range(2):
                    body(2 * q + p, q, p)
            for p in range(2):
                body(E - 2 + p, E // 2 - 1, p)

        @block.sync
        def _(sp):
            def body(e, q, p):
                sp.wait_ge(s_yc, NB * e + 1)
                sp.sem_inc(s_alone, 1)
                sp.dma_start(w1[p][:], src["w1"][e]).then_inc(s_w[p], 16)
                sp.dma_start(w2[p][:], src["w2"][e].rearrange("(c p) d -> p c d", p=P))\
                  .then_inc(s_w[p], 16)
                sp.dma_start(b1[p][:], src["b1"][e]).then_inc(s_w[p], 16)
                sp.dma_start(b2[p][:], src["b2"][e].partition_broadcast(P))\
                  .then_inc(s_w[p], 16)

            for dst, tensor in ahead:
                sp.dma_start(dst[:], tensor).then_inc(s_ahead, 16)
            pairs(sp, body)
            if ahead:
                sp.wait_ge(s_ahead, 16 * len(ahead))

        @block.gpsimd
        def _(pool):
            pool.memset(credit[:, 0:1], 0.0).then_inc(s_g, 4)
            pool.memset(credit[:, 1:2], 0.0).then_inc(s_dn, 2)
            pool.memset(credit[:, 2:3], 0.0).then_inc(s_yc, NB + 1)
            pool.memset(K.acc, 0.0).then_inc(s_a, 2)

            def body(e, q, p):
                for n in range(NB):
                    m = NB * e + n
                    a = slice(CB * n, CB * n + CB)
                    pool.wait_ge(s_yc, m + 2 + NB)
                    pool.wait_ge(s_a, 2 + m)
                    pool.tensor_tensor(K.acc[:, a, :], K.acc[:, a, :], y[n % 2][:], ALU.add).then_inc(s_a, 1)

            pairs(pool, body)

        @block.scalar
        def _(act):
            def body(e, q, p):
                act.wait_ge(s_w[p], 64 * (q + 1))
                for n in range(NB):
                    m = NB * e + n
                    act.wait_ge(s_dn, m + 1)
                    for f in range(FC):
                        act.wait_ge(s_up, FC * m + f + 1)
                        act.activation(hid[n % 2][:, f, :], (K.work[f] if n % 2 else K.st[f])[:],
                                       ACT.Gelu, bias=b1[p][:, f:f + 1]).then_inc(s_g, 1)

            pairs(act, body)

        @block.vector
        def _(dve):
            def split(e, q, p):
                dve.wait_ge(s_w[p], 64 * (q + 1))
                dve.tensor_copy(w1h[p][:], w1[p][:]).then_inc(s_wh, 1)
                dve.wait_ge(s_wh, e + 1)
                dve.tensor_tensor(w1l[p][:], w1[p][:], w1h[p][:].bitcast(F32), ALU.subtract).then_inc(s_ws, 1)

            def body(e, q, p):
                for n in range(NB):
                    m = NB * e + n
                    dve.wait_ge(s_dn, m + 3)
                    dve.wait_ge(s_a, m + 1)
                    dve.tensor_tensor(y[n % 2][:], K.o_ps[:, BANK * (n % 2):BANK * (n % 2) + BANK]
                                      .rearrange("p (c d) -> p c d", d=D),
                                      b2[p][:].unsqueeze(1).broadcast_to([P, CB, D]), ALU.add).then_inc(s_y, 1)
                    dve.wait_ge(s_y, m + 1)
                    dve.tensor_tensor(y[n % 2][:], y[n % 2][:],
                                      K.comb[:, e, CB * n:CB * n + CB].unsqueeze(2).broadcast_to([P, CB, D]),
                                      ALU.mult).then_inc(s_yc, 1)
                    if n == 1 and not (isinstance(e, int) and e == E - 1):
                        split(e + 1, q + p, 1 - p)

            split(0, 0, 0)
            pairs(dve, body)

        @block.tensor
        def _(pe):
            def up(e, p, n):
                m = NB * e + n
                for f in range(FC):
                    pe.wait_ge(s_g, FC * m + f + 1)
                    t = (K.work[f] if n % 2 else K.st[f])[:]
                    a, r = slice(P * f, P * f + P), slice(BANK * n, BANK * n + BANK)
                    pe.matmul(t, w1h[p][:, a], K.xh[:, r], start=True, stop=False)
                    pe.matmul(t, w1h[p][:, a], K.xl[:, r], start=False, stop=False)
                    pe.matmul(t, w1l[p][:, a], K.xh[:, r], start=False, stop=True).then_inc(s_up, 1)

            def down(e, p, n, m):
                pe.wait_ge(s_g, FC * m + FC + 4)
                for c in range(CB):
                    for f in range(FC):
                        last = pe.matmul(K.o_ps[:, BANK * (n % 2) + P * c:BANK * (n % 2) + P * c + P], hid[n % 2][:, f, P * c:P * c + P],
                                         w2[p][:, f, :], start=(f == 0), stop=(f == FC - 1))
                last.then_inc(s_dn, 1)

            def body(e, q, p):
                pe.wait_ge(s_ws, e + 1)
                for n in range(NB):
                    up(e, p, n)
                    if n:
                        pe.wait_ge(s_yc, NB * e + n - 1 + NB)
                        down(e, p, n - 1, NB * e + n - 1)
                pe.wait_ge(s_yc, NB * e + NB - 1 + NB)
                down(e, p, NB - 1, NB * e + NB - 1)

            pairs(pe, body)


def row_units(proj, smax, st, den, out):
    u = []
    for k in range(CH + 1):
        if smax and k < CH:
            u += [("max", k, h) for h in range(key_tiles(True, k))]
        if proj and k:
            u += [("k", k // 2)] if k < CH and k % 2 == 0 else [("q", k // 2)] if k < CH else \
                 [("v", 0), ("v", 1)]
            if k == 7:
                u += [("k", 0)]
        if k == 1 and den:
            u += [("den", 0)]
        if k == 3 and out:
            u += [("out", 0)]
        if k in (5, 8) and smax:
            u += [("t", k // 8)]
    return u


class RowWeights:
    def __init__(self, nc, stack):
        def sb(name, shape):
            return stack.enter_context(nc.sbuf_tensor(name, shape, F32))

        self.wq = sb("wq", [D, H, P])
        self.wk = sb("wk", [D, H, P])
        self.wv = sb("wv", [D, H * HS])
        self.pw = sb("pw", [P, H // 2, D])


def rows_phase(nc, K, rw, tag, scale):
    ph = Phase(nc, tag)
    XT, acc = K.XT, K.acc_slots
    wq, wk, wv, pw = rw.wq, rw.wk, rw.wv, rw.pw
    xt = ph.sb("xt", [D, P])
    qa = [ph.sb(f"qa{i}", [P, 2 * S], F32R) for i in range(2)]
    qb = [ph.sb(f"qb{i}", [P, 2 * S], F32R) for i in range(2)]
    ka = [ph.sb(f"ka{i}", [P, 2 * S], F32R) for i in range(2)]
    kb = [ph.sb(f"kb{i}", [P, 2 * S], F32R) for i in range(2)]
    vs = ph.sb("vs", [P, H * HS])
    v = [ph.sb(f"v{i}", [P, 2 * CH, HS]) for i in range(2)]
    ps = [ph.sb(f"ps{i}", [P, S]) for i in range(2)]
    pr = [None] + [ph.sb(f"p{c}", [P, S - P * c]) for c in range(1, CH)]
    ones = ph.sb("ones", [P, HS])
    mx = ph.sb("mx", [P, 2, 2])
    mz = ph.sb("mz", [P, CH, P])
    rd = ph.sb("rd", [P, BANK])
    on = [ph.sb(f"on{i}", [P, BANK]) for i in range(2)]
    credit = ph.sb("credit", [P, 4])
    vd = [nc.dram_tensor(f"{tag}_values{i}", [P * H, HS], F32).ap() for i in range(2)]

    banks = Banks(ph, K.work)
    s_alone = ph.sem("alone")
    s_set = ph.sem("rows_set")
    s_zero, s_xt, s_rnd, s_kb, s_vs, s_vd, s_v = (ph.sem(x) for x in (
        "zeroed", "tokens_staged", "rounded", "kb_made", "values", "values_in_dram", "values_in_rows"))
    s_mz, s_st, s_p, s_pv, s_add, s_on = (ph.sem(x) for x in (
        "maxima", "scores_t", "exp_done", "pv_done", "added", "normalized"))

    head = [row_units(True, False, False, False, False), row_units(False, True, False, False, False)]
    quad = [row_units(r % 2 == 0, True, True, True, r % 2 == 0) for r in range(4)]
    last = [row_units(True, True, True, True, True), quad[1], row_units(False, True, True, True, True),
            row_units(False, False, True, True, False), row_units(False, False, False, True, True)]

    head, quad, last = Places(head), Places(quad), Places(last)
    NQUAD = NP // 4
    scores = Scores([(c, i) for c in range(CH) for i in range(len(pieces(P * c)))])

    def last_of(c):
        return c, len(pieces(P * c)) - 1

    def turns(eng, body):
        body(-2, 2, -1, *head.turn(0), NONE, True, False, False)
        body(-1, 3, -1, *head.turn(1), NONE, False, True, False)
        with eng.Fori(0, NQUAD - 1) as q:
            base = [n + m * q for n, m in zip(head.total, quad.total)]
            for r in range(4):
                body(4 * q + r, r, 2 * q + r // 2, *quad.turn(r), base, r % 2 == 0, True, True)
        n, base = NP - 4, [n + m * (NQUAD - 1) for n, m in zip(head.total, quad.total)]
        for r in range(5):
            body(n + r, r % 4, (n + r) // 2, *last.turn(r), base, r == 0, r < 3, r < 4)

    with ph.block() as block:

        @block.sync
        def _(sp):
            def body(n, r, pair, at, first, base, proj, smax, st):
                if proj:
                    i = 1 - r // 2
                    sp.wait_ge(s_vs, 2 * (pair + 2))
                    sp.dma_start(vd[i].rearrange("(x i) k -> x (i k)", i=H), vs[:]).then_inc(s_vd, 16)
                    sp.wait_ge(s_vd, 16 * (pair + 2))
                    sp.dma_start(v[i][:], vd[i].rearrange("(c p) k -> p c k", p=P)).then_inc(s_v, 16)

            turns(sp, body)

        @block.gpsimd
        def _(pool):
            pool.memset(mz[:], 0.0).then_inc(s_zero, 1)
            pool.memset(ones[:], 1.0).then_inc(s_zero, 1)
            pool.memset(ps[1][:], 1.0).then_inc(s_zero, 1)
            pool.memset(on[0][:], 0.0).then_inc(s_zero, 1)
            pool.memset(credit[:, 0:1], 0.0).then_inc(s_p, SB)
            pool.memset(credit[:, 3:4], 0.0).then_inc(s_on, 1)
            pool.memset(credit[:, 1:2], 0.0).then_inc(s_pv, CH)
            pool.memset(credit[:, 2:3], 0.0).then_inc(s_add, CH - 1)

            def body(n, r, pair, at, first, base, proj, smax, st):
                i = 1 - r // 2
                if proj:
                    banks.all_read(pool, base, first)
                    pool.sem_inc(s_alone, 1)
                    pool.tensor_copy(xt[:], XT[:, bass.ds((pair + 1) * P, P)]).then_inc(s_xt, 1)
                for c in range(1, CH):
                    if st:
                        if c == 1:
                            pool.wait_ge(s_pv, CH * n + 1 + CH)
                        pool.wait_ge(s_p, scores.through(n, last_of(c)))
                        pool.wait_ge(s_add, (CH - 1) * n + c - 1 + CH - 1)
                        pool.tensor_tensor(ps[r % 2][:, P * c:], ps[r % 2][:, P * c:], pr[c][:],
                                           ALU.add).then_inc(s_add, 1)
                if proj:
                    for h in range(4):
                        banks.read(pool, base, at["k", h])
                    pool.sem_inc(s_alone, 1)
                    pool.tensor_copy(kb[i][0:HS, :], ka[i][0:HS, :].bitcast(F32)).then_inc(s_kb, 1)

            turns(pool, body)

        @block.scalar
        def _(act):
            act.wait_ge(s_set, 7)

            def body(n, r, pair, at, first, base, proj, smax, st):
                i = 1 - r // 2
                for k in range(CH + 1):
                    if st and k < CH:
                        if k == 0:
                            act.wait_ge(s_on, n + 1)
                        else:
                            act.wait_ge(s_add, (CH - 1) * n + k)
                            act.wait_ge(s_pv, CH * n + k + 1)
                        for x, (a, b) in enumerate(pieces(P * k)):
                            act.wait_ge(s_st, scores.n * n + scores.at[k, x] + 1)
                            dst = pr[k][:, a - P * k:b - P * k] if k else ps[r % 2][:, a:b]
                            act.activation(dst, K.st[scores.bank((k, x))][:, 0:b - a], ACT.Exp, scale=scale).then_inc(s_p, 1)
                    if proj and k >= 1:
                        for x, u in enumerate(u for u in at if u[0] in "kq" and step_of(u) == k):
                            w = banks.filled(act, base, at[u])
                            dst = (ka if u[0] == "k" else qa)[i][:].rearrange("p (t i) -> p i t", i=H)
                            act.activation(dst[:, 4 * u[1]:4 * u[1] + 4, :],
                                           w[:].rearrange("p (i t) -> p i t", i=4), ACT.Copy).then_inc(s_rnd, 1)
                        if k == CH:
                            if not (isinstance(n, int) and n < 0):
                                act.wait_ge(s_vd, 16 * (pair + 1))
                            for h in range(2):
                                w = banks.filled(act, base, at["v", h])
                                act.activation(vs[:, BANK * h:BANK * h + BANK], w[:], ACT.Copy)\
                                   .then_inc(banks.free[at["v", h][0]], 1)
                                banks.read(act, base, at["v", h])
                                act.nop().then_inc(s_vs, 1)
                    if k in (5, 8) and smax:
                        u = at["t", k // 8]
                        w = banks.filled(act, base, u)
                        m, j = (r + 1) % 4 // 2, (r + 1) % 2
                        a = S * j + BANK * (k // 8)
                        act.activation(qb[m][HS:HS + 1, a:a + BANK], w[HS:HS + 1, :], ACT.Copy)\
                           .then_inc(banks.free[u[0]], 1)

            turns(act, body)

        @block.vector
        def _(dve):

            def body(n, r, pair, at, first, base, proj, smax, st):
                i = 1 - r // 2
                for k in range(CH + 1):
                    c = k
                    if smax and k < CH:
                        tiles = key_tiles(True, c)
                        for h in range(tiles):
                            u = at["max", c, h]
                            w = banks.filled(dve, base, u)
                            cols = min(BANK, P * (c + 1) - BANK * h)
                            dst = mx[:, c % 2, h:h + 1] if tiles == 2 else mz[:, c, HS:HS + 1]
                            dve.reduce_max(dst, w[:, 0:cols], AX.X, negate=True).then_inc(banks.free[u[0]], 1)
                        if tiles == 2:
                            banks.read(dve, base, at["max", c, 0])
                            banks.read(dve, base, u)
                            dve.tensor_tensor(mz[:, c, HS:HS + 1], mx[:, c % 2, 0:1], mx[:, c % 2, 1:2],
                                              ALU.min).then_inc(s_mz, 1)
                    if proj and k:
                        for x in (x for x in at if x[0] in "kq" and step_of(x) == k):
                            w = banks.filled(dve, base, at[x])
                            done = [y for y in at if y[0] in "kq"].index(x)
                            dve.wait_ge(s_rnd, 8 * (pair + 1) + done + 1)
                            hi, lo, rows = (ka, ka, slice(HS, P)) if x[0] == "k" else (qa, qb, slice(0, HS))
                            hi, lo = (b[i][rows, :].rearrange("p (t i) -> p i t", i=H)[:, 4 * x[1]:4 * x[1] + 4, :]
                                      for b in (hi, lo))
                            dve.tensor_tensor(lo, w[rows, :].rearrange("p (i t) -> p i t", i=4),
                                              hi.bitcast(F32), ALU.subtract).then_inc(banks.free[at[x][0]], 1)
                    if k == 1 and ("den", 0) in at:
                        u = at["den", 0]
                        w = banks.filled(dve, base, u)
                        dve.wait_ge(s_on, n + 1)
                        dve.reciprocal(rd[:], w[:]).then_inc(banks.free[u[0]], 1)
                        banks.read(dve, base, u)
                        o = (r + 1) % 2
                        dve.tensor_tensor(on[o][:], K.o_ps[:, BANK * o:BANK * o + BANK], rd[:],
                                          ALU.mult).then_inc(s_on, 1)
                    if k == 3 and ("out", 0) in at:
                        u = at["out", 0]
                        w = banks.filled(dve, base, u)
                        dve.tensor_copy(acc[:, pair, :], w[:, 0:D]).then_inc(banks.free[u[0]], 1)

            for i in range(2):
                dve.memset(kb[i][HS:P, :].bitcast(F32), 0.0).then_inc(s_set, 1)
                dve.memset(qb[i][HS:P, :].bitcast(F32), 0.0).then_inc(s_set, 1)
            dve.memset(K.o_ps[:, BANK:], 0.0).then_inc(s_set, 1)
            dve.wait_ge(s_set, 5)
            dve.memset(kb[0][HS:HS + 1, :].bitcast(F32), 1.0).then_inc(s_set, 1)
            dve.memset(kb[1][HS:HS + 1, :].bitcast(F32), 1.0).then_inc(s_set, 1)
            dve.wait_ge(s_zero, 4)
            turns(dve, body)

        @block.tensor
        def _(pe):
            pe.wait_ge(s_set, 7)
            pe.wait_ge(s_zero, 4)

            def body(n, r, pair, at, first, base, proj, smax, st):
                cur, j = r // 2, r % 2
                nxt, nj = (r + 1) % 4 // 2, (r + 1) % 2
                banks.all_read(pe, base, first, but_last=st)
                if st:
                    pe.wait_ge(s_kb, pair + 1)
                    if j == 0:
                        pe.wait_ge(s_v, 16 * (pair + 1))
                for k in range(CH + 1):
                    for h in range(2):
                        if smax and k < CH and h < key_tiles(True, k):
                            c = k
                            u = at["max", c, h]
                            w = banks.claim(pe, base, u)
                            cols = min(BANK, P * (c + 1) - BANK * h)
                            diag = BANK * h + cols == P * (c + 1)
                            a = S * nj
                            last = pe.matmul(w[:, 0:cols], qa[nxt][:, a + P * c:a + P * c + P],
                                             ka[nxt][:, a + BANK * h:a + BANK * h + cols],
                                             start=True, stop=not diag)
                            if diag:
                                last = pe.matmul(w[:, cols - P:cols], K.identb[:], K.maskq[:],
                                                 start=False, stop=True)
                            last.then_inc(banks.full[u[0]], 1)
                        if st and k < CH and h < len(pieces(P * k)):
                            a, b = pieces(P * k)[h]
                            if k == 0 and h == 1:
                                banks.all_read(pe, base, first)
                            pe.wait_ge(s_p, scores.before(n, (k, h)))
                            bank = K.st[scores.bank((k, h))]
                            s0, t = S * j, bank[:, 0:b - a]
                            diag = a == P * k
                            pe.matmul(t, ka[cur][:, s0 + P * k:s0 + P * k + P], qa[cur][:, s0 + a:s0 + b],
                                      start=True, stop=False)
                            last = pe.matmul(t, kb[cur][:, s0 + P * k:s0 + P * k + P], qb[cur][:, s0 + a:s0 + b],
                                             start=False, stop=not diag)
                            if diag:
                                last = pe.matmul(bank[:, 0:P], K.identb[:], K.maskk[:],
                                                 start=False, stop=True)
                            last.then_inc(s_st, 1)
                    if st and k >= 1:
                        c = k - 1
                        pe.wait_ge(s_p, scores.through(n, last_of(c)))
                        if c == 0:
                            pe.wait_ge(s_on, n + 1)
                        p = pr[c] if c else ps[j]
                        for odd in range(2):
                            last = pe.matmul(K.o_ps[HS * odd:HS * odd + HS, BANK * j + P // 2 * c:BANK * (j + 1)],
                                             v[cur][:, CH * j + c, :], p[:, odd::2],
                                             start=(c == 0), stop=(c == CH - 1))
                        last.then_inc(s_pv, 1)
                    if proj and k >= 1:
                        if k == 1:
                            pe.wait_ge(s_xt, pair + 2)
                        for x in (x for x in at if x[0] in "kq" and step_of(x) == k):
                            w = banks.claim(pe, base, at[x])
                            for e in range(4):
                                last = pe.matmul(w[:, P * e:P * e + P], (wk if x[0] == "k" else wq)[:, 4 * x[1] + e, :],
                                                 xt[:], start=True, stop=True)
                            last.then_inc(banks.full[at[x][0]], 1)
                        if k == CH:
                            for h in range(2):
                                w = banks.claim(pe, base, at["v", h])
                                pe.matmul(w[:], xt[:], wv[:, BANK * h:BANK * h + BANK],
                                          start=True, stop=True).then_inc(banks.full[at["v", h][0]], 1)
                    if k == 1 and ("den", 0) in at:
                        u = at["den", 0]
                        w = banks.claim(pe, base, u)
                        pe.wait_ge(s_add, (CH - 1) * n + CH - 1)
                        for odd in range(2):
                            last = pe.matmul(w[HS * odd:HS * odd + HS, :], ones[:], ps[1 - j][:, odd::2],
                                             start=True, stop=True)
                        last.then_inc(banks.full[u[0]], 1)
                    if k == 3 and ("out", 0) in at:
                        u = at["out", 0]
                        w = banks.claim(pe, base, u)
                        pe.wait_ge(s_on, n + 2)
                        for e in range(H // 2):
                            for m in range(2):
                                last = pe.matmul(w[HS * m:HS * m + HS, 0:D], on[m][:, e::H // 2], pw[:, e, :],
                                                 start=(e == 0), stop=(e == H // 2 - 1))
                        last.then_inc(banks.full[u[0]], 1)
                    if k in (5, 8) and smax:
                        u = at["t", k // 8]
                        w = banks.claim(pe, base, u)
                        if k == 8:
                            pe.wait_ge(s_mz, CB * (n + 2))
                        for c in range(CB):
                            last = pe.transpose(w[:, P * c:P * c + P], mz[:, CB * (k // 8) + c, :], K.ident[:])
                        last.then_inc(banks.full[u[0]], 1)

            turns(pe, body)


def step_of(unit):
    kind, h = unit
    return {"q": 2 * h + 1, "k": 2 * h if h else 7}[kind]


def build(nc, t):
    with ExitStack() as stack:
        K = Kept(nc, stack)
        with ExitStack() as layer0:
            K.CT = layer0.enter_context(nc.sbuf_tensor("CT", [P, G * B + 1, S], F32))
            gb = GroupBuffers(nc, layer0)
            load_phase(nc, K, gb, {"x": t["x"], "ident": t["ident"], "maskq": t["maskq"], "maskk": t["maskk"],
                                   "gw": t["gw0"], "negc": t["negc"], "sel": t["sel"]})
            groups_phase(nc, K, gb, "attn0", True, (D // H) ** -0.5)
            norm_phase(nc, K, {"wo": t["wo0"], "bias": t["bo0"]}, "norm0", "context", ahead=[(gb.gw, t["gw1"])])
            groups_phase(nc, K, gb, "attn1", False, (D // H // 2) ** -0.5)
            route_phase(nc, K, {"wo": t["wo1"], "ob": t["ob1"], "rw": t["rw0"], "rb": t["rb0"],
                                "rank": t["rank0"]}, "route0", E0, True, 0.0, 1e-8)
        with ExitStack() as layer1:
            rw = RowWeights(nc, layer1)
            experts_phase(nc, K, {n: t[n + "_0"] for n in ("w1", "b1", "w2", "b2")}, "moe0", E0,
                          ahead=[(rw.wq, t["wq2"]), (rw.wk, t["wk2"]), (rw.wv, t["wv2"]), (rw.pw, t["pw2"])])
            norm_phase(nc, K, {}, "norm1", "moe")
            rows_phase(nc, K, rw, "attn2", HS ** -0.5)
        norm_phase(nc, K, {"bias": t["pb2"]}, "norm2", "rows")
        route_phase(nc, K, {"rw": t["rw1"], "rb": t["rb1"], "rank": t["rank1"]}, "route1", E1, False,
                    1e-10, 0.0)
        experts_phase(nc, K, {n: t[n + "_1"] for n in ("w1", "b1", "w2", "b2")}, "moe1", E1)
        norm_phase(nc, K, {}, "norm3", "clip", out=t["out"])


def kernel(**inputs):
    import numpy as np
    import concourse.bacc as bacc
    from concourse.bass_utils import run_bass_kernel_spmd

    a = {n: np.asarray(v) for n, v in inputs.items()}
    f32 = np.float32

    def packed(wk, bk, wq, bq, wv, bv, hd, stride):
        gw = np.zeros((P, G, GW), f32)
        for h in range(H):
            g, at = divmod(h, HG)
            for part in range(3):
                c = 32 * at + ONE * part
                gw[:, g, c:c + hd] = wk[:, hd * h:hd * h + hd]
                gw[:, g, P + c:P + c + hd] = wq[:, stride * h:stride * h + hd]
                gw[c:c + hd, g, 4 * P] = bk[hd * h:hd * h + hd]
                gw[c:c + hd, g, 4 * P + 1] = bq[stride * h:stride * h + hd]
            c = 32 * at
            gw[:, g, 2 * P + c:2 * P + c + hd] = wv[:, hd * h:hd * h + hd]
            gw[:, g, 3 * P + c:3 * P + c + hd] = bv[hd * h:hd * h + hd]
            gw[:, g, 3 * P + c + ONE] = 1.0
            gw[c + MROW, g, 4 * P] = 1.0
        return gw

    def rows_of(w, hd):
        wo = np.zeros((P, G, D), f32)
        for h in range(H):
            g, at = divmod(h, HG)
            wo[32 * at:32 * at + hd, g] = w[hd * h:hd * h + hd]
        return wo

    zero = np.zeros(D, f32)
    rows = np.arange(P)
    negc = np.zeros((P, 2), f32)
    negc[rows % 32 // ONE == 1, 0] = -1.0
    negc[rows % 32 // ONE == 2, 1] = -1.0
    later = rows[:, None] < rows[None, :]
    wq, wk, wv = (a[f"L1_attn_W{x}"].transpose(1, 0, 2) for x in "qkv")
    arrays = {
        "x": a["L0_attn_x"],
        "ident": np.eye(P, dtype=f32),
        "maskq": np.where(later, f32(-1e30), f32(0.0)),
        "maskk": np.where(later.T, f32(-1e30), f32(0.0)),
        "negc": negc,
        "sel": (rows[:, None] == rows[None, :] // 32 * 32 + ONE).astype(f32),
        "gw0": packed(a["L0_attn_Wk"], zero, a["L0_attn_Wq"], zero, a["L0_attn_Wv"], zero, D // H, D // H),
        "wo0": rows_of(a["L0_attn_Wo"], D // H),
        "bo0": a["L0_attn_bo"],
        "gw1": packed(a["L0_ffn_k_w"], a["L0_ffn_k_b"], a["L0_ffn_q_w"], a["L0_ffn_q_b"], a["L0_ffn_v_w"],
                      a["L0_ffn_v_b"], D // H // 2, D // H),
        "wo1": rows_of(a["L0_ffn_o_w"], D // H // 2),
        "ob1": a["L0_ffn_o_b"].reshape(D, 1),
        "rw0": a["L0_ffn_router_w"],
        "rb0": a["L0_ffn_router_b"],
        "rank0": np.tile(np.arange(E0, 0, -1, dtype=f32), (P, 1)),
        "wq2": np.concatenate([wq, wq], axis=2),
        "wk2": np.concatenate([wk, wk], axis=2),
        "wv2": wv.reshape(D, H * HS),
        "pw2": a["L1_attn_proj_w"].reshape(D, H // 2, 2 * HS).transpose(2, 1, 0),
        "pb2": a["L1_attn_proj_b"],
        "rw1": a["L1_ffn_gate_w"].T,
        "rb1": np.zeros(E1, f32),
        "rank1": np.tile(np.arange(E1, 0, -1, dtype=f32), (P, 1)),
    }
    for n, layer in enumerate(("L0_ffn", "L1_ffn")):
        arrays[f"w1_{n}"] = a[f"{layer}_w1"]
        arrays[f"b1_{n}"] = a[f"{layer}_b1"].reshape(-1, FC, P).transpose(0, 2, 1)
        arrays[f"w2_{n}"] = a[f"{layer}_w2"]
        arrays[f"b2_{n}"] = a[f"{layer}_b2"]

    nc = bacc.Bacc("TRN2", target_bir_lowering=False, num_devices=1)
    feeds, tensors = {}, {}
    for name, array in arrays.items():
        array = np.ascontiguousarray(array)
        feeds[f"in_{name}"] = array
        tensors[name] = nc.dram_tensor(f"in_{name}", array.shape, mybir.dt.from_np(array.dtype),
                                       kind="ExternalInput").ap()
    tensors["out"] = nc.dram_tensor("out", (B, S, D), F32, kind="ExternalOutput").ap()
    build(nc, tensors)
    result = run_bass_kernel_spmd(nc, [feeds], core_ids=[0])
    return result.results[0]["out"]
```

```python
from contextlib import ExitStack, contextmanager

import concourse.bass as bass
from concourse import mybir

F32 = mybir.dt.float32
F32R = mybir.dt.float32r
BF16 = mybir.dt.bfloat16
ALU = mybir.AluOpType
ACT = mybir.ActivationFunctionType
AX = mybir.AxisListType

P = 128
D = 128
B, S = 2, 1024
NT = B * S
NC = NT // P
H = 16
BANK = 512
NB = NT // BANK
CB = BANK // P
CH = S // P
G = 4
HG = H // G
ONE = 8
MROW = 24
GW = 4 * P + 2
E0, E1 = 8, 14
F = 256
FC = F // P
HS = 64
XP = S // H
NP = NT // XP
EPS = 1e-5


class Phase:

    def __init__(self, nc, tag):
        self.nc, self.tag, self.buffers, self.semaphores = nc, tag, ExitStack(), []

    def sb(self, name, shape, dt=F32):
        return self.buffers.enter_context(self.nc.sbuf_tensor(f"{self.tag}_{name}", shape, dt))

    def sem(self, name):
        self.semaphores.append(self.nc.alloc_semaphore(name=f"{self.tag}_{name}"))
        return self.semaphores[-1]

    @contextmanager
    def block(self):
        with self.buffers:
            with self.nc.Block() as block:
                yield block
            self.nc.clear_and_free_semaphores(self.semaphores)
            self.nc.all_engine_barrier()


class Banks:

    def __init__(self, ph, tensors):
        self.full = [ph.sem(f"bank{i}_full") for i in range(len(tensors))]
        self.free = [ph.sem(f"bank{i}_free") for i in range(len(tensors))]
        self.tensors = tensors

    def claim(self, pe, base, place):
        b, i = place
        if not (isinstance(base[b], int) and base[b] + i == 0):
            pe.wait_ge(self.free[b], base[b] + i)
        return self.tensors[b]

    def filled(self, eng, base, place):
        b, i = place
        eng.wait_ge(self.full[b], base[b] + i + 1)
        return self.tensors[b]

    def all_of(self, eng, base, places, but):
        latest = {}
        for b, i in places:
            latest[b] = max(i, latest.get(b, 0))
        for b, i in latest.items():
            if b != but:
                self.read(eng, base, (b, i))

    def read(self, eng, base, place):
        b, i = place
        eng.wait_ge(self.free[b], base[b] + i + 1)

    def all_read(self, eng, base, first):
        for b, i in enumerate(first):
            if not (isinstance(base[b], int) and base[b] + i == 0):
                eng.wait_ge(self.free[b], base[b] + i)

    def last_read(self, eng, base, first):
        eng.wait_ge(self.free[-1], base[-1] + first[-1])


class Places:

    def __init__(self, turns, banks):
        self.at, self.first, self.total = [], [], [0] * banks
        for units in turns:
            self.first.append(list(self.total))
            self.at.append({})
            skip = 0
            for n, u in enumerate(units):
                skip += u == (("inv", 0) if ("inv", 0) in units else ("t", 1)) and (len(units) - 1) % banks == 0
                b = banks - 1 if u == ("t", 0) else (n + skip) % banks
                self.at[-1][u] = (b, self.total[b])
                self.total[b] += 1

    def turn(self, r):
        return self.at[r], self.first[r]


class Scores:

    def __init__(self, keys, banks):
        self.banks = banks
        self.at = {key: n for n, key in enumerate(keys)}
        self.n = len(keys)

    def bank(self, key):
        return self.at[key] % self.banks

    def through(self, t, key):
        return self.n * t + self.at[key] + 1 + self.banks

    def before(self, t, key):
        n = self.at[key]
        m = n - self.banks
        if m < 0:
            m = max(m for m in range(self.n) if m % self.banks == n % self.banks) - self.n
        return self.n * t + m + 1 + self.banks


WORK = 6
GWB, RWB = 3, 4
NONE = (0,) * WORK


def alternate(n):
    return n % 2, n // 2


def group_units(causal, proj, smax, den):
    u = []
    for k in range(CH + 1):
        if smax and k < CH:
            u += [("max", CH - 1 - k, j, h) for j, h in max_order(causal, k)]
        if k == 2 and proj:
            u += [("k", 0), ("k", 1)]
        if k == 3 and proj:
            u += [("q", 0), ("q", 1)]
        if k == 4 and den:
            u += [("den", 0), ("den", 1)]
        if k == (8 if causal else 6) and smax:
            u += [("v", 0), ("v", 1)]
        if k in (5, 8) and smax:
            u += [("t", int(k == 5))]
    return u


def key_tiles(causal, c):
    return 1 if causal and c < CB else 2


def max_order(causal, k):
    n = key_tiles(causal, CH - 1 - k)
    return [(j, h) for j in range(HG) for h in range(n)] if k else [(j, h) for h in range(n) for j in range(HG)]


def pieces(q0):
    return [(max(q0, a), a + BANK) for a in range(0, S, BANK) if q0 < a + BANK]


def load_phase(nc, K, gb, src):
    ph = Phase(nc, "load")
    mf = [ph.sb(f"maskf{i}", [P, P]) for i in range(2)]
    s_in, s_x, s_b = ph.sem("in"), ph.sem("x"), ph.sem("cast")
    banks = Banks(ph, K.psum[:2])
    X, XT = K.X, K.XT
    xv = src["x"].rearrange("b (c p) d -> p (b c) d", p=P)
    s_w = ph.sem("weights")
    with ph.block() as block:

        @block.gpsimd
        def _(pool):
            pool.memset(gb.kpad[0][:].bitcast(F32), 0.0)

        @block.sync
        def _(sp):
            sp.dma_start(K.ident[:], src["ident"]).then_inc(s_in, 16)
            for n in range(NB):
                sp.dma_start(X[:, CB * n:CB * n + CB, :], xv[:, CB * n:CB * n + CB, :]).then_inc(s_x, 16)
            sp.dma_start(gb.gw[:], src["gw"]).then_inc(s_w, 16)
            sp.dma_start(gb.negc[:], src["negc"]).then_inc(s_w, 16)
            sp.dma_start(gb.sel_f[:], src["sel"]).then_inc(s_w, 16)
            sp.wait_ge(s_w, 48)

        @block.scalar
        def _(act):
            act.dma_start(mf[0][:], src["maskq"]).then_inc(s_b, 16)
            act.dma_start(mf[1][:], src["maskk"]).then_inc(s_b, 16)
            for n in range(NB):
                t = banks.filled(act, NONE, alternate(n))
                act.activation(XT[:, BANK * n:BANK * n + BANK], t[:], ACT.Copy).then_inc(banks.free[n % 2], 1)

        @block.vector
        def _(dve):
            dve.memset(gb.kpad[1][:].bitcast(F32), 0.0)
            dve.memset(gb.mz[:].bitcast(F32), 0.0)
            dve.memset(gb.rr[:].bitcast(F32), 0.0)
            dve.memset(gb.oe[:], 1.0)
            dve.wait_ge(s_b, 32)
            dve.tensor_copy(K.maskq[:], mf[0][:])
            dve.tensor_copy(K.maskk[:], mf[1][:])
            dve.wait_ge(s_in, 16)
            dve.tensor_copy(K.identb[:], K.ident[:])
            dve.tensor_copy(K.identr[:], K.ident[:])
            dve.wait_ge(s_w, 48)
            dve.tensor_copy(gb.sel[:], gb.sel_f[:])

        @block.tensor
        def _(pe):
            pe.wait_ge(s_in, 16)
            for n in range(NB):
                pe.wait_ge(s_x, 16 * NB)
                t = banks.claim(pe, NONE, alternate(n))
                for c in range(CB):
                    last = pe.transpose(t[:, P * c:P * c + P], X[:, CB * n + c, :], K.ident[:])
                last.then_inc(banks.full[n % 2], 1)


def groups_phase(nc, K, gb, tag, causal, scale, ahead=()):
    ph = Phase(nc, tag)
    XT, CT = K.XT, K.CT
    gw, negc, sel, kpad, mz, oe, rr = gb.gw, gb.negc, gb.sel, gb.kpad, gb.mz, gb.oe, gb.rr
    wkq = ph.sb("wkq", [P, 2 * P + 2])
    wv = ph.sb("wv", [P, 2 * P])
    raw = ph.sb("raw", [P, 2, BANK])
    hi = ph.sb("hi", [P, 2, BANK], F32R)
    kc = ph.sb("kc", [P, S], F32R)
    qp = [ph.sb(f"qp{i}", [P, S], F32R) for i in range(2)]
    qa = [ph.sb(f"qa{i}", [P, S], F32R) for i in range(2)]
    v = [ph.sb(f"v{i}", [P, CH, P]) for i in range(2)]
    pr = [[ph.sb(f"p{i}{j}", [P, S]) for j in range(HG)] for i in range(2)]
    mx = ph.sb("mx", [P, 2, HG, 2])
    dn = ph.sb("dn", [P, 32])
    rd = ph.sb("rd", [P, 32])
    rh = ph.sb("rh", [P, 64], F32R)
    credit = ph.sb("credit", [P, 4])

    banks, st_ps = Banks(ph, K.psum[:GWB]), K.psum[GWB:]
    s_alone = ph.sem("alone")
    s_ahead = ph.sem("ahead")
    s_wkq = ph.sem("wkq_staged")
    s_wv = ph.sem("wv_staged")
    s_hi = ph.sem("hi_made")
    s_kc = ph.sem("kc_made")
    s_dn = ph.sem("denominators_spread")
    s_rc = ph.sem("reciprocals")
    s_rh = ph.sem("reciprocals_hi")
    s_rd = ph.sem("reciprocals_split")
    s_rr = ph.sem("reciprocals_back")
    s_qp = ph.sem("qp_made")
    s_kpad = [ph.sem(f"kpad_staged{i}") for i in range(2)]
    s_mz = ph.sem("maxima")
    s_st = ph.sem("scores_t")
    s_p = ph.sem("exp_done")
    s_pv = ph.sem("pv_done")
    s_oe = ph.sem("outputs_evacuated")

    head = Places([group_units(causal, True, False, False), group_units(causal, True, True, False)], GWB)
    pair = Places([group_units(causal, True, True, True)] * B, GWB)
    tail = Places([group_units(causal, False, True, True), group_units(causal, False, False, True),
                   group_units(causal, False, False, True)], GWB)
    NQ = sum(key_tiles(causal, c) == 2 for c in range(CH))

    def q0_of(c):
        return P * c if causal else 0

    def banks_of(c):
        n = len(pieces(q0_of(c)))
        return [(j, i) for i in (1, 0) for j in range(HG)] if c == 0 else \
            [(j, i) for j in range(HG) for i in range(n)]

    scores = Scores([(c, j, i) for c in range(CH) for j, i in banks_of(c)], len(st_ps))

    def last_of(c):
        return (c, *banks_of(c)[-1])

    def turns(eng, body):
        body(-2, -1, 0, *head.turn(0), NONE, False, False, True)
        body(-1, -1, 1, *head.turn(1), NONE, False, True, True)
        with eng.Fori(0, G - 1) as g:
            base = [n + m * g for n, m in zip(head.total, pair.total)]
            for p in range(B):
                body(2 * g + p, g, p, *pair.turn(p), base, True, True, True)
        t, base = B * (G - 1), [n + m * (G - 1) for n, m in zip(head.total, pair.total)]
        body(t, G - 1, 0, *tail.turn(0), base, True, True, False)
        body(t + 1, G - 1, 1, *tail.turn(1), base, True, False, False)
        body(t + 2, G, 0, *tail.turn(2), base, False, False, False)

    with ph.block() as block:

        @block.sync
        def _(sp):
            def body(t, g, p, units, first, base, st, smax, proj):
                if ("den", 0) in units:
                    sp.wait_ge(s_oe, t + 1)
                    sp.sem_inc(s_alone, 1)
                    sp.dma_start(dn[:], oe[ONE::32, :].rearrange("j (a f) -> j a f", f=32)).then_inc(s_dn, 16)
                    sp.wait_ge(s_rd, t + 1)
                    sp.sem_inc(s_alone, 1)
                    for i in range(2):
                        sp.dma_start(rr[ONE + i::32, :].bitcast(F32).rearrange("j (a f) -> j a f", f=32),
                                     rh[:, 32 * i:32 * i + 32].bitcast(F32)).then_inc(s_rr, 16)
                if proj:
                    for n in range(2):
                        sp.wait_ge(s_kc, 2 * (t + 2) + n + 1)
                        sp.sem_inc(s_alone, 1)
                        if st:
                            sp.wait_ge(s_p, scores.through(t, last_of(CB * n + CB - 1)))
                            sp.sem_inc(s_alone, 1)
                        for j in range(HG):
                            r, a = slice(32 * j, 32 * j + 32), slice(BANK * n, BANK * n + BANK)
                            sp.dma_start(kpad[p][r, j, a].bitcast(F32), kc[r, a].bitcast(F32))\
                              .then_inc(s_kpad[n], 16)

            for dst, tensor in ahead:
                sp.dma_start(dst, tensor).then_inc(s_ahead, 16)
            turns(sp, body)
            if ahead:
                sp.wait_ge(s_ahead, 16 * len(ahead))

        @block.gpsimd
        def _(pool):
            pool.memset(credit[:, 0:1], 0.0).then_inc(s_p, len(st_ps))
            pool.memset(credit[:, 2:3], 0.0).then_inc(s_oe, 1)
            pool.memset(credit[:, 1:2], 0.0).then_inc(s_pv, 2)

            def body(t, g, p, units, first, base, st, smax, proj):
                if st and (proj or smax):
                    banks.all_read(pool, base, first)
                pool.sem_inc(s_alone, 1)
                if proj and p == 0:
                    pool.tensor_copy(wkq[:, 0:2 * P], gw[:, g + 1, 0:2 * P])
                    pool.tensor_copy(wkq[:, 2 * P:], gw[:, g + 1, 4 * P:]).then_inc(s_wkq, 1)
                if smax and p == 1:
                    pool.tensor_copy(wv[:], gw[:, g + 1, 2 * P:4 * P]).then_inc(s_wv, 1)
                if proj:
                    for w, (dst, s_dst, what) in enumerate(((kc, s_kc, 0), (kc, s_kc, 0),
                                                            (qp[p], s_qp, 1), (qp[p], s_qp, 1))):
                        n = w % 2
                        banks.read(pool, base, units["kq"[what], n])
                        if w >= 2:
                            pool.wait_ge(s_kc, 2 * (t + 2) + n + 1)
                        elif isinstance(t, int) and t == -2:
                            pass
                        else:
                            pool.wait_ge(s_qp, 2 * (t + 2) + n - 1)
                        pool.sem_inc(s_alone, 1)
                        pool.tensor_scalar(hi[:, n, :], raw[:, n, :], negc[:, what:what + 1], None,
                                           ALU.mult).then_inc(s_hi, 1)
                        if w < 2 and smax:
                            pool.wait_ge(s_kpad[n], 16 * HG * (t + 2))
                        pool.wait_ge(s_hi, 4 * (t + 2) + w + 1)
                        pool.tensor_tensor(dst[:, BANK * n:BANK * n + BANK], raw[:, n, :],
                                           hi[:, n, :].bitcast(F32), ALU.add).then_inc(s_dst, 1)

            turns(pool, body)

        @block.scalar
        def _(act):
            def body(t, g, p, units, first, base, st, smax, proj):
                for k in range(CH):
                    if st:
                        act.wait_ge(s_pv, CH * t + k + 1)
                        for j, i in banks_of(k):
                            a, b = pieces(q0_of(k))[i]
                            act.wait_ge(s_st, scores.n * t + scores.at[k, j, i] + 1)
                            act.activation(pr[k % 2][j][:, a:b], st_ps[scores.bank((k, j, i))][:, 0:b - a],
                                           ACT.Exp, scale=scale).then_inc(s_p, 1)
                    if k in (2, 3) and proj:
                        for h in range(2):
                            n = units["kq"[k - 2], h]
                            w = banks.filled(act, base, n)
                            if k == 2 and smax:
                                act.wait_ge(s_qp, 2 * (t + 1) + h + 1)
                            if k == 3:
                                act.wait_ge(s_kc, 2 * (t + 2) + h + 1)
                            act.activation(raw[:, h, :], w[:], ACT.Identity,
                                           bias=wkq[:, 2 * P + k - 2:2 * P + k - 1]).then_inc(banks.free[n[0]], 1)
                if st:
                    act.wait_ge(s_pv, CH * t + CH + 2)
                    for h in range(2):
                        banks.read(act, base, units["den", h])
                    act.activation(oe[:], K.o_ps[:], ACT.Copy).then_inc(s_oe, 1)

            turns(act, body)

        @block.vector
        def _(dve):
            def body(t, g, p, units, first, base, st, smax, proj):
                for k in range(CH + 1):
                    c = CH - 1 - k
                    if smax and k < CH:
                        tiles = key_tiles(causal, c)
                        for j, h in max_order(causal, k):
                            n = units["max", c, j, h]
                            w = banks.filled(dve, base, n)
                            cols = min(BANK, P * (c + 1) - BANK * h) if causal else BANK
                            dst = mx[:, c % 2, j, h:h + 1] if tiles == 2 else \
                                mz[:, c, 32 * j + MROW:32 * j + MROW + 1]
                            dve.reduce_max(dst, w[:, 0:cols], AX.X, negate=True)\
                               .then_inc(banks.free[n[0]], 1)
                        if tiles == 2:
                            banks.read(dve, base, units["max", c, HG - 1, 0])
                            banks.read(dve, base, n)
                            dve.tensor_tensor(mz[:, c, MROW::32], mx[:, c % 2, :, 0], mx[:, c % 2, :, 1],
                                              ALU.min).then_inc(s_mz, 1)
                    if k == 1 and ("den", 0) in units:
                        dve.wait_ge(s_dn, 16 * (t + 1))
                        dve.reciprocal(rd[:], dn[:]).then_inc(s_rc, 1)
                        dve.wait_ge(s_rc, t + 1)
                        dve.tensor_copy(rh[:, 0:32], rd[:]).then_inc(s_rh, 1)
                        dve.wait_ge(s_rh, t + 1)
                        dve.tensor_tensor(rh[:, 32:64], rd[:], rh[:, 0:32].bitcast(F32), ALU.subtract)\
                           .then_inc(s_rd, 1)
                    if k == 4 and ("den", 0) in units:
                        for h in range(2):
                            n = units["den", h]
                            w = banks.filled(dve, base, n)
                            dve.tensor_tensor(CT[:, t, BANK * h:BANK * h + BANK], oe[:, BANK * h:BANK * h + BANK],
                                              w[:], ALU.mult).then_inc(banks.free[n[0]], 1)
                    if k == (8 if causal else 6) and smax:
                        for h in range(2):
                            n = units["v", h]
                            w = banks.filled(dve, base, n)
                            dve.tensor_tensor(v[1 - p][:, CB * h:CB * h + CB, :],
                                              w[:].rearrange("p (c d) -> p c d", d=P),
                                              wv[:, P:].unsqueeze(1).broadcast_to([P, CB, P]),
                                              ALU.add).then_inc(banks.free[n[0]], 1)
                    if k in (5, 8) and smax:
                        i = int(k == 5)
                        n = units["t", i]
                        w = banks.filled(dve, base, n)
                        a = slice(BANK * i, BANK * i + BANK)
                        dve.tensor_tensor(qa[1 - p][:, a], qp[1 - p][:, a].bitcast(F32), w[:],
                                          ALU.add).then_inc(banks.free[n[0]], 1)

            turns(dve, body)

        @block.tensor
        def _(pe):
            def weigh(k, h, t, p):
                a, b = max(q0_of(k), BANK * h), BANK * h + BANK
                if a >= b:
                    return None
                last_k = CB * h + CB - 1 if causal else CH - 1
                for j in range(HG):
                    r = slice(32 * j, 32 * j + 32)
                    last = pe.matmul(K.o_ps[r, a:b], v[p][:, k, r], pr[k % 2][j][:, a:b],
                                     start=(k == 0), stop=(k == last_k))
                return last

            def score(k, j, h, t, p, base, first):
                if (k, j, h) == (0, 0, 0):
                    banks.last_read(pe, base, first)
                a, b = pieces(q0_of(k))[h]
                pe.wait_ge(s_p, scores.before(t, (k, j, h)))
                bank = st_ps[scores.bank((k, j, h))]
                diag = causal and a == q0_of(k)
                last = pe.matmul(bank[:, 0:b - a], kpad[p][:, j, P * k:P * k + P], qa[p][:, a:b],
                                 start=True, stop=not diag)
                if diag:
                    last = pe.matmul(bank[:, 0:P], K.identb[:], K.maskk[:], start=False, stop=True)
                last.then_inc(s_st, 1)

            def body(t, g, p, units, first, base, st, smax, proj):
                if not (st and smax):
                    banks.all_read(pe, base, first)
                for k in range(CH + 1):
                    if k == 0 and smax:
                        pe.wait_ge(s_qp, 2 * (t + 2))
                    maxima = max_order(causal, k) if smax and k < CH else []
                    rounds = 2 if len(maxima) == 2 * HG else 1
                    for y in range(HG):
                        for x in range(2):
                            if x < rounds and maxima:
                                j, h = maxima[rounds * y + x]
                                if k == 0 and j == 0:
                                    pe.wait_ge(s_kpad[h], 16 * HG * (t + 2))
                                c = CH - 1 - k
                                n = units["max", c, j, h]
                                w = banks.claim(pe, base, n)
                                cols = min(BANK, P * (c + 1) - BANK * h) if causal else BANK
                                diag = causal and BANK * h + cols == P * (c + 1)
                                last = pe.matmul(w[:, 0:cols], qp[1 - p][:, P * c:P * c + P],
                                                 kpad[1 - p][:, j, BANK * h:BANK * h + cols],
                                                 start=True, stop=not diag)
                                if diag:
                                    last = pe.matmul(w[:, cols - P:cols], K.identb[:], K.maskq[:],
                                                     start=False, stop=True)
                                last.then_inc(banks.full[n[0]], 1)
                            if st and k < CH and len(banks_of(k)) == 2 * HG:
                                score(k, *banks_of(k)[2 * y + x], t, p, base, first)
                            elif st and k < CH and x == 0:
                                score(k, *banks_of(k)[y], t, p, base, first)
                        if st and 1 <= k < CH + (not causal) and y % 2 == 1:
                            if y == 1:
                                pe.wait_ge(s_p, scores.through(t, last_of(k - 1)))
                                if k == 1:
                                    pe.wait_ge(s_oe, t + 1)
                            if y == 1:
                                weigh(k - 1, 0, t, p)
                            elif k < CH and not (proj and k in (2, 3)):
                                weigh(k - 1, 1, t, p).then_inc(s_pv, 1)
                    if k == 4 and ("den", 0) in units:
                        pe.wait_ge(s_rr, 32 * (t + 1))
                        for h in range(2):
                            n = units["den", h]
                            w = banks.claim(pe, base, n)
                            pe.matmul(w[:], sel[:], rr[:, BANK * h:BANK * h + BANK],
                                      start=True, stop=True).then_inc(banks.full[n[0]], 1)
                    if k in (2, 3) and proj:
                        pe.wait_ge(s_wkq, g + 2)
                        for h in range(2):
                            n = units["kq"[k - 2], h]
                            w = banks.claim(pe, base, n)
                            pe.matmul(w[:], wkq[:, P * (k - 2):P * (k - 1)],
                                      XT[:, p * S + BANK * h:p * S + BANK * h + BANK],
                                      start=True, stop=True).then_inc(banks.full[n[0]], 1)
                        if st:
                            weigh(k - 1, 1, t, p).then_inc(s_pv, 1)
                    if k == (8 if causal else 6) and smax:
                        pe.wait_ge(s_wv, g + 1 + p)
                        for h in range(2):
                            n = units["v", h]
                            w = banks.claim(pe, base, n)
                            for c in range(CB):
                                a = (1 - p) * S + P * (CB * h + c)
                                last = pe.matmul(w[:, P * c:P * c + P], XT[:, a:a + P], wv[:, 0:P],
                                                 start=True, stop=True)
                            last.then_inc(banks.full[n[0]], 1)
                    if k in (5, 8) and smax:
                        i = int(k == 5)
                        n = units["t", i]
                        if not i and units["t", 1][0] != n[0]:
                            banks.read(pe, base, units["t", 1])
                        w = banks.claim(pe, base, n)
                        ready = sum(key_tiles(causal, c) == 2 for c in range(CB * i, CH))
                        pe.wait_ge(s_mz, NQ * (t + 1) + ready)
                        if key_tiles(causal, CB * i) == 1:
                            banks.all_of(pe, base, [units["max", CB * i, j, 0] for j in range(HG)], n[0])
                        for c in range(CB):
                            last = pe.matmul(w[:, P * c:P * c + P], mz[:, CB * i + c, :], K.identr[:],
                                             start=True, stop=True)
                        last.then_inc(banks.full[n[0]], 1)
                if st:
                    if causal:
                        pe.wait_ge(s_p, scores.through(t, last_of(CH - 1)))
                    weigh(CH - 1, 1, t, p).then_inc(s_pv, 1)

            turns(pe, body)


class Kept:

    def __init__(self, nc, stack):
        def sb(name, shape, dt=F32):
            return stack.enter_context(nc.sbuf_tensor(name, shape, dt))

        self.X = sb("X", [P, NC, D])
        self.XT = sb("XT", [D, NT])
        self.CT = None
        self.xh = sb("xh", [D, NT], F32R)
        self.xl = sb("xl", [D, NT], F32R)
        self.comb = sb("comb", [P, E1, NC])
        self.acc_slots = sb("acc", [P, NC + 1, D])
        self.acc = self.acc_slots[:, 1:, :]
        self.wo = [self.acc_slots[:, 1 + G * i:1 + G * i + G, :] for i in range(2)]
        self.bo = self.acc_slots[:, 1 + 2 * G, :]
        self.ob = sb("ob", [P, 1])
        self.pb = sb("pb", [P, D])
        self.router = [[sb(f"router{i}{x}", [P, e]) for x in "wbr"] for i, e in enumerate((E0, E1))]
        self.expert = [sb("first_w1", [D, F]), sb("first_w2", [P, FC, D]), sb("first_b1", [P, FC]),
                       sb("first_b2", [P, D])]
        self.ident = sb("ident_sb", [P, P])
        self.identr = sb("identr", [P, P], F32R)
        self.identb = sb("identb", [P, P], BF16)
        self.maskq = sb("maskq_sb", [P, P], BF16)
        self.maskk = sb("maskk_sb", [P, P], BF16)
        self.psum = [stack.enter_context(nc.psum_tensor(f"bank{i}", [P, BANK], F32)) for i in range(WORK)]
        self.o_ps = stack.enter_context(nc.psum_tensor("o_ps", [P, S], F32))


class GroupBuffers:

    def __init__(self, nc, stack):
        def sb(name, shape, dt=F32):
            return stack.enter_context(nc.sbuf_tensor(name, shape, dt))

        self.gw = sb("gw", [P, G, GW])
        self.negc = sb("negc_sb", [P, 2])
        self.sel_f = sb("sel_f", [P, P])
        self.sel = sb("sel_sb", [P, P], F32R)
        self.kpad = [sb(f"kpad{i}", [P, HG, S], F32R) for i in range(2)]
        self.mz = sb("mz", [P, CH, P], F32R)
        self.oe = sb("oe", [P, S])
        self.rr = sb("rr", [P, S], F32R)


def norm_phase(nc, K, tag, add, out=None, split=False, router=None, ahead=()):
    ph = Phase(nc, tag)
    X, XT, CT = K.X, K.XT, K.CT
    bias, wo = K.bo if add == "context" else K.pb[:], K.wo[0]
    z = ph.sb("z", [P, NB, CB, D])
    stats = ph.sb("stats", [P, 2, CB, 6])
    mv = ph.sb("mv", [P, 2, CB, 2])
    var = ph.sb("var", [P, 2, CB])
    std = ph.sb("std", [P, 2, CB])
    rs = ph.sb("rs", [P, 2, CB])
    shift = ph.sb("shift", [P, 2, CB])
    banks = Banks(ph, K.psum[:2])
    s_z, s_rs = ph.sem("first_sum"), ph.sem("scale_and_shift")
    s_v, s_var, s_std, s_x, s_out = (ph.sem(x) for x in ("step", "variance", "std", "x", "out"))
    s_y = ph.sem("projected")
    s_xt, s_lo, s_lg = ph.sem("transposed"), ph.sem("lo"), ph.sem("logits")
    s_ahead = ph.sem("ahead")
    s_yr = ph.sem("projection_read")

    with ph.block() as block:

        @block.sync
        def _(sp):
            for dst, tensor in ahead:
                sp.dma_start(dst, tensor).then_inc(s_ahead, 16)
            if out is not None:
                ov = out.rearrange("b (c p) d -> p (b c) d", p=P)
                for n in range(NB):
                    sp.wait_ge(s_x, n + 1)
                    sp.dma_start(ov[:, CB * n:CB * n + CB, :], X[:, CB * n:CB * n + CB, :]).then_inc(s_out, 16)
                sp.wait_ge(s_out, 16 * NB)
            if ahead:
                sp.wait_ge(s_ahead, 16 * len(ahead))

        @block.gpsimd
        def _(pool):
            def lo(pool, n):
                a = slice(BANK * n, BANK * n + BANK)
                banks.read(pool, NONE, alternate(n))
                pool.tensor_tensor(K.xl[:, a], XT[:, a], K.xh[:, a].bitcast(F32), ALU.subtract).then_inc(s_lo, 1)

            for n in range(NB):
                xs, zs = X[:, CB * n:CB * n + CB, :], z[:, n]
                other = {"moe": xs, "clip": K.acc[:, CB * n:CB * n + CB, :]}.get(
                    add, bias.unsqueeze(1).broadcast_to([P, CB, D]))
                pool.tensor_tensor(zs, xs, other, ALU.add).then_inc(s_z, 1)
            if split:
                for n in range(NB):
                    lo(pool, n)

        @block.scalar
        def _(act):
            def evacuate(n):
                w = banks.filled(act, NONE, alternate(n))
                a = slice(BANK * n, BANK * n + BANK)
                last = act.activation(XT[:, a], w[:], ACT.Copy)
                if split:
                    last.then_inc(s_xt, 1)
                    last = act.activation(K.xh[:, a], w[:], ACT.Copy)
                last.then_inc(banks.free[n % 2], 1)

            for n in range(NB):
                act.wait_ge(s_var, n + 1)
                act.activation(std[:, n % 2, :], var[:, n % 2, :], ACT.Sqrt).then_inc(s_std, 1)
                if out is None and n >= 2:
                    evacuate(n - 2)
                act.wait_ge(s_rs, n + 1)
                for c in range(CB):
                    last = act.activation(X[:, CB * n + c, :], z[:, n, c, :], ACT.Identity,
                                          bias=shift[:, n % 2, c:c + 1], scale=rs[:, n % 2, c:c + 1])
                last.then_inc(s_x, 1)
            if out is None:
                evacuate(NB - 2)
                evacuate(NB - 1)

        @block.vector
        def _(dve):
            steps = [0]

            def then(ins):
                steps[0] += 1
                ins.then_inc(s_v, 1)
                dve.wait_ge(s_v, steps[0])

            for n in range(NB):
                xs, zs = X[:, CB * n:CB * n + CB, :], z[:, n]
                acc = K.acc[:, CB * n:CB * n + CB, :]
                dve.wait_ge(s_z, n + 1)
                if add == "context":
                    dve.wait_ge(s_y, n + 1)
                    w = K.psum[2 + n % 2][:, 0:BANK].rearrange("p (c d) -> p c d", d=D)
                    dve.tensor_tensor(zs, w, zs, ALU.add).then_inc(s_yr, 1)
                    dve.wait_ge(s_yr, n + 1)
                elif add == "moe":
                    then(dve.scalar_tensor_tensor(zs, acc, 0.3, zs, ALU.mult, ALU.add))
                elif add == "rows":
                    then(dve.tensor_tensor(zs, acc, zs, ALU.add))
                else:
                    then(dve.tensor_scalar(zs, zs, -100.0, 100.0, ALU.max, ALU.min))
                    then(dve.tensor_tensor(zs, zs, xs, ALU.add))
                for c in range(CB):
                    last = dve.bn_stats(stats[:, n % 2, c, :], z[:, n, c, :])
                then(last)
                for c in range(CB):
                    last = dve.bn_aggr(mv[:, n % 2, c, :], stats[:, n % 2, c, :])
                then(last)
                dve.tensor_scalar(var[:, n % 2, :], mv[:, n % 2, :, 1], EPS, None, ALU.add).then_inc(s_var, 1)
                dve.wait_ge(s_std, n + 1)
                then(dve.reciprocal(rs[:, n % 2, :], std[:, n % 2, :]))
                dve.scalar_tensor_tensor(shift[:, n % 2, :], mv[:, n % 2, :, 0], -1.0, rs[:, n % 2, :],
                                         ALU.mult, ALU.mult).then_inc(s_rs, 1)

        @block.tensor
        def _(pe):
            def project(n):
                if n >= 2:
                    pe.wait_ge(s_yr, n - 1)
                for c in range(CB):
                    b, a = divmod(P * (CB * n + c), S)
                    for g in range(G):
                        last = pe.matmul(K.psum[2 + n % 2][:, P * c:P * c + P], CT[:, B * g + b + 1, a:a + P],
                                         wo[:, g, :], start=(g == 0), stop=(g == G - 1))
                last.then_inc(s_y, 1)

            def logits(n):
                pe.wait_ge(s_xt, n + 1)
                for c in range(CB * n, CB * n + CB):
                    last = pe.matmul(K.o_ps[:, E1 * c:E1 * c + E1], XT[:, P * c:P * c + P], router[:],
                                     start=True, stop=True)
                return last

            if add == "context":
                project(0)
            for n in range(NB):
                if add == "context" and n + 1 < NB:
                    project(n + 1)
                if out is None:
                    pe.wait_ge(s_x, n + 1)
                    w = banks.claim(pe, NONE, alternate(n))
                    for c in range(CB):
                        last = pe.transpose(w[:, P * c:P * c + P], X[:, CB * n + c, :], K.ident[:])
                    last.then_inc(banks.full[n % 2], 1)
                if router is not None and n:
                    logits(n - 1)
            if router is not None:
                logits(NB - 1).then_inc(s_lg, 1)


def route_phase(nc, K, tag, rw):
    ph = Phase(nc, tag)
    E = E0
    CT = K.CT
    wo, ob = K.wo[1], K.ob
    MT = ph.sb("MT", [D, NT])
    s_lg = ph.sem("logits")
    s_lo = ph.sem("lo")
    s_mt = ph.sem("mt")
    banks = Banks(ph, K.psum[:2])

    with ph.block() as block:

        @block.scalar
        def _(act):
            for n in range(NB):
                a = slice(BANK * n, BANK * n + BANK)
                w = banks.filled(act, NONE, alternate(n))
                act.activation(MT[:, a], w[:], ACT.Identity, bias=ob[:]).then_inc(s_mt, 1)
                act.activation(K.xh[:, a], w[:], ACT.Identity, bias=ob[:]).then_inc(banks.free[n % 2], 1)

        @block.gpsimd
        def _(pool):
            for n in range(NB):
                a = slice(BANK * n, BANK * n + BANK)
                banks.read(pool, NONE, alternate(n))
                pool.tensor_tensor(K.xl[:, a], MT[:, a], K.xh[:, a].bitcast(F32), ALU.subtract).then_inc(s_lo, 1)

        @block.tensor
        def _(pe):
            def logits(n):
                pe.wait_ge(s_mt, n + 1)
                for c in range(CB * n, CB * n + CB):
                    last = pe.matmul(K.o_ps[:, E * c:E * c + E], MT[:, P * c:P * c + P], rw[:], start=True, stop=True)
                return last

            for n in range(NB):
                w = banks.claim(pe, NONE, alternate(n))
                b, a = divmod(BANK * n, S)
                for g in range(G):
                    last = pe.matmul(w[:], wo[:, g, :], CT[:, B * g + b + 1, a:a + BANK],
                                     start=(g == 0), stop=(g == G - 1))
                last.then_inc(banks.full[n % 2], 1)
                if n:
                    logits(n - 1)
            logits(NB - 1).then_inc(s_lg, 1)


def experts_phase(nc, K, src, tag, weights, experts, floor, plus, ahead=()):
    ph = Phase(nc, tag)
    E = experts
    w1 = [K.expert[0], ph.sb("w1", [D, F])]
    w2 = [K.expert[1], ph.sb("w2", [P, FC, D])]
    b1 = [K.expert[2], ph.sb("b1", [P, FC])]
    b2 = [K.expert[3], ph.sb("b2", [P, D])]
    w1h = [ph.sb(f"w1h{i}", [D, F], F32R) for i in range(2)]
    w1l = [ph.sb(f"w1l{i}", [D, F], F32R) for i in range(2)]
    hid = [ph.sb(f"hid{i}", [P, FC, BANK]) for i in range(2)]
    y = [ph.sb(f"y{i}", [P, CB, D]) for i in range(2)]
    credit = ph.sb("credit", [P, 4])
    rb, rank = weights[1:]
    lg = ph.sb("lg", [P, NC, E])
    pb = ph.sb("probs", [P, NC, E])
    eq = ph.sb("eq", [P, NC, E])
    one = ph.sb("one", [P, 2, NC, E])
    m = ph.sb("m", [P, 8, NC])
    s_v, s_e, s_s = (ph.sem(x) for x in ("step", "shifted", "exp"))
    s_w = [ph.sem(f"weights{i}") for i in range(2)]
    s_alone = ph.sem("alone")
    s_ahead = ph.sem("ahead")
    s_wh, s_ws = ph.sem("w1_hi"), ph.sem("w1_split")
    s_up, s_g, s_dn, s_y, s_yc, s_a = (ph.sem(x) for x in ("up", "gelu", "down", "biased", "weighted", "added"))

    def over(x):
        return x.unsqueeze(2).broadcast_to([P, NC, E])

    with ph.block() as block:

        def pairs(eng, body):
            with eng.Fori(0, E // 2 - 1) as q:
                for p in range(2):
                    body(2 * q + p, q, p)
            for p in range(2):
                body(E - 2 + p, E // 2 - 1, p)

        @block.sync
        def _(sp):
            def load(e, p):
                sp.wait_ge(s_yc, NB * e + 1)
                sp.sem_inc(s_alone, 1)
                sp.dma_start(w1[p][:], src["w1"][e]).then_inc(s_w[p], 16)
                sp.dma_start(w2[p][:], src["w2"][e].rearrange("(c p) d -> p c d", p=P))\
                  .then_inc(s_w[p], 16)
                sp.dma_start(b1[p][:], src["b1"][e]).then_inc(s_w[p], 16)
                sp.dma_start(b2[p][:], src["b2"][e].partition_broadcast(P))\
                  .then_inc(s_w[p], 16)

            for dst, tensor in ahead:
                sp.dma_start(dst, tensor).then_inc(s_ahead, 16)
            with sp.Fori(0, E // 2 - 1) as q:
                load(2 * q + 1, 1)
                load(2 * q + 2, 0)
            load(E - 1, 1)
            if ahead:
                sp.wait_ge(s_ahead, 16 * len(ahead))

        @block.gpsimd
        def _(pool):
            pool.memset(credit[:, 3:4], 0.0).then_inc(s_w[0], 64)
            pool.memset(credit[:, 0:1], 0.0).then_inc(s_g, 4)
            pool.memset(credit[:, 1:2], 0.0).then_inc(s_dn, 2)
            pool.memset(credit[:, 2:3], 0.0).then_inc(s_yc, NB + 1)
            pool.memset(K.acc, 0.0).then_inc(s_a, 2)

            def body(e, q, p):
                for n in range(NB):
                    m = NB * e + n
                    a = slice(CB * n, CB * n + CB)
                    pool.wait_ge(s_yc, m + 2 + NB)
                    pool.wait_ge(s_a, 2 + m)
                    pool.tensor_tensor(K.acc[:, a, :], K.acc[:, a, :], y[n % 2][:], ALU.add).then_inc(s_a, 1)

            pairs(pool, body)

        @block.scalar
        def _(act):
            act.wait_ge(s_e, 1)
            act.activation(pb[:], lg[:], ACT.Exp).then_inc(s_s, 1)

            def body(e, q, p):
                act.wait_ge(s_w[p], 64 * (q + 1))
                for n in range(NB):
                    m = NB * e + n
                    act.wait_ge(s_dn, m + 1)
                    for f in range(FC):
                        act.wait_ge(s_up, FC * m + f + 1)
                        act.activation(hid[n % 2][:, f, :], K.psum[FC * (n % 2) + f][:],
                                       ACT.Gelu, bias=b1[p][:, f:f + 1]).then_inc(s_g, 1)

            pairs(act, body)

        @block.vector
        def _(dve):
            steps = [0]

            def then(ins):
                steps[0] += 1
                ins.then_inc(s_v, 1)
                dve.wait_ge(s_v, steps[0])

            def split(e, q, p):
                dve.wait_ge(s_w[p], 64 * (q + 1))
                dve.tensor_copy(w1h[p][:], w1[p][:]).then_inc(s_wh, 1)
                dve.wait_ge(s_wh, e + 1)
                dve.tensor_tensor(w1l[p][:], w1[p][:], w1h[p][:].bitcast(F32), ALU.subtract).then_inc(s_ws, 1)

            def body(e, q, p):
                for n in range(NB):
                    m = NB * e + n
                    dve.wait_ge(s_dn, m + 3)
                    dve.wait_ge(s_a, m + 1)
                    dve.tensor_tensor(y[n % 2][:], K.o_ps[:, BANK * (n % 2):BANK * (n % 2) + BANK]
                                      .rearrange("p (c d) -> p c d", d=D),
                                      b2[p][:].unsqueeze(1).broadcast_to([P, CB, D]), ALU.add).then_inc(s_y, 1)
                    dve.wait_ge(s_y, m + 1)
                    dve.tensor_tensor(y[n % 2][:], y[n % 2][:],
                                      K.comb[:, e, CB * n:CB * n + CB].unsqueeze(2).broadcast_to([P, CB, D]),
                                      ALU.mult).then_inc(s_yc, 1)
                    if n == 1 and not (isinstance(e, int) and e == E - 1):
                        split(e + 1, q + p, 1 - p)

            w = K.o_ps[:, 0:NC * E].rearrange("p (c e) -> p c e", e=E)
            then(dve.tensor_tensor(lg[:], w, rb[:].unsqueeze(1).broadcast_to([P, NC, E]), ALU.add))
            then(dve.reduce_max(m[:, 0, :], lg[:], AX.X))
            dve.tensor_tensor(lg[:], lg[:], over(m[:, 0, :]), ALU.subtract).then_inc(s_e, 1)
            split(0, 0, 0)
            dve.wait_ge(s_s, 1)
            then(dve.reduce_sum(m[:, 1, :], pb[:], AX.X))
            then(dve.reciprocal(m[:, 2, :], m[:, 1, :]))
            then(dve.tensor_tensor(pb[:], pb[:], over(m[:, 2, :]), ALU.mult))
            for i in range(2):
                then(dve.reduce_max(m[:, 3 + i, :], pb[:], AX.X))
                then(dve.tensor_tensor(eq[:], pb[:], over(m[:, 3 + i, :]), ALU.is_equal))
                then(dve.tensor_tensor(eq[:], eq[:], rank[:].unsqueeze(1).broadcast_to([P, NC, E]), ALU.mult))
                then(dve.reduce_max(m[:, 5, :], eq[:], AX.X))
                then(dve.tensor_tensor(one[:, i], eq[:], over(m[:, 5, :]), ALU.is_equal))
                if i == 0:
                    then(dve.scalar_tensor_tensor(pb[:], one[:, 0], -4.0, pb[:], ALU.mult, ALU.add))
            then(dve.tensor_tensor(m[:, 6, :], m[:, 3, :], m[:, 4, :], ALU.add))
            then(dve.tensor_scalar(m[:, 6, :], m[:, 6, :], plus, floor, ALU.add, ALU.max))
            then(dve.reciprocal(m[:, 7, :], m[:, 6, :]))
            for i in range(2):
                then(dve.tensor_tensor(m[:, 3 + i, :], m[:, 3 + i, :], m[:, 7, :], ALU.mult))
                then(dve.tensor_tensor(one[:, i], one[:, i], over(m[:, 3 + i, :]), ALU.mult))
            then(dve.tensor_tensor(K.comb[:, 0:E, :].rearrange("p e c -> p c e"), one[:, 0], one[:, 1], ALU.add))
            pairs(dve, body)

        @block.tensor
        def _(pe):
            def up(e, p, n):
                m = NB * e + n
                for f in range(FC):
                    pe.wait_ge(s_g, FC * m + f + 1)
                    t = K.psum[FC * (n % 2) + f][:]
                    a, r = slice(P * f, P * f + P), slice(BANK * n, BANK * n + BANK)
                    pe.matmul(t, w1h[p][:, a], K.xh[:, r], start=True, stop=False)
                    pe.matmul(t, w1h[p][:, a], K.xl[:, r], start=False, stop=False)
                    pe.matmul(t, w1l[p][:, a], K.xh[:, r], start=False, stop=True).then_inc(s_up, 1)

            def down(e, p, n, m):
                pe.wait_ge(s_g, FC * m + FC + 4)
                for c in range(CB):
                    for f in range(FC):
                        a = BANK * (n % 2) + P * c
                        last = pe.matmul(K.o_ps[:, a:a + P], hid[n % 2][:, f, P * c:P * c + P], w2[p][:, f, :],
                                         start=(f == 0), stop=(f == FC - 1))
                last.then_inc(s_dn, 1)

            def body(e, q, p):
                pe.wait_ge(s_ws, e + 1)
                for n in range(NB):
                    up(e, p, n)
                    if n:
                        pe.wait_ge(s_yc, NB * e + n - 1 + NB)
                        down(e, p, n - 1, NB * e + n - 1)
                pe.wait_ge(s_yc, NB * e + NB - 1 + NB)
                down(e, p, NB - 1, NB * e + NB - 1)

            pe.wait_ge(s_v, 1)
            pairs(pe, body)


ROW_PROJECTIONS = {0: ("q", 0), 1: ("q", 1), 2: ("k", 0), 3: ("k", 1), 5: ("v", 0), 7: ("v", 1)}


def row_units(proj, smax, st, den, out):
    u = []
    for k in range(CH + 1):
        if smax and k < CH:
            u += [("max", CH - 1 - k, h) for h in range(key_tiles(True, CH - 1 - k))]
        if proj and k in ROW_PROJECTIONS:
            u += [ROW_PROJECTIONS[k]]
        if k == 0 and den:
            u += [("den", 0)]
        if k == 6 and den:
            u += [("inv", 0)]
        if k == 8 and out:
            u += [("out", 0)]
        if k in (5, 8) and smax:
            u += [("t", int(k == 5))]
    return u


class RowWeights:
    def __init__(self, nc, stack):
        def sb(name, shape):
            return stack.enter_context(nc.sbuf_tensor(name, shape, F32))

        self.wq = sb("wq", [D, H * HS])
        self.wk = sb("wk", [D, H * HS])
        self.wv = sb("wv", [D, H * HS])
        self.pw = sb("pw", [P, H // 2, D])
        self.sel_f = sb("sel2", [P, P])


def rows_phase(nc, K, rw, tag, scale):
    ph = Phase(nc, tag)
    XT, acc = K.XT, K.acc_slots
    wq, wk, wv, pw = rw.wq, rw.wk, rw.wv, rw.pw
    xt = [ph.sb(f"xt{i}", [D, P]) for i in range(2)]
    qa = [ph.sb(f"qa{i}", [P, 2 * S], F32R) for i in range(2)]
    qb = [ph.sb(f"qb{i}", [P, 2 * S], F32R) for i in range(2)]
    ka = [ph.sb(f"ka{i}", [P, 2 * S], F32R) for i in range(2)]
    kb = [ph.sb(f"kb{i}", [P, 2 * S], F32R) for i in range(2)]
    vs = ph.sb("vs", [P, H * HS])
    v = [ph.sb(f"v{i}", [P, 2 * CH, HS]) for i in range(2)]
    ps = [ph.sb(f"ps{i}", [P, S]) for i in range(2)]
    pr = [None] + [ph.sb(f"p{c}", [P, S - P * c]) for c in range(1, CH)]
    ones = ph.sb("ones", [P, 32])
    mx = ph.sb("mx", [P, 2, 2])
    mz = ph.sb("mz", [P, CH, P], F32R)
    rd = ph.sb("rd", [HS, H])
    rh = ph.sb("rh", [HS, 2 * H], F32R)
    rr = ph.sb("rr", [P, BANK], F32R)
    ri = ph.sb("ri", [P, BANK])
    sel = ph.sb("sel", [P, P], F32R)
    on = [ph.sb(f"on{i}", [P, BANK]) for i in range(4)]
    ds = ph.sb("ds", [HS, BANK])
    dn = ph.sb("dn", [HS, H])
    credit = ph.sb("credit", [P, 5])
    vd = [nc.dram_tensor(f"{tag}_values{i}", [P * H, HS], F32).ap() for i in range(2)]

    banks, st_ps = Banks(ph, K.psum[:RWB]), K.psum[RWB:]
    s_alone = ph.sem("alone")
    s_set = ph.sem("rows_set")
    s_ds, s_dn, s_rc, s_rh, s_rd, s_rr, s_ri = (ph.sem(x) for x in (
        "denominators", "denominators_spread", "reciprocals", "reciprocals_hi", "reciprocals_split",
        "reciprocals_back", "inverse_evacuated"))
    s_qd = ph.sem("queries_hi_twice")
    s_zero, s_xt, s_rnd, s_kb, s_vs, s_vd, s_v = (ph.sem(x) for x in (
        "zeroed", "tokens_staged", "rounded", "kb_made", "values", "values_in_dram", "values_in_rows"))
    s_mz, s_st, s_p, s_pv, s_add, s_on = (ph.sem(x) for x in (
        "maxima", "scores_t", "exp_done", "pv_done", "added", "normalized"))

    head = [row_units(True, False, False, False, False), row_units(False, True, False, False, False)]
    quad = [row_units(r % 2 == 0, True, True, True, r % 2 == 1) for r in range(4)]
    last = [quad[0], quad[1], row_units(False, True, True, True, False),
            row_units(False, False, True, True, True), row_units(False, False, False, True, True)]

    head, quad, last = (Places(x, RWB) for x in (head, quad, last))
    NQUAD = NP // 4

    def heads(x, rows, h, odd):
        return x[rows, :].rearrange("p (t i) -> p i t", i=H)[:, 8 * h + odd:8 * h + 8:2, :]

    def banks_of(c):
        return range(len(pieces(P * c)))[::-1]

    scores = Scores([(c, i) for c in range(CH) for i in banks_of(c)], len(st_ps))

    def last_of(c):
        return c, 0

    def turns(eng, body):
        body(-2, 2, -1, *head.turn(0), NONE, True, False, False)
        body(-1, 3, -1, *head.turn(1), NONE, False, True, False)
        with eng.Fori(0, NQUAD - 1) as q:
            base = [n + m * q for n, m in zip(head.total, quad.total)]
            for r in range(4):
                body(4 * q + r, r, 2 * q + r // 2, *quad.turn(r), base, r % 2 == 0, True, True)
        n, base = NP - 4, [n + m * (NQUAD - 1) for n, m in zip(head.total, quad.total)]
        for r in range(5):
            body(n + r, r % 4, (n + r) // 2, *last.turn(r), base, r == 0, r < 3, r < 4)

    with ph.block() as block:

        @block.sync
        def _(sp):
            def body(n, r, pair, at, first, base, proj, smax, st):
                if ("den", 0) in at:
                    sp.wait_ge(s_ds, n + 1)
                    sp.sem_inc(s_alone, 1)
                    sp.dma_start(dn[:], ds[0:HS:32, :].rearrange("h (x f) -> h x f", f=H)).then_inc(s_dn, 16)
                if proj:
                    i = 1 - r // 2
                    sp.wait_ge(s_rnd, 8 * (pair + 1) + 4)
                    sp.sem_inc(s_alone, 1)
                    sp.dma_start(qa[i][HS:P, :].bitcast(F32), qa[i][0:HS, :].bitcast(F32)).then_inc(s_qd, 16)
                if smax and r % 2:
                    i = 1 - r // 2
                    sp.wait_ge(s_vs, 2 * (pair + 2))
                    sp.dma_start(vd[i].rearrange("(x i) k -> x (i k)", i=H), vs[:]).then_inc(s_vd, 16)
                if ("den", 0) in at:
                    sp.wait_ge(s_rd, n + 1)
                    sp.sem_inc(s_alone, 1)
                    for part in range(4):
                        sp.dma_start(rr[part:part + 1, :].bitcast(F32).rearrange("o (x f) -> o x f", f=CH),
                                     rh[0:HS, CH * part:CH * part + CH].bitcast(F32)).then_inc(s_rr, 16)
                if smax and r % 2:
                    sp.wait_ge(s_vd, 16 * (pair + 2))
                    sp.dma_start(v[i][:], vd[i].rearrange("(c p) k -> p c k", p=P)).then_inc(s_v, 16)
                if proj:
                    sp.wait_ge(s_rnd, 8 * (pair + 1) + 8)
                    sp.sem_inc(s_alone, 1)
                    sp.dma_start(kb[i][0:HS, :].bitcast(F32), ka[i][0:HS, :].bitcast(F32)).then_inc(s_kb, 16)

            turns(sp, body)

        @block.gpsimd
        def _(pool):
            pool.memset(mz[:].bitcast(F32), 0.0).then_inc(s_zero, 1)
            pool.memset(ones[:], 1.0).then_inc(s_zero, 1)
            pool.memset(ps[1][:], 1.0).then_inc(s_zero, 1)
            pool.memset(on[2][:], 0.0).then_inc(s_zero, 1)
            pool.memset(credit[:, 4:5], 0.0).then_inc(s_dn, 16)
            pool.memset(credit[:, 0:1], 0.0).then_inc(s_p, len(st_ps))
            pool.memset(credit[:, 3:4], 0.0).then_inc(s_on, 1)
            pool.memset(credit[:, 1:2], 0.0).then_inc(s_pv, CH)
            pool.memset(credit[:, 2:3], 0.0).then_inc(s_add, CH - 1)

            def body(n, r, pair, at, first, base, proj, smax, st):
                i = 1 - r // 2
                for c in range(1, CH):
                    if st:
                        if c == 1:
                            pool.wait_ge(s_pv, CH * n + 1 + CH)
                        pool.wait_ge(s_p, scores.through(n, last_of(c)))
                        pool.wait_ge(s_add, (CH - 1) * n + c - 1 + CH - 1)
                        pool.tensor_tensor(ps[r % 2][:, P * c:], ps[r % 2][:, P * c:], pr[c][:],
                                           ALU.add).then_inc(s_add, 1)
                if proj and not (isinstance(n, int) and n >= 0):
                    banks.all_read(pool, base, first)
                    pool.sem_inc(s_alone, 1)
                    pool.tensor_copy(xt[1 - i][:], XT[:, bass.ds((pair + 2) * P, P)]).then_inc(s_xt, 1)

            pool.tensor_copy(xt[0][:], XT[:, 0:P]).then_inc(s_xt, 1)
            turns(pool, body)

        @block.scalar
        def _(act):
            act.wait_ge(s_set, 7)

            def body(n, r, pair, at, first, base, proj, smax, st):
                i = 1 - r // 2
                for k in range(CH + 1):
                    if st and k < CH:
                        if k == 0:
                            act.wait_ge(s_on, n + 1)
                        else:
                            act.wait_ge(s_add, (CH - 1) * n + k)
                            act.wait_ge(s_pv, CH * n + k + 1)
                        for x in banks_of(k):
                            a, b = pieces(P * k)[x]
                            act.wait_ge(s_st, scores.n * n + scores.at[k, x] + 1)
                            dst = pr[k][:, a - P * k:b - P * k] if k else ps[r % 2][:, a:b]
                            act.activation(dst, st_ps[scores.bank((k, x))][:, 0:b - a], ACT.Exp,
                                           scale=scale).then_inc(s_p, 1)
                    if proj and k in ROW_PROJECTIONS:
                        kind, h = u = ROW_PROJECTIONS[k]
                        w = banks.filled(act, base, at[u])
                        if kind == "v":
                            if h == 0 and not (isinstance(n, int) and n < 0):
                                act.wait_ge(s_vd, 16 * (pair + 1))
                            act.activation(vs[:, BANK * h:BANK * h + BANK], w[:], ACT.Copy)\
                               .then_inc(banks.free[at[u][0]], 1)
                            banks.read(act, base, at[u])
                            act.nop().then_inc(s_vs, 1)
                        else:
                            for odd in range(2):
                                act.activation(heads((ka if kind == "k" else qa)[i], slice(0, HS), h, odd),
                                               w[HS * odd:HS * odd + HS, :].rearrange("p (i t) -> p i t", i=4),
                                               ACT.Copy).then_inc(s_rnd, 1)
                    if k == 0 and ("den", 0) in at:
                        w = banks.filled(act, base, at["den", 0])
                        act.wait_ge(s_dn, 16 * n + 16)
                        act.activation(ds[:], w[0:HS, :], ACT.Copy).then_inc(banks.free[at["den", 0][0]], 1)
                        banks.read(act, base, at["den", 0])
                        act.sem_inc(s_ds, 1)
                    if k == 6 and ("inv", 0) in at:
                        w = banks.filled(act, base, at["inv", 0])
                        act.wait_ge(s_on, n + 1)
                        act.activation(ri[:], w[:], ACT.Copy).then_inc(banks.free[at["inv", 0][0]], 1)
                    if k in (5, 8) and smax:
                        u = at["t", int(k == 5)]
                        w = banks.filled(act, base, u)
                        m, j = (r + 1) % 4 // 2, (r + 1) % 2
                        a = S * j + BANK * int(k == 5)
                        act.activation(qb[m][HS:HS + 1, a:a + BANK], w[HS:HS + 1, :], ACT.Copy)\
                           .then_inc(banks.free[u[0]], 1)

            turns(act, body)

        @block.vector
        def _(dve):

            def body(n, r, pair, at, first, base, proj, smax, st):
                i = 1 - r // 2
                for k in range(CH + 1):
                    c = CH - 1 - k
                    if smax and k < CH:
                        tiles = key_tiles(True, c)
                        for h in range(tiles):
                            u = at["max", c, h]
                            w = banks.filled(dve, base, u)
                            cols = min(BANK, P * (c + 1) - BANK * h)
                            dst = mx[:, c % 2, h:h + 1] if tiles == 2 else mz[:, c, HS:HS + 1]
                            dve.reduce_max(dst, w[:, 0:cols], AX.X, negate=True).then_inc(banks.free[u[0]], 1)
                        if tiles == 2:
                            banks.read(dve, base, at["max", c, 0])
                            banks.read(dve, base, u)
                            dve.tensor_tensor(mz[:, c, HS:HS + 1], mx[:, c % 2, 0:1], mx[:, c % 2, 1:2],
                                              ALU.min).then_inc(s_mz, 1)
                    if proj and ROW_PROJECTIONS.get(k, "v")[0] in "kq":
                        kind, h = u = ROW_PROJECTIONS[k]
                        w = banks.filled(dve, base, at[u])
                        for odd in range(2):
                            dve.wait_ge(s_rnd, 8 * (pair + 1) + 2 * k + odd + 1)
                            hi, lo, rows = (ka, ka, slice(HS, P)) if kind == "k" else (qa, qb, slice(0, HS))
                            last = dve.tensor_tensor(heads(lo[i], rows, h, odd),
                                                     w[HS * odd:HS * odd + HS, :].rearrange("p (i t) -> p i t", i=4),
                                                     heads(hi[i], slice(0, HS), h, odd).bitcast(F32), ALU.subtract)
                        last.then_inc(banks.free[at[u][0]], 1)
                    if k == 2 and ("den", 0) in at:
                        dve.wait_ge(s_dn, 16 * n + 32)
                        dve.reciprocal(rd[:], dn[:]).then_inc(s_rc, 1)
                        dve.wait_ge(s_rc, n + 1)
                        split, odd = rh[:].rearrange("x (s o f) -> x s o f", s=2, o=2), rd[:].rearrange(
                            "x (f o) -> x o f", o=2)
                        dve.tensor_copy(split[:, 0], odd).then_inc(s_rh, 1)
                        dve.wait_ge(s_rh, n + 1)
                        dve.tensor_tensor(split[:, 1], odd, split[:, 0].bitcast(F32), ALU.subtract).then_inc(s_rd, 1)
                    if k == 7 and ("inv", 0) in at:
                        banks.read(dve, base, at["inv", 0])
                        o = (r + 1) % 2
                        dve.tensor_tensor(on[(r + 3) % 4][:], K.o_ps[:, BANK * o:BANK * o + BANK], ri[:],
                                          ALU.mult).then_inc(s_on, 1)
                    if k == 8 and ("out", 0) in at:
                        u = at["out", 0]
                        w = banks.filled(dve, base, u)
                        dve.tensor_copy(acc[:, pair, :], w[:, 0:D]).then_inc(banks.free[u[0]], 1)

            dve.memset(rr[:].bitcast(F32), 0.0)
            dve.tensor_copy(sel[:], rw.sel_f[:])
            for i in range(2):
                dve.memset(kb[i][HS:P, :].bitcast(F32), 0.0).then_inc(s_set, 1)
                dve.memset(qb[i][HS:P, :].bitcast(F32), 0.0).then_inc(s_set, 1)
            dve.memset(K.o_ps[:, BANK:], 0.0).then_inc(s_set, 1)
            dve.wait_ge(s_set, 5)
            dve.memset(kb[0][HS:HS + 1, :].bitcast(F32), 1.0).then_inc(s_set, 1)
            dve.memset(kb[1][HS:HS + 1, :].bitcast(F32), 1.0).then_inc(s_set, 1)
            dve.wait_ge(s_zero, 4)
            turns(dve, body)

        @block.tensor
        def _(pe):
            pe.wait_ge(s_set, 7)
            pe.wait_ge(s_zero, 4)

            def weigh(c, n, r, pair):
                cur, j = r // 2, r % 2
                pe.wait_ge(s_p, scores.through(n, last_of(c)))
                if c == 0:
                    pe.wait_ge(s_on, n + 1)
                    if j == 0:
                        pe.wait_ge(s_v, 16 * (pair + 1))
                p = pr[c] if c else ps[j]
                for odd in range(2):
                    last = pe.matmul(K.o_ps[HS * odd:HS * odd + HS, BANK * j + P // 2 * c:BANK * (j + 1)],
                                     v[cur][:, CH * j + c, :], p[:, odd::2],
                                     start=(c == 0), stop=(c == CH - 1))
                last.then_inc(s_pv, 1)

            def body(n, r, pair, at, first, base, proj, smax, st):
                cur, j = r // 2, r % 2
                nxt, nj = (r + 1) % 4 // 2, (r + 1) % 2
                if not st:
                    banks.all_read(pe, base, first)
                if smax and j == 1:
                    pe.wait_ge(s_qd, 16 * (pair + 2))
                for k in range(CH + 1):
                    for h in range(2):
                        if smax and k < CH and h < key_tiles(True, CH - 1 - k):
                            c = CH - 1 - k
                            u = at["max", c, h]
                            w = banks.claim(pe, base, u)
                            cols = min(BANK, P * (c + 1) - BANK * h)
                            diag = BANK * h + cols == P * (c + 1)
                            a = S * nj
                            last = pe.matmul(w[:, 0:cols], qa[nxt][:, a + P * c:a + P * c + P],
                                             ka[nxt][:, a + BANK * h:a + BANK * h + cols],
                                             start=True, stop=not diag)
                            if diag:
                                last = pe.matmul(w[:, cols - P:cols], K.identb[:], K.maskq[:],
                                                 start=False, stop=True)
                            last.then_inc(banks.full[u[0]], 1)
                        if st and k < CH and h < len(pieces(P * k)):
                            x = banks_of(k)[h]
                            a, b = pieces(P * k)[x]
                            if k == 0 and h == 0 and j == 0:
                                pe.wait_ge(s_kb, 16 * (pair + 1))
                            if k == 0 and x == 0:
                                banks.last_read(pe, base, first)
                            pe.wait_ge(s_p, scores.before(n, (k, x)))
                            bank = st_ps[scores.bank((k, x))]
                            s0, t = S * j, bank[:, 0:b - a]
                            diag = a == P * k
                            pe.matmul(t, ka[cur][:, s0 + P * k:s0 + P * k + P], qa[cur][:, s0 + a:s0 + b],
                                      start=True, stop=False)
                            last = pe.matmul(t, kb[cur][:, s0 + P * k:s0 + P * k + P], qb[cur][:, s0 + a:s0 + b],
                                             start=False, stop=not diag)
                            if diag:
                                last = pe.matmul(bank[:, 0:P], K.identb[:], K.maskk[:],
                                                 start=False, stop=True)
                            last.then_inc(s_st, 1)
                    if proj and k in ROW_PROJECTIONS:
                        if k == 0:
                            pe.wait_ge(s_xt, pair + 2)
                        kind, h = u = ROW_PROJECTIONS[k]
                        w = banks.claim(pe, base, at[u])
                        if kind == "v":
                            last = pe.matmul(w[:], xt[1 - cur][:], wv[:, BANK * h:BANK * h + BANK], start=True, stop=True)
                        else:
                            for e in range(4):
                                last = pe.matmul(w[:, P * e:P * e + P],
                                                 (wk if kind == "k" else wq)[:, BANK * h + P * e:BANK * h + P * e + P],
                                                 xt[1 - cur][:], start=True, stop=True)
                        last.then_inc(banks.full[at[u][0]], 1)
                    if st and 1 <= k < CH:
                        weigh(k - 1, n, r, pair)
                    if k == 0 and ("den", 0) in at:
                        u = at["den", 0]
                        w = banks.claim(pe, base, u)
                        pe.wait_ge(s_add, (CH - 1) * n + CH - 1)
                        for h in range(2):
                            last = pe.matmul(w[32 * h:32 * h + 32, :], ones[:], ps[1 - j][:, BANK * h:BANK * h + BANK],
                                             start=True, stop=True)
                        last.then_inc(banks.full[u[0]], 1)
                    if k == 6 and ("inv", 0) in at:
                        u = at["inv", 0]
                        w = banks.claim(pe, base, u)
                        pe.wait_ge(s_rr, 64 * n + 64)
                        pe.matmul(w[:], sel[:], rr[:], start=True, stop=True).then_inc(banks.full[u[0]], 1)
                    if k == 8 and ("out", 0) in at:
                        u = at["out", 0]
                        w = banks.claim(pe, base, u)
                        ended = r + (1 if r % 2 else 2)
                        pe.wait_ge(s_on, n + 1 if r % 2 else n + 2)
                        for e in range(H // 2):
                            for m in range(2):
                                last = pe.matmul(w[HS * m:HS * m + HS, 0:D], on[(ended + m) % 4][:, e::H // 2], pw[:, e, :],
                                                 start=(e == 0), stop=(e == H // 2 - 1))
                        last.then_inc(banks.full[u[0]], 1)
                    if k in (5, 8) and smax:
                        i = int(k == 5)
                        u = at["t", i]
                        if not i and at["t", 1][0] != u[0]:
                            banks.read(pe, base, at["t", 1])
                        w = banks.claim(pe, base, u)
                        if i:
                            pe.wait_ge(s_mz, CB * (n + 2))
                        else:
                            banks.all_of(pe, base, [at["max", c, 0] for c in range(CB)], u[0])
                        for c in range(CB):
                            last = pe.matmul(w[:, P * c:P * c + P], mz[:, CB * i + c, :], K.identr[:],
                                             start=True, stop=True)
                        last.then_inc(banks.full[u[0]], 1)
                if st:
                    weigh(CH - 1, n, r, pair)

            turns(pe, body)


def first_expert(K, t, layer):
    w1, w2, b1, b2 = K.expert
    return [(w1[:], t[f"w1_{layer}"][0]), (w2[:], t[f"w2_{layer}"][0].rearrange("(c p) d -> p c d", p=P)),
            (b1[:], t[f"b1_{layer}"][0]), (b2[:], t[f"b2_{layer}"][0].partition_broadcast(P))]


def build(nc, t):
    with ExitStack() as stack:
        K = Kept(nc, stack)
        with ExitStack() as layer0:
            K.CT = layer0.enter_context(nc.sbuf_tensor("CT", [P, G * B + 1, S], F32))
            gb = GroupBuffers(nc, layer0)
            load_phase(nc, K, gb, {"x": t["x"], "ident": t["ident"], "maskq": t["maskq"], "maskk": t["maskk"],
                                   "gw": t["gw0"], "negc": t["negc"], "sel": t["sel"]})
            small = [(K.wo[0], t["wo0"]), (K.wo[1], t["wo1"]), (K.bo, t["bo0"].partition_broadcast(P)),
                     (K.ob[:], t["ob1"]), (K.pb[:], t["pb2"].partition_broadcast(P))]
            for i, (w, b, rank) in enumerate(K.router):
                small += [(w[:], t[f"rw{i}"]), (b[:], t[f"rb{i}"].partition_broadcast(P)), (rank[:], t[f"rank{i}"])]
            groups_phase(nc, K, gb, "attn0", True, (D // H) ** -0.5, ahead=small)
            norm_phase(nc, K, "norm0", "context", ahead=[(gb.gw[:], t["gw1"])])
            groups_phase(nc, K, gb, "attn1", False, (D // H // 2) ** -0.5, ahead=first_expert(K, t, 0))
            route_phase(nc, K, "route0", K.router[0][0])
        with ExitStack() as layer1:
            rw = RowWeights(nc, layer1)
            experts_phase(nc, K, {n: t[n + "_0"] for n in ("w1", "b1", "w2", "b2")}, "moe0", K.router[0], E0,
                          0.0, 1e-8,
                          ahead=[(rw.sel_f[:], t["sel2"]), (rw.wq[:], t["wq2"]), (rw.wk[:], t["wk2"]),
                                 (rw.wv[:], t["wv2"]), (rw.pw[:], t["pw2"])])
            norm_phase(nc, K, "norm1", "moe", ahead=first_expert(K, t, 1))
            rows_phase(nc, K, rw, "attn2", HS ** -0.5)
        norm_phase(nc, K, "norm2", "rows", split=True, router=K.router[1][0])
        experts_phase(nc, K, {n: t[n + "_1"] for n in ("w1", "b1", "w2", "b2")}, "moe1", K.router[1], E1, 1e-10, 0.0)
        norm_phase(nc, K, "norm3", "clip", out=t["out"])


def kernel(**inputs):
    import numpy as np
    import concourse.bacc as bacc
    from concourse.bass_utils import run_bass_kernel_spmd

    a = {n: np.asarray(v) for n, v in inputs.items()}
    f32 = np.float32

    def packed(wk, bk, wq, bq, wv, bv, hd, stride):
        gw = np.zeros((P, G, GW), f32)
        for h in range(H):
            g, at = divmod(h, HG)
            for part in range(3):
                c = 32 * at + ONE * part
                gw[:, g, c:c + hd] = wk[:, hd * h:hd * h + hd]
                gw[:, g, P + c:P + c + hd] = wq[:, stride * h:stride * h + hd]
                gw[c:c + hd, g, 4 * P] = bk[hd * h:hd * h + hd]
                gw[c:c + hd, g, 4 * P + 1] = bq[stride * h:stride * h + hd]
            c = 32 * at
            gw[:, g, 2 * P + c:2 * P + c + hd] = wv[:, hd * h:hd * h + hd]
            gw[:, g, 3 * P + c:3 * P + c + hd] = bv[hd * h:hd * h + hd]
            gw[:, g, 3 * P + c + ONE] = 1.0
            gw[c + MROW, g, 4 * P] = 1.0
        return gw

    def rows_of(w, hd):
        wo = np.zeros((P, G, D), f32)
        for h in range(H):
            g, at = divmod(h, HG)
            wo[32 * at:32 * at + hd, g] = w[hd * h:hd * h + hd]
        return wo

    zero = np.zeros(D, f32)
    rows = np.arange(P)
    negc = np.zeros((P, 2), f32)
    negc[rows % 32 // ONE == 1, 0] = -1.0
    negc[rows % 32 // ONE == 2, 1] = -1.0
    later = rows[:, None] < rows[None, :]
    wq, wk, wv = (a[f"L1_attn_W{x}"].transpose(1, 0, 2) for x in "qkv")
    arrays = {
        "x": a["L0_attn_x"],
        "ident": np.eye(P, dtype=f32),
        "maskq": np.where(later, f32(-1e30), f32(0.0)),
        "maskk": np.where(later.T, f32(-1e30), f32(0.0)),
        "negc": negc,
        "sel": ((rows[:, None] // 32 == rows[None, :] // 32) & (rows[:, None] % 32 // 2 == ONE // 2)).astype(f32),
        "sel2": ((rows[:, None] < 4) & (rows[:, None] % 2 == rows[None, :] // HS)).astype(f32),
        "gw0": packed(a["L0_attn_Wk"], zero, a["L0_attn_Wq"], zero, a["L0_attn_Wv"], zero, D // H, D // H),
        "wo0": rows_of(a["L0_attn_Wo"], D // H),
        "bo0": a["L0_attn_bo"],
        "gw1": packed(a["L0_ffn_k_w"], a["L0_ffn_k_b"], a["L0_ffn_q_w"], a["L0_ffn_q_b"], a["L0_ffn_v_w"],
                      a["L0_ffn_v_b"], D // H // 2, D // H),
        "wo1": rows_of(a["L0_ffn_o_w"], D // H // 2),
        "ob1": a["L0_ffn_o_b"].reshape(D, 1),
        "rw0": a["L0_ffn_router_w"],
        "rb0": a["L0_ffn_router_b"],
        "rank0": np.tile(np.arange(E0, 0, -1, dtype=f32), (P, 1)),
        "wq2": wq.reshape(D, H * HS),
        "wk2": wk.reshape(D, H * HS),
        "wv2": wv.reshape(D, H * HS),
        "pw2": a["L1_attn_proj_w"].reshape(D, H // 2, 2 * HS).transpose(2, 1, 0),
        "pb2": a["L1_attn_proj_b"],
        "rw1": a["L1_ffn_gate_w"].T,
        "rb1": np.zeros(E1, f32),
        "rank1": np.tile(np.arange(E1, 0, -1, dtype=f32), (P, 1)),
    }
    for n, layer in enumerate(("L0_ffn", "L1_ffn")):
        arrays[f"w1_{n}"] = a[f"{layer}_w1"]
        arrays[f"b1_{n}"] = a[f"{layer}_b1"].reshape(-1, FC, P).transpose(0, 2, 1)
        arrays[f"w2_{n}"] = a[f"{layer}_w2"]
        arrays[f"b2_{n}"] = a[f"{layer}_b2"]

    nc = bacc.Bacc("TRN2", target_bir_lowering=False, num_devices=1)
    feeds, tensors = {}, {}
    for name, array in arrays.items():
        array = np.ascontiguousarray(array)
        feeds[f"in_{name}"] = array
        tensors[name] = nc.dram_tensor(f"in_{name}", array.shape, mybir.dt.from_np(array.dtype),
                                       kind="ExternalInput").ap()
    tensors["out"] = nc.dram_tensor("out", (B, S, D), F32, kind="ExternalOutput").ap()
    build(nc, tensors)
    result = run_bass_kernel_spmd(nc, [feeds], core_ids=[0])
    return result.results[0]["out"]
```
